# Optimizing a Trainium2 kernel written in Bass

```python
import numpy as np
import jax
import jax.numpy as jnp

def _softmax(x, axis=-1):
    return jax.nn.softmax(x, axis=axis)

def _gelu(x):
    return jax.nn.gelu(x, approximate=True)

def _silu(x):
    return jax.nn.silu(x)

def _sigmoid(x):
    return jax.nn.sigmoid(x)

def _layernorm(x, axis=-1, eps=1e-05):
    m = jnp.mean(x, axis=axis, keepdims=True)
    v = jnp.var(x, axis=axis, keepdims=True)
    return (x - m) / jnp.sqrt(v + eps)

def _scatter_add(tgt, idx, src, axis=0):
    return tgt.at[idx].add(src)

def _segment_sum(src, seg, n):
    return jax.ops.segment_sum(src, seg, n)
kernel_name = 'mk_lm_tower_d2_tok_ids1024_r4_85170c'

def setup_inputs(seed: int=0):
    np.random.seed(seed)
    _w = jnp.asarray

    def _rec_inputs():
        import jax
        import jax.numpy as jnp
        _rk = jax.random.key(seed)
        x = jax.random.randint(jax.random.fold_in(_rk, 1), (8, 1024), 0, 64, jnp.int32)
        return x
    x = _rec_inputs()

    def _L0_tok_setup():
        import jax, jax.numpy as jnp
        import numpy as np
        from jax import lax
        RMS_EPS = 1.1920929e-07
        ROPE_BASE = 10000.0

        def _rope(x):
            seq_len, d = (x.shape[1], x.shape[2])
            inv_freq = 1.0 / ROPE_BASE ** (jnp.arange(0, d, 2, dtype=jnp.float32) / d)
            freqs = jnp.arange(seq_len, dtype=jnp.float32)[:, None] * inv_freq[None, :]
            emb = jnp.concatenate([freqs, freqs], axis=-1)
            cos, sin = (jnp.cos(emb), jnp.sin(emb))
            x1, x2 = (x[..., ::2], x[..., 1::2])
            r1 = x1 * cos[:, ::2] - x2 * sin[:, ::2]
            r2 = x1 * sin[:, 1::2] + x2 * cos[:, 1::2]
            return jnp.stack([r1, r2], axis=-1).reshape(x.shape)
        key = jax.random.key(seed)
        k1, k2, k3, k4 = jax.random.split(key, 4)
        d_model, vocab, n_gram = (256, 64, 4)
        batch, seq_len = (4, 2048)
        return {'bytes_input': jax.random.randint(k1, (batch, seq_len), 0, vocab), 'embed_table': jax.random.normal(k2, (vocab, d_model), dtype=jnp.float32) * 0.02, 'conv_w': jax.random.normal(k3, (d_model, d_model, n_gram), dtype=jnp.float32) * 0.02, 'conv_b': jax.random.normal(k4, (d_model,), dtype=jnp.float32) * 0.02, 'norm_w': jnp.ones((d_model,), dtype=jnp.float32)}
    _L0_tok_all = _L0_tok_setup()
    _L0_tok_in = {k: v for k, v in _L0_tok_all.items() if k in ('embed_table', 'conv_w', 'conv_b', 'norm_w')}
    del _L0_tok_all

    def _L0_attn_setup():
        import jax, jax.numpy as jnp
        import numpy as np
        D_MODEL = 256
        D_STATE = 16
        EXPAND = 2
        D_INNER = D_MODEL * EXPAND
        BATCH = 2
        SEQ = 1024
        K = 3
        key = jax.random.key(seed)
        ks = jax.random.split(key, 8)
        s = 0.02
        f = lambda k, shp: jax.random.normal(k, shp, dtype=jnp.float32) * s
        return {'x': jax.random.normal(ks[0], (BATCH, SEQ, D_MODEL), dtype=jnp.float32), 'conv_w': f(ks[1], (D_INNER, D_MODEL, K)), 'conv_b': jnp.zeros((D_INNER,), jnp.float32), 'in_w': f(ks[2], (D_INNER, D_INNER)), 'in_b': jnp.zeros((D_INNER,), jnp.float32), 'A_log': jnp.log(jnp.broadcast_to(jnp.arange(1, D_STATE + 1, dtype=jnp.float32), (D_INNER, D_STATE))), 'Dskip': jnp.ones((D_INNER,), jnp.float32), 'dt_w': f(ks[3], (D_INNER, D_INNER)), 'dt_b': jnp.full((D_INNER,), -4.0, jnp.float32), 'Bp_w': f(ks[4], (D_STATE, D_INNER)), 'Bp_b': jnp.zeros((D_STATE,), jnp.float32), 'Cp_w': f(ks[5], (D_STATE, D_INNER)), 'Cp_b': jnp.zeros((D_STATE,), jnp.float32), 'out_w': f(ks[6], (D_MODEL, D_INNER)), 'out_b': jnp.zeros((D_MODEL,), jnp.float32)}
    _L0_attn_all = _L0_attn_setup()
    _L0_attn_in = {k: v for k, v in _L0_attn_all.items() if k in ('conv_w', 'conv_b', 'in_w', 'in_b', 'A_log', 'Dskip', 'dt_w', 'dt_b', 'Bp_w', 'Bp_b', 'Cp_w', 'Cp_b', 'out_w', 'out_b')}
    del _L0_attn_all

    def _L0_ffn_setup():
        import jax, jax.numpy as jnp
        import numpy as np
        LN_EPS = 1e-05

        def _layernorm(x, g, b):
            m = jnp.mean(x, axis=-1, keepdims=True)
            v = jnp.mean(jnp.square(x - m), axis=-1, keepdims=True)
            return (x - m) * jax.lax.rsqrt(v + LN_EPS) * g + b
        K_TOP = 2
        key = jax.random.key(seed)
        ks = jax.random.split(key, 4)
        B, N, D, E = (8, 512, 256, 4)
        s = 0.02
        return {'x': jax.random.normal(ks[0], (B, N, D), dtype=jnp.float32), 'gate_W': jax.random.normal(ks[1], (D, E), dtype=jnp.float32) * s, 'gate_b': jnp.zeros((E,), jnp.float32), 'W1': jax.random.normal(ks[2], (E, D, D), dtype=jnp.float32) * s, 'b1': jnp.zeros((E, D), jnp.float32), 'g1': jnp.ones((E, D), jnp.float32), 'be1': jnp.zeros((E, D), jnp.float32), 'W2': jax.random.normal(ks[3], (E, D, D), dtype=jnp.float32) * s, 'b2': jnp.zeros((E, D), jnp.float32), 'g2': jnp.ones((E, D), jnp.float32), 'be2': jnp.zeros((E, D), jnp.float32)}
    _L0_ffn_all = _L0_ffn_setup()
    _L0_ffn_in = {k: v for k, v in _L0_ffn_all.items() if k in ('gate_W', 'gate_b', 'W1', 'b1', 'g1', 'be1', 'W2', 'b2', 'g2', 'be2')}
    del _L0_ffn_all

    def _L1_attn_setup():
        import math
        import jax, jax.numpy as jnp
        import numpy as np
        D = 256
        NH = 16
        DH = D // NH

        def _rope(q, k, base=10000.0):
            half = q.shape[-1] // 2
            freqs = jnp.arange(half, dtype=q.dtype) / half
            theta = 1.0 / base ** freqs
            t = jnp.arange(q.shape[-2], dtype=q.dtype)
            ang = t[:, None] * theta[None, :]
            cos = jnp.cos(ang)[None, None, :, :]
            sin = jnp.sin(ang)[None, None, :, :]

            def rot(x):
                x1, x2 = (x[..., :half], x[..., half:])
                return jnp.concatenate([x1 * cos - x2 * sin, x1 * sin + x2 * cos], axis=-1)
            return (rot(q), rot(k))
        key = jax.random.key(seed)
        k1, k2, k3 = jax.random.split(key, 3)
        x = jax.random.normal(k1, (2, 512, D), dtype=jnp.float32)
        s = 1.0 / math.sqrt(D)
        W_qkv = jax.random.normal(k2, (D, 3 * D), dtype=jnp.float32) * s
        W_o = jax.random.normal(k3, (D, D), dtype=jnp.float32) * s
        return {'x': x, 'W_qkv': W_qkv, 'W_o': W_o}
    _L1_attn_all = _L1_attn_setup()
    _L1_attn_in = {k: v for k, v in _L1_attn_all.items() if k in ('W_qkv', 'W_o')}
    del _L1_attn_all

    def _L1_ffn_setup():
        import math
        import jax, jax.numpy as jnp
        import numpy as np
        D_CONTENT = 256
        D_POSITION = 32
        NUM_TILES = 8
        BATCH = 8
        SEQ = 512

        def make_pe(seq_len, d_pos):
            pos = jnp.arange(seq_len, dtype=jnp.float32)[:, None]
            div = jnp.exp(jnp.arange(0, d_pos, 2, dtype=jnp.float32) * (-math.log(10000.0) / d_pos))
            ang = pos * div
            pe = jnp.zeros((seq_len, d_pos), dtype=jnp.float32)
            pe = pe.at[:, 0::2].set(jnp.sin(ang))
            pe = pe.at[:, 1::2].set(jnp.cos(ang))
            return pe
        key = jax.random.key(seed)
        k1, k2, k3, k4 = jax.random.split(key, 4)
        x = jax.random.normal(k1, (BATCH, SEQ, D_CONTENT), dtype=jnp.float32)
        tile_sigs = jax.random.normal(k2, (NUM_TILES, D_POSITION), dtype=jnp.float32)
        lim = 1.0 / math.sqrt(D_CONTENT)
        W = jax.random.uniform(k3, (NUM_TILES, D_CONTENT, D_CONTENT), minval=-lim, maxval=lim, dtype=jnp.float32)
        b = jax.random.uniform(k4, (NUM_TILES, D_CONTENT), minval=-lim, maxval=lim, dtype=jnp.float32)
        return {'x': x, 'tile_sigs': tile_sigs, 'W': W, 'b': b}
    _L1_ffn_all = _L1_ffn_setup()
    _L1_ffn_in = {k: v for k, v in _L1_ffn_all.items() if k in ('tile_sigs', 'W', 'b')}
    del _L1_ffn_all
    return {'x': x, 'L0_tok_embed_table': _L0_tok_in['embed_table'], 'L0_tok_conv_w': _L0_tok_in['conv_w'], 'L0_tok_conv_b': _L0_tok_in['conv_b'], 'L0_tok_norm_w': _L0_tok_in['norm_w'], 'L0_attn_conv_w': _L0_attn_in['conv_w'], 'L0_attn_conv_b': _L0_attn_in['conv_b'], 'L0_attn_in_w': _L0_attn_in['in_w'], 'L0_attn_in_b': _L0_attn_in['in_b'], 'L0_attn_A_log': _L0_attn_in['A_log'], 'L0_attn_Dskip': _L0_attn_in['Dskip'], 'L0_attn_dt_w': _L0_attn_in['dt_w'], 'L0_attn_dt_b': _L0_attn_in['dt_b'], 'L0_attn_Bp_w': _L0_attn_in['Bp_w'], 'L0_attn_Bp_b': _L0_attn_in['Bp_b'], 'L0_attn_Cp_w': _L0_attn_in['Cp_w'], 'L0_attn_Cp_b': _L0_attn_in['Cp_b'], 'L0_attn_out_w': _L0_attn_in['out_w'], 'L0_attn_out_b': _L0_attn_in['out_b'], 'L0_ffn_gate_W': _L0_ffn_in['gate_W'], 'L0_ffn_gate_b': _L0_ffn_in['gate_b'], 'L0_ffn_W1': _L0_ffn_in['W1'], 'L0_ffn_b1': _L0_ffn_in['b1'], 'L0_ffn_g1': _L0_ffn_in['g1'], 'L0_ffn_be1': _L0_ffn_in['be1'], 'L0_ffn_W2': _L0_ffn_in['W2'], 'L0_ffn_b2': _L0_ffn_in['b2'], 'L0_ffn_g2': _L0_ffn_in['g2'], 'L0_ffn_be2': _L0_ffn_in['be2'], 'L1_attn_W_qkv': _L1_attn_in['W_qkv'], 'L1_attn_W_o': _L1_attn_in['W_o'], 'L1_ffn_tile_sigs': _L1_ffn_in['tile_sigs'], 'L1_ffn_W': _L1_ffn_in['W'], 'L1_ffn_b': _L1_ffn_in['b']}

def reference(x, L0_tok_embed_table, L0_tok_conv_w, L0_tok_conv_b, L0_tok_norm_w, L0_attn_conv_w, L0_attn_conv_b, L0_attn_in_w, L0_attn_in_b, L0_attn_A_log, L0_attn_Dskip, L0_attn_dt_w, L0_attn_dt_b, L0_attn_Bp_w, L0_attn_Bp_b, L0_attn_Cp_w, L0_attn_Cp_b, L0_attn_out_w, L0_attn_out_b, L0_ffn_gate_W, L0_ffn_gate_b, L0_ffn_W1, L0_ffn_b1, L0_ffn_g1, L0_ffn_be1, L0_ffn_W2, L0_ffn_b2, L0_ffn_g2, L0_ffn_be2, L1_attn_W_qkv, L1_attn_W_o, L1_ffn_tile_sigs, L1_ffn_W, L1_ffn_b):
    import jax
    import jax.numpy as jnp

    def _L0_tok_ref(bytes_input, embed_table, conv_w, conv_b, norm_w):
        import jax, jax.numpy as jnp
        import numpy as np
        from jax import lax
        RMS_EPS = 1.1920929e-07
        ROPE_BASE = 10000.0

        def _rope(x):
            seq_len, d = (x.shape[1], x.shape[2])
            inv_freq = 1.0 / ROPE_BASE ** (jnp.arange(0, d, 2, dtype=jnp.float32) / d)
            freqs = jnp.arange(seq_len, dtype=jnp.float32)[:, None] * inv_freq[None, :]
            emb = jnp.concatenate([freqs, freqs], axis=-1)
            cos, sin = (jnp.cos(emb), jnp.sin(emb))
            x1, x2 = (x[..., ::2], x[..., 1::2])
            r1 = x1 * cos[:, ::2] - x2 * sin[:, ::2]
            r2 = x1 * sin[:, 1::2] + x2 * cos[:, 1::2]
            return jnp.stack([r1, r2], axis=-1).reshape(x.shape)
        n_gram = conv_w.shape[-1]
        x = embed_table[bytes_input]
        x_t = jnp.swapaxes(x, 1, 2)
        y = lax.conv_general_dilated(x_t, conv_w, window_strides=(1,), padding=[(n_gram - 1, 0)], dimension_numbers=('NCH', 'OIH', 'NCH'))
        y = y + conv_b[None, :, None]
        x = x + jnp.swapaxes(y, 1, 2)
        x = _rope(x)
        x = x * lax.rsqrt(jnp.mean(x * x, axis=-1, keepdims=True) + RMS_EPS) * norm_w
        return x

    def _L0_attn_ref(x, conv_w, conv_b, in_w, in_b, A_log, Dskip, dt_w, dt_b, Bp_w, Bp_b, Cp_w, Cp_b, out_w, out_b):
        import jax, jax.numpy as jnp
        import numpy as np
        D_MODEL = 256
        D_STATE = 16
        EXPAND = 2
        D_INNER = D_MODEL * EXPAND
        BATCH = 2
        SEQ = 1024
        K = 3
        pad = (K - 1) // 2
        xc = jax.lax.conv_general_dilated(x.transpose(0, 2, 1), conv_w, (1,), [(pad, pad)], dimension_numbers=('NCH', 'OIH', 'NCH'))
        xc = (xc + conv_b[None, :, None]).transpose(0, 2, 1)
        u = jax.nn.silu(jnp.einsum('ble,fe->blf', xc, in_w) + in_b)
        A = -jnp.exp(A_log)
        delta = jax.nn.softplus(jnp.einsum('ble,fe->blf', u, dt_w) + dt_b)
        Bt = jnp.einsum('ble,ne->bln', u, Bp_w) + Bp_b
        Ct = jnp.einsum('ble,ne->bln', u, Cp_w) + Cp_b

        def step(h, inp):
            d_, b_, c_, u_ = inp
            dA = jnp.exp(d_[..., None] * A)
            h = dA * h + (d_ * u_)[..., None] * b_[:, None, :]
            y = jnp.einsum('ben,bn->be', h, c_)
            return (h, y)
        h0 = jnp.zeros((x.shape[0], D_INNER, D_STATE), u.dtype)
        _, ys = jax.lax.scan(step, h0, (delta.transpose(1, 0, 2), Bt.transpose(1, 0, 2), Ct.transpose(1, 0, 2), u.transpose(1, 0, 2)))
        y = ys.transpose(1, 0, 2) + u * Dskip
        return jnp.einsum('ble,de->bld', y, out_w) + out_b

    def _L0_ffn_ref(x, gate_W, gate_b, W1, b1, g1, be1, W2, b2, g2, be2):
        import jax, jax.numpy as jnp
        import numpy as np
        LN_EPS = 1e-05

        def _layernorm(x, g, b):
            m = jnp.mean(x, axis=-1, keepdims=True)
            v = jnp.mean(jnp.square(x - m), axis=-1, keepdims=True)
            return (x - m) * jax.lax.rsqrt(v + LN_EPS) * g + b
        K_TOP = 2
        B, N, D = x.shape
        BN = B * N
        xf = x.reshape(BN, D)
        gate_scores = xf @ gate_W + gate_b
        topk_scores, topk_idx = jax.lax.top_k(gate_scores, K_TOP)
        weights = jax.nn.softmax(topk_scores, axis=-1)

        def expert(w1, bb1, gg1, bbe1, w2, bb2, gg2, bbe2):
            h = jax.nn.relu(_layernorm(xf @ w1 + bb1, gg1, bbe1))
            return _layernorm(h @ w2 + bb2, gg2, bbe2)
        all_out = jax.vmap(expert)(W1, b1, g1, be1, W2, b2, g2, be2)
        exp_out = all_out[topk_idx, jnp.arange(BN)[:, None]]
        out = jnp.sum(weights[..., None] * exp_out, axis=1)
        return (out + xf).reshape(B, N, D)

    def _L1_attn_ref(x, W_qkv, W_o):
        import math
        import jax, jax.numpy as jnp
        import numpy as np
        D = 256
        NH = 16
        DH = D // NH

        def _rope(q, k, base=10000.0):
            half = q.shape[-1] // 2
            freqs = jnp.arange(half, dtype=q.dtype) / half
            theta = 1.0 / base ** freqs
            t = jnp.arange(q.shape[-2], dtype=q.dtype)
            ang = t[:, None] * theta[None, :]
            cos = jnp.cos(ang)[None, None, :, :]
            sin = jnp.sin(ang)[None, None, :, :]

            def rot(x):
                x1, x2 = (x[..., :half], x[..., half:])
                return jnp.concatenate([x1 * cos - x2 * sin, x1 * sin + x2 * cos], axis=-1)
            return (rot(q), rot(k))
        B, T, d = x.shape
        qkv = x @ W_qkv
        q, k, v = jnp.split(qkv, 3, axis=-1)
        q = q.reshape(B, T, NH, DH).transpose(0, 2, 1, 3)
        k = k.reshape(B, T, NH, DH).transpose(0, 2, 1, 3)
        v = v.reshape(B, T, NH, DH).transpose(0, 2, 1, 3)
        q, k = _rope(q, k)
        att = jnp.einsum('bhtd,bhsd->bhts', q, k) / math.sqrt(DH)
        mask = jnp.triu(jnp.full((T, T), -jnp.inf, dtype=att.dtype), 1)
        att = att + mask
        w = jax.nn.softmax(att, axis=-1)
        y = jnp.einsum('bhts,bhsd->bhtd', w, v)
        y = y.transpose(0, 2, 1, 3).reshape(B, T, d)
        return y @ W_o

    def _L1_ffn_ref(x, tile_sigs, W, b):
        import math
        import jax, jax.numpy as jnp
        import numpy as np
        D_CONTENT = 256
        D_POSITION = 32
        NUM_TILES = 8
        BATCH = 8
        SEQ = 512

        def make_pe(seq_len, d_pos):
            pos = jnp.arange(seq_len, dtype=jnp.float32)[:, None]
            div = jnp.exp(jnp.arange(0, d_pos, 2, dtype=jnp.float32) * (-math.log(10000.0) / d_pos))
            ang = pos * div
            pe = jnp.zeros((seq_len, d_pos), dtype=jnp.float32)
            pe = pe.at[:, 0::2].set(jnp.sin(ang))
            pe = pe.at[:, 1::2].set(jnp.cos(ang))
            return pe
        B, S, D = x.shape
        P = tile_sigs.shape[1]
        pe = make_pe(S, P)
        scores = jnp.einsum('sp,tp->st', pe, jnp.sign(tile_sigs))
        idx = jnp.argmax(scores, axis=-1)
        y_all = jnp.einsum('bsd,tod->bsto', x, W) + b
        idx4 = jnp.broadcast_to(idx[None, :, None, None], (B, S, 1, D))
        out = jnp.take_along_axis(y_all, idx4, axis=2)[:, :, 0]
        return out
    h = _L0_tok_ref(x, L0_tok_embed_table, L0_tok_conv_w, L0_tok_conv_b, L0_tok_norm_w)
    h = h + _L0_attn_ref(_layernorm(h, axis=-1), L0_attn_conv_w, L0_attn_conv_b, L0_attn_in_w, L0_attn_in_b, L0_attn_A_log, L0_attn_Dskip, L0_attn_dt_w, L0_attn_dt_b, L0_attn_Bp_w, L0_attn_Bp_b, L0_attn_Cp_w, L0_attn_Cp_b, L0_attn_out_w, L0_attn_out_b)
    h = h + _L0_ffn_ref(_layernorm(h, axis=-1), L0_ffn_gate_W, L0_ffn_gate_b, L0_ffn_W1, L0_ffn_b1, L0_ffn_g1, L0_ffn_be1, L0_ffn_W2, L0_ffn_b2, L0_ffn_g2, L0_ffn_be2)
    h = h + _L1_attn_ref(_layernorm(h, axis=-1), L1_attn_W_qkv, L1_attn_W_o)
    h = h + _L1_ffn_ref(_layernorm(h, axis=-1), L1_ffn_tile_sigs, L1_ffn_W, L1_ffn_b)
    return h

_drawn_inputs = setup_inputs


def setup_inputs(seed=0):
    import zlib

    import numpy as np

    out = dict(_drawn_inputs(seed))
    spreads = {'L0_tok_norm_w': (1.0, 0.2),
     'L0_attn_conv_b': (0.0, 0.282),
     'L0_attn_in_b': (0.0, 0.1),
     'L0_attn_Dskip': (1.0, 0.2),
     'L0_attn_dt_b': (-4.0, 0.6),
     'L0_attn_Bp_b': (0.0, 0.8),
     'L0_attn_Cp_b': (0.0, 0.8),
     'L0_attn_out_b': (0.0, 0.1),
     'L0_ffn_gate_b': (0.0, 0.1),
     'L0_ffn_b1': (0.0, 0.1),
     'L0_ffn_g1': (1.0, 0.2),
     'L0_ffn_be1': (0.0, 0.1),
     'L0_ffn_b2': (0.0, 0.1),
     'L0_ffn_g2': (1.0, 0.2),
     'L0_ffn_be2': (0.0, 0.1)}
    factors = {'L0_attn_A_log': 8.0,
     'L0_attn_dt_w': 8.0,
     'L0_attn_Bp_w': 8.0,
     'L0_attn_Cp_w': 8.0,
     'L1_ffn_b': 3.659}
    for name, (base, spread) in spreads.items():
        noise = np.random.default_rng([zlib.crc32(name.encode()), seed]).standard_normal(out[name].shape)
        drawn = base * np.exp(spread * noise) if base else spread * noise
        out[name] = jnp.asarray(drawn.astype(out[name].dtype))
    for name, factor in factors.items():
        out[name] = (out[name] * factor).astype(out[name].dtype)
    return out
```

```python
from contextlib import ExitStack

import numpy as np

import concourse.bass as bass
from concourse import mybir

ALU = mybir.AluOpType
ACT = mybir.ActivationFunctionType
F32 = mybir.dt.float32
BF16 = mybir.dt.bfloat16
I32 = mybir.dt.int32
AX_X = mybir.AxisListType.X

P = 128
B = 8
S = 1024
D = 256
NT = S // P
DC = D // P
HALF = 512
NH = S // HALF
VOCAB = 64
TAPS = 4
E = 512
EC = E // P
NS = 16
K3 = 3
NE = 4
HEADS = 16
DH = 16
QUADS = HEADS // 4
TILES = 8
PDIM = 32
RMS_EPS = 1.1920929e-07
LN_EPS = 1e-05
MASKED = -1e30


class Signal:

    def __init__(self, sem, per_batch, start):
        self.sem, self.per_batch, self.start = sem, per_batch, start

    def at(self, b, n):
        return b * self.per_batch + (n + self.start)


class Chain:

    def __init__(self, eng, signal, base):
        self.eng, self.sem, self.base, self.n = eng, signal.sem, base, 0

    def step(self, ins):
        self.n += 1
        ins.then_inc(self.sem, 1)

    def settle(self):
        self.eng.wait_ge(self.sem, self.base + self.n)


MAX_GROUPS = [(i, c * HALF, min((i + 1) * P - c * HALF, HALF), (i * P) // HALF == c)
              for i in range(NT) for c in range(NH) if c * HALF < (i + 1) * P]
PROB_GROUPS = [(half, i, max(half * HALF, i * P), i * P >= half * HALF)
               for half in range(NH) for i in range(NT) if i * P < (half + 1) * HALF]
UNITS = 2 * len(MAX_GROUPS)
RING = 3


def build(nc, a, out):
    with ExitStack() as ctx:
        def sb(name, shape, dt=F32):
            return ctx.enter_context(nc.sbuf_tensor(name, shape, dt))

        def signal(name, per_batch=0, start=0):
            return Signal(ctx.enter_context(nc.semaphore(name)), per_batch, start)

        ident = sb("ident", [P, P])
        ident_bf = sb("ident_bf", [P, P], BF16)
        mask_rows = sb("mask_rows", [P, P], BF16)
        mask_cols = sb("mask_cols", [P, P], BF16)
        ones_row = sb("ones_row", [1, P])
        vocab_col = sb("vocab_col", [P, 1])
        table = sb("table", [P, 3, 2, 2 * D], BF16)
        minus_half = sb("minus_half", [P, NT])
        conv_in = sb("conv_in", [P, K3, DC, E])
        u_bias = sb("u_bias", [P, EC])
        in_b = sb("in_b", [P, EC])
        conv_b = sb("conv_b", [P, EC])
        dt_w = sb("dt_w", [P, EC, E])
        dt_b = sb("dt_b", [P, EC])
        bc_w = sb("bc_w", [P, EC, 2 * NS])
        bc_b = sb("bc_b", [2 * NS, 1])
        neg_a = sb("neg_a", [P, NS, EC])
        d_skip = sb("d_skip", [P, EC])
        out_w = sb("out_w", [P, EC, D])
        out_b = sb("out_b", [1, D])
        pick_state = sb("pick_state", [3 * 2 * NS, 2 * NS, P], BF16)
        gate_w = sb("gate_w", [P, DC, NE])
        gate_b = sb("gate_b", [1, NE])
        b1 = sb("b1", [1, NE, D])
        b2 = sb("b2", [1, NE, D])
        g1 = sb("g1", [P, NE, DC])
        be1 = sb("be1", [P, NE, DC])
        g2 = sb("g2", [P, NE, D])
        be2 = sb("be2", [P, NE, D])
        head_rot = sb("head_rot", [P, S])
        pair_sum = sb("pair_sum", [P, P])
        one_row16 = sb("one_row16", [P, 1])
        spread_den = sb("spread_den", [P, P])
        w_o = sb("w_o", [P, QUADS, D])
        route = sb("route", [P, NT, TILES])
        route_b = sb("route_b", [P, NT, D])
        w_stream = sb("w_stream", [P, 8 * DC * D])
        w_moe = w_stream[:, :].rearrange("p (l e c n) -> p l e c n", l=2, e=NE, c=DC)
        w_route = w_stream[:, :].rearrange("p (t c n) -> p t c n", t=TILES, c=DC)
        w_qkv = sb("w_qkv", [P, DC, 2 * P + 64])

        h = sb("h", [P, NT, D])
        xn = sb("xn", [P, NT, D])
        xT = sb("xT", [P, DC, S + 2])
        stats = sb("stats", [P, NT, 6])
        mv = sb("mv", [P, NT, 2])
        rstd = sb("rstd", [P, NT])
        scores4 = sb("scores4", [P, NT, NE])
        top = sb("top", [P, NT])
        beats = sb("beats", [P, NT, NE, NE])
        rank = sb("rank", [P, NT, NE])
        gate = sb("gate", [P, NT, NE])
        head_max = sb("head_max", [P, NT, 4])
        part_max = sb("part_max", [P, NT, NH, 4])

        buf_u = sb("buf_u", [P, EC * S])
        buf_delta = sb("buf_delta", [P, EC * S])
        buf_du = sb("buf_du", [P, EC * S])
        buf_y = sb("buf_y", [P, EC * S])
        buf_decay = sb("buf_decay", [P, EC * S])
        buf_scan = sb("buf_scan", [P, 2 * S])
        conv_in_w = buf_decay[:, 0:EC * K3 * D].rearrange("p (e k n) -> p e k n", e=EC, k=K3)
        in_w = buf_u[:, 0:EC * E].rearrange("p (e n) -> p e n", e=EC)
        tok_w = buf_delta[:, :].rearrange("p (c j n) -> p c j n", c=DC, j=TAPS)
        emb_T = buf_u[:, 2048:2048 + DC * VOCAB].rearrange("p (c v) -> p c v", c=DC)
        emb_rows = buf_u[:, 2304:2304 + 2 * D]
        tok_b = buf_u[:, 2816:2816 + 2 * D]
        pe_T = buf_u[0:PDIM, 3328:3328 + 512].bitcast(F32)
        table_f = buf_y[:, 0:1024]
        table_r = buf_y[:, 1024:2048]
        sigs_T = buf_y[0:PDIM, 2048:2048 + TILES]
        a_log = buf_y[:, 2064:2064 + NS * EC].rearrange("p (n c) -> p n c", c=EC)
        sign_T = buf_y[0:PDIM, 2136:2136 + TILES]
        route_T = buf_y[0:TILES, 2176:2176 + S]
        b_tiles = buf_y[0:TILES, 3200:3200 + D]
        best = buf_y[:, 3456:3456 + NT]
        taken = buf_y[:, 3472:3472 + NT]
        is_best = buf_y[:, 3488:3488 + NT * TILES].rearrange("p (i t) -> p i t", t=TILES)
        pe_full = buf_du[0:PDIM, 0:S]
        ids = buf_scan[:, :].bitcast(I32).rearrange("p (c s) -> p c s", c=2)
        onehot = buf_y[:, 0:S].bitcast(BF16).rearrange("p (c s) -> p c s", c=2)
        trig = buf_delta[:, :].rearrange("p (i n) -> p i n", i=NT)
        rotated = buf_du[:, 0:1024].rearrange("p (r n) -> p r n", r=2)
        norm_w = buf_decay[:, 3 * S:3 * S + D]
        squares = buf_du[:, 1024:1024 + NT * D].rearrange("p (i n) -> p i n", i=NT)
        square_sum = sb("square_sum", [P, NT])
        u = buf_u[:, :].rearrange("p (c s) -> p c s", c=EC)
        delta = buf_delta[:, :].rearrange("p (c s) -> p c s", c=EC)
        du = buf_du[:, :].rearrange("p (c s) -> p c s", c=EC)
        y = buf_y[:, :].rearrange("p (c s) -> p c s", c=EC)
        decay = buf_decay[:, :].rearrange("p (c s) -> p c s", c=EC)
        scan = buf_scan[:, :].rearrange("p (c s) -> p c s", c=2)
        drive = buf_u[:, 0:2 * S].rearrange("p (c s) -> p c s", c=2)
        c_rows = buf_u[:, 2 * S:4 * S].rearrange("p (c s) -> p c s", c=2)
        bc_full = buf_decay[0:2 * NS, 0:S]
        bc_rest = buf_decay[0:2 * NS, S:2 * S]
        bc_part = buf_decay[0:2 * NS, 2 * S:3 * S].bitcast(BF16)
        bc_parts = w_qkv[0:3 * 2 * NS, :, :].rearrange("p c n -> p (c n)")[:, 0:S // 2].bitcast(BF16)
        z = buf_du[:, 0:NT * D].rearrange("p (i n) -> p i n", i=NT)
        hid_T = buf_du[:, NT * D:].rearrange("p (c s) -> p c s", c=DC)
        qk_prod = buf_du[:, 0:2 * S].rearrange("p (r s) -> p r s", r=2)
        q_T = buf_y[:, 0:S]
        k_T = buf_y[:, S:2 * S]
        probs = buf_decay[:, 0:RING * S].rearrange("p (r j s) -> p r j s", r=RING, j=2)
        y_sum = buf_y[:, 2 * S:3 * S]
        y_rec = buf_y[:, 3 * S:4 * S]
        y_T = buf_u[:, 0:S]
        neg_max = buf_u[:, 2 * S:3 * S].rearrange("p (i j d) -> p i j d", i=NT, j=4)
        v_ext = buf_u[:, 3 * S:4 * S].rearrange("p (i j d) -> p i j d", i=NT, j=4)

        ps = ctx.enter_context(nc.psum_tensor("ps", [P, 8, HALF], F32))

        def tile_bank(i):
            return ps[:, i // 2, (i % 2) * D:(i % 2 + 1) * D]

        def span(i):
            return slice(1 + i * P, 1 + (i + 1) * P)

        weights_in = signal("weights_in")
        preset = signal("preset")
        prep_mm = signal("prep_mm")
        prep_act = signal("prep_act")
        prep_dve = signal("prep_dve")
        ids_clear = signal("ids_clear", 1)
        ids_in = signal("ids_in", 16 * TAPS)
        trig_in = signal("trig_in", 32)
        moe_w_in = signal("moe_w_in", 16)
        route_w_in = signal("route_w_in", 16)
        onehot_done = signal("onehot_done", 2)
        tok_mm = signal("tok_mm", NT)
        tok_rot = signal("tok_rot", NT)
        tok_sum = signal("tok_sum", NT)
        tok_sq = signal("tok_sq", NT)
        tok_scale = signal("tok_scale", 2)
        h_ready = signal("h_ready", 4)
        ln_stats = signal("ln_stats", 4)
        ln_rstd = signal("ln_rstd", 8)
        ln_norm = signal("ln_norm", 4 * NT)
        ln_turned = signal("ln_turned", 4 * NT // 2)
        xT_ready = signal("xT_ready", 4 * NT // 2)
        dve_chain_a = signal("dve_chain_a", 0)
        u_mm = signal("u_mm", EC * NH)
        u_ready = signal("u_ready", EC * NH)
        dt_mm = signal("dt_mm", EC * NH)
        dt_out = signal("dt_out", EC * NH)
        sp_exp = signal("sp_exp", EC)
        sp_ln = signal("sp_ln", EC)
        delta_ready = signal("delta_ready", EC)
        du_ready = signal("du_ready", EC)
        y_init = signal("y_init", EC)
        bc_mm = signal("bc_mm", 1)
        bc_split = signal("bc_split", 1)
        b_rows_mm = signal("b_rows_mm", NS)
        c_rows_mm = signal("c_rows_mm", NS)
        c_rows_out = signal("c_rows_out", NS, start=1)
        decay_ready = signal("decay_ready", NS * EC, start=1)
        drive_ready = signal("drive_ready", NS * EC, start=1)
        scan_ready = signal("scan_ready", NS * EC, start=1)
        read_out = signal("read_out", NS * EC, start=1)
        y_added = signal("y_added", NS * EC, start=1)
        mix_mm = signal("mix_mm", NT // 2)
        gate_mm = signal("gate_mm", 1)
        gate_shift = signal("gate_shift", 1)
        gate_exp = signal("gate_exp", 1)
        gate_ready = signal("gate_ready", 1)
        hid_mm = signal("hid_mm", NE * NT // 2)
        exp_stats = signal("exp_stats", 2 * NE)
        exp_rstd = signal("exp_rstd", 5 * NE)
        hid_norm = signal("hid_norm", NE * NT)
        hid_turned = signal("hid_turned", NE * NT // 2)
        hid_ready = signal("hid_ready", NE * NT // 2)
        out_mm = signal("out_mm", NE * NT // 2)
        out_norm = signal("out_norm", NE * NT, start=1)
        out_scaled = signal("out_scaled", NE * NT)
        qkv_in = signal("qkv_in", 16 * QUADS)
        att_clear = signal("att_clear", 2)
        qkv_mm = signal("qkv_mm", 3 * QUADS, start=1)
        qk_rot = signal("qk_rot", 2 * QUADS)
        v_ready = signal("v_ready", QUADS)
        qk_mm = signal("qk_mm", 2 * QUADS)
        qk_ready = signal("qk_ready", 2 * QUADS)
        raw_mm = signal("raw_mm", UNITS * QUADS)
        raw_max = signal("raw_max", UNITS * QUADS)
        max_ready = signal("max_ready", QUADS)
        max_turned = signal("max_turned", QUADS)
        q_shifted = signal("q_shifted", QUADS)
        score_mm = signal("score_mm", UNITS * QUADS)
        prob_ready = signal("prob_ready", UNITS * QUADS)
        pv_done = signal("pv_done", UNITS * QUADS)
        y_copied = signal("y_copied", NH * QUADS, start=1)
        den_mm = signal("den_mm", QUADS)
        y_rec_done = signal("y_rec_done", QUADS)
        y_norm = signal("y_norm", QUADS)
        wo_mm = signal("wo_mm", QUADS)
        att_added = signal("att_added", QUADS, start=1)
        route_mm = signal("route_mm", TILES, start=1)
        routed = signal("routed", TILES, start=1)
        h_final = signal("h_final", 1)
        stored = signal("stored", 16, start=1)
        dve_own = signal("dve_own", 0)

        loads = [
            (ident, a["c_ident"]), (vocab_col, a["c_vocab"]),
            (in_b, a["in_b"]), (conv_b, a["mix_conv_b"]), (dt_w, a["dt_w"]), (dt_b, a["dt_b"]), (bc_w, a["bc_w"]),
            (bc_b, a["bc_b"]), (d_skip, a["d_skip"]), (out_w, a["out_w"]), (out_b, a["out_b"]),
            (gate_w, a["gate_w"]), (gate_b, a["gate_b"]), (b1, a["b1"]), (b2, a["b2"]), (g1, a["g1"]),
            (be1, a["be1"]), (g2, a["g2"].partition_broadcast(P)), (be2, a["be2"].partition_broadcast(P)),
            (head_rot, a["c_head_rot"]), (pair_sum, a["c_pair_sum"]), (one_row16, a["c_one_row16"]),
            (spread_den, a["c_spread_den"]), (w_o, a["w_o"]), (pick_state, a["c_pick_state"].bitcast(BF16)),
            (ident_bf, a["c_ident_bf"].bitcast(BF16)), (mask_rows, a["c_mask_rows"].bitcast(BF16)), (mask_cols, a["c_mask_cols"].bitcast(BF16)),
            (conv_in_w, a["mix_conv_w"]), (in_w, a["in_w"]), (tok_w, a["tok_conv_w"]), (emb_T, a["emb_T"]),
            (emb_rows[VOCAB:P, :], a["emb_rows"]), (tok_b[VOCAB:P, :], a["tok_conv_b"].partition_broadcast(VOCAB)),
            (pe_full, a["c_pe_T"]), (sigs_T, a["sigs_T"]), (a_log, a["a_log"]), (b_tiles, a["route_b"]),
        ]
        ALL_IN = 16 * len(loads)

        def alone(eng):
            eng.sem_inc(passed.sem, 1)

        passed = signal("passed")

        block = ctx.enter_context(nc.Block())

        @block.sync
        def _(sp):
            for dst, src in loads:
                sp.dma_start(dst if isinstance(dst, bass.AP) else dst.ap(), src).then_inc(weights_in.sem, 16)
            sp.wait_ge(prep_mm.sem, PREP_MM)
            sp.wait_ge(prep_dve.sem, PREP_DVE)
            with sp.Fori(0, B) as b:
                sp.wait_ge(decay_ready.sem, decay_ready.at(b, 0))
                sp.wait_ge(scan_ready.sem, scan_ready.at(b, 0))
                sp.dma_start(trig, a["c_trig"]).then_inc(trig_in.sem, 16)
                sp.dma_start(norm_w, a["tok_norm_w"].partition_broadcast(P)).then_inc(trig_in.sem, 16)
                sp.wait_ge(ids_clear.sem, ids_clear.at(b, 1))
                for j in range(TAPS):
                    late = TAPS - 1 - j
                    half = slice((j % 2) * VOCAB, (j % 2 + 1) * VOCAB)
                    sp.dma_start(ids[half, j // 2, late:S],
                                 a["x"][b, 0:S - late].partition_broadcast(VOCAB)).then_inc(ids_in.sem, 16)
                sp.wait_ge(route_mm.sem, route_mm.at(b, 0))
                sp.dma_start(w_stream[:, :], a["w_moe"]).then_inc(moe_w_in.sem, 16)
                sp.wait_ge(out_mm.sem, out_mm.at(b, NE * NT // 2))
                sp.dma_start(w_stream[:, :], a["w_route"]).then_inc(route_w_in.sem, 16)
                with sp.Fori(0, QUADS) as g:
                    sp.wait_ge(qkv_mm.sem, qkv_mm.at(b, 0) + g * 3)
                    sp.dma_start(w_qkv[:, :, :], a["w_qkv"][g]).then_inc(qkv_in.sem, 16)
                sp.wait_ge(h_final.sem, h_final.at(b, 1))
                sp.dma_start(out[b].rearrange("(i p) n -> p i n", p=P), h[:, :, :]).then_inc(stored.sem, 16)
            sp.wait_ge(stored.sem, stored.at(B, 0))

        @block.gpsimd
        def _(pool):
            for s in (decay_ready, scan_ready, route_mm, qkv_mm, read_out, y_added, drive_ready, c_rows_out, out_norm, att_added, y_copied, routed, stored):
                pool.sem_inc(s.sem, s.start)
            pool.memset(xT[:, :, 0:1], 0.0).then_inc(preset.sem, 1)
            pool.memset(xT[:, :, S + 1:S + 2], 0.0).then_inc(preset.sem, 1)
            pool.memset(ones_row[:, :], 1.0).then_inc(preset.sem, 1)
            pool.memset(minus_half[:, :], -0.5).then_inc(preset.sem, 1)
            pool.memset(beats[:, :, :, :], 0.0).then_inc(preset.sem, 1)

            def root(src, scale, eps, done, first):
                nc.gpsimd.tensor_scalar(rstd[:, :], src, scale, eps, ALU.mult, ALU.add).then_inc(done.sem, 1)
                pool.wait_ge(done.sem, first)
                nc.gpsimd.tensor_tensor(rstd[:, :], rstd[:, :], minus_half[:, :], ALU.pow).then_inc(done.sem, 1)

            def layer_norm(b, k):
                pool.wait_ge(ln_stats.sem, ln_stats.at(b, k + 1))
                alone(pool)
                root(mv[:, :, 1], 1.0, LN_EPS, ln_rstd, ln_rstd.at(b, 2 * k + 1))

            pool.wait_ge(prep_dve.sem, PREP_DVE)
            with pool.Fori(0, B) as b:
                pool.wait_ge(read_out.sem, read_out.at(b, 0))
                alone(pool)
                pool.memset(ids[:, :, 0:TAPS - 1], -1).then_inc(ids_clear.sem, 1)
                pool.wait_ge(tok_sq.sem, tok_sq.at(b, NT))
                alone(pool)
                root(square_sum[:, :], 1.0 / D, RMS_EPS, tok_scale, tok_scale.at(b, 1))
                layer_norm(b, 0)
                for c in range(EC):
                    pool.wait_ge(u_ready.sem, u_ready.at(b, NH * (c + 1)))
                    alone(pool)
                    nc.gpsimd.tensor_scalar(y[:, c, :], u[:, c, :], d_skip[:, c:c + 1], None,
                                            ALU.mult).then_inc(y_init.sem, 1)
                for c in range(EC):
                    pool.wait_ge(delta_ready.sem, delta_ready.at(b, c + 1))
                    nc.gpsimd.tensor_tensor(du[:, c, :], delta[:, c, :], u[:, c, :],
                                            ALU.mult).then_inc(du_ready.sem, 1)
                pool.wait_ge(y_init.sem, y_init.at(b, EC))
                alone(pool)
                with pool.Fori(0, NS) as n:
                    for c in range(EC):
                        pool.wait_ge(read_out.sem, read_out.at(b, 1 + c) + n * EC)
                        pool.wait_ge(y_added.sem, y_added.at(b, 0) + n * EC)
                        nc.gpsimd.tensor_tensor(y[:, c, :], y[:, c, :], scan[:, c % 2, :],
                                                ALU.add).then_inc(y_added.sem, 1)
                layer_norm(b, 1)
                with pool.Fori(0, NE) as e:
                    base = exp_rstd.at(b, 0) + e * 5
                    pool.wait_ge(exp_stats.sem, exp_stats.at(b, 1) + e * 2)
                    alone(pool)
                    root(mv[:, :, 1], 1.0, LN_EPS, exp_rstd, base + 1)
                    pool.wait_ge(exp_stats.sem, exp_stats.at(b, 2) + e * 2)
                    alone(pool)
                    root(mv[:, :, 1], 1.0, LN_EPS, exp_rstd, base + 3)
                    pool.wait_ge(exp_rstd.sem, base + 4)
                    alone(pool)
                    nc.gpsimd.tensor_tensor(rstd[:, :], rstd[:, :], gate[:, :, e],
                                            ALU.mult).then_inc(exp_rstd.sem, 1)
                    for i in range(NT):
                        pool.wait_ge(out_norm.sem, out_norm.at(b, i + 1) + e * NT)
                        alone(pool)
                        nc.gpsimd.tensor_tensor(z[:, i, :], z[:, i, :], g2[:, e, :],
                                                ALU.mult).then_inc(out_scaled.sem, 1)
                pool.memset(neg_max[:, :, :, :], 0.0).then_inc(att_clear.sem, 1)
                pool.memset(v_ext[:, :, :, :], 0.0).then_inc(att_clear.sem, 1)
                layer_norm(b, 2)
                layer_norm(b, 3)

        @block.scalar
        def _(act):
            act.wait_ge(weights_in.sem, ALL_IN)
            nc.scalar.activation(neg_a[:, :, :], a_log, ACT.Exp).then_inc(prep_act.sem, 1)
            nc.scalar.activation(sign_T, sigs_T, ACT.Sign).then_inc(prep_act.sem, 1)
            for n in range(K3 * DC):
                act.wait_ge(prep_mm.sem, n + 1)
                nc.scalar.activation(conv_in[:, n // DC, n % DC, :], ps[:, n % 4, :],
                                     ACT.Copy).then_inc(prep_act.sem, 1)

            def copy_turned(b, k):
                for p in range(NT // 2):
                    act.wait_ge(ln_turned.sem, ln_turned.at(b, k * 4 + p + 1))
                    nc.scalar.activation(xT[:, :, 1 + 2 * P * p:1 + 2 * P * (p + 1)],
                                         ps[:, 6 + p % 2, :].rearrange("p (c s) -> p c s", c=DC),
                                         ACT.Copy).then_inc(xT_ready.sem, 1)

            act.wait_ge(prep_dve.sem, PREP_DVE)
            with act.Fori(0, B) as b:
                for i in range(NT):
                    act.wait_ge(tok_sum.sem, tok_sum.at(b, i + 1))
                    nc.scalar.activation(squares[:, i, :], h[:, i, :], ACT.Square,
                                         accum_out=square_sum[:, i:i + 1]).then_inc(tok_sq.sem, 1)
                copy_turned(b, 0)
                for n in range(EC * NH):
                    c, half = n // NH, n % NH
                    act.wait_ge(u_mm.sem, u_mm.at(b, n + 1))
                    nc.scalar.activation(u[:, c, half * HALF:(half + 1) * HALF], ps[:, n % 4, :], ACT.Silu,
                                         bias=u_bias[:, c:c + 1]).then_inc(u_ready.sem, 1)
                for n in range(EC * NH):
                    c, half = n // NH, n % NH
                    act.wait_ge(dt_mm.sem, dt_mm.at(b, n + 1))
                    cols = slice(half * HALF, (half + 1) * HALF)
                    nc.scalar.activation(delta[:, c, cols], ps[:, n % 4, :], ACT.Abs, bias=dt_b[:, c:c + 1])
                    nc.scalar.activation(du[:, c, cols], ps[:, n % 4, :], ACT.Relu,
                                         bias=dt_b[:, c:c + 1]).then_inc(dt_out.sem, 1)
                for c in range(EC):
                    act.wait_ge(dt_out.sem, dt_out.at(b, NH * (c + 1)))
                    nc.scalar.activation(delta[:, c, :], delta[:, c, :], ACT.Exp,
                                         scale=-1.0).then_inc(sp_exp.sem, 1)
                for c in range(EC):
                    act.wait_ge(sp_exp.sem, sp_exp.at(b, c + 1))
                    nc.scalar.activation(delta[:, c, :], delta[:, c, :], ACT.Ln,
                                         bias=1.0).then_inc(sp_ln.sem, 1)
                act.wait_ge(bc_split.sem, bc_split.at(b, 1))
                act.wait_ge(delta_ready.sem, delta_ready.at(b, EC))
                act.wait_ge(du_ready.sem, du_ready.at(b, EC))
                alone(act)
                with act.Fori(0, NS // 2) as m:
                    for k in range(2):
                        states = m * 2 + k
                        act.wait_ge(c_rows_mm.sem, c_rows_mm.at(b, 1) + states)
                        act.wait_ge(read_out.sem, read_out.at(b, 0) + m * (2 * EC))
                        nc.scalar.activation(c_rows[:, k, :],
                                             ps[:, 4 + 2 * k:6 + 2 * k, :].rearrange("p r s -> p (r s)"),
                                             ACT.Copy).then_inc(c_rows_out.sem, 1)
                        for c in range(EC):
                            act.wait_ge(scan_ready.sem, scan_ready.at(b, 0) + states * EC)
                            alone(act)
                            nc.scalar.activation(decay[:, c, :], delta[:, c, :], ACT.Exp,
                                                 scale=neg_a[:, states, c:c + 1]).then_inc(decay_ready.sem, 1)
                copy_turned(b, 1)
                act.wait_ge(gate_shift.sem, gate_shift.at(b, 1))
                nc.scalar.activation(gate[:, :, :], gate[:, :, :], ACT.Exp).then_inc(gate_exp.sem, 1)
                with act.Fori(0, NE) as e:
                    for p in range(NT // 2):
                        act.wait_ge(hid_turned.sem, hid_turned.at(b, p + 1) + e * (NT // 2))
                        alone(act)
                        for c in range(DC):
                            last = nc.scalar.activation(hid_T[:, c, 2 * P * p:2 * P * (p + 1)],
                                                        ps[:, 6 + p % 2, c * 2 * P:(c + 1) * 2 * P], ACT.Relu,
                                                        bias=be1[:, e, c:c + 1], scale=g1[:, e, c:c + 1])
                        last.then_inc(hid_ready.sem, 1)
                copy_turned(b, 2)
                with act.Fori(0, QUADS) as g:
                    act.wait_ge(qk_mm.sem, qk_mm.at(b, 1) + g * 2)
                    nc.scalar.activation(q_T, ps[:, 0:2, :].rearrange("p r s -> p (r s)"),
                                         ACT.Copy).then_inc(qk_ready.sem, 1)
                    act.wait_ge(qk_mm.sem, qk_mm.at(b, 2) + g * 2)
                    nc.scalar.activation(k_T, ps[:, 2:4, :].rearrange("p r s -> p (r s)"), ACT.Identity,
                                         bias=one_row16[:, 0:1]).then_inc(qk_ready.sem, 1)
                    n = 0
                    for half, i, t0, diag in PROB_GROUPS:
                        cols = (half + 1) * HALF - t0
                        for pair in range(2):
                            act.wait_ge(score_mm.sem, score_mm.at(b, n + 1) + g * UNITS)
                            if n >= RING:
                                act.wait_ge(pv_done.sem, pv_done.at(b, n + 1 - RING) + g * UNITS)
                            slot = n % RING
                            nc.scalar.activation(probs[:, slot, :, 0:cols], ps[:, 2 * slot:2 * slot + 2, 0:cols],
                                                 ACT.Exp, scale=float(DH) ** -0.5).then_inc(prob_ready.sem, 1)
                            n += 1
                        if i == (half + 1) * (NT // NH) - 1:
                            act.wait_ge(pv_done.sem, pv_done.at(b, n) + g * UNITS)
                            nc.scalar.activation(y_sum[:, half * HALF:(half + 1) * HALF], ps[:, 6 + half, :],
                                                 ACT.Copy).then_inc(y_copied.sem, 1)
                copy_turned(b, 3)

        @block.tensor
        def _(pe):
            mm = nc.tensor.matmul
            pe.wait_ge(weights_in.sem, ALL_IN)
            pe.wait_ge(preset.sem, 5)
            for n in range(K3 * DC):
                k, c = n // DC, n % DC
                if n >= 4:
                    pe.wait_ge(prep_act.sem, 2 + n - 3)
                for e in range(EC):
                    last = mm(ps[:, n % 4, :], conv_in_w[:, e, k, c * P:(c + 1) * P], in_w[:, e, :],
                              start=(e == 0), stop=(e == EC - 1))
                last.then_inc(prep_mm.sem, 1)
            for f in range(EC):
                for e in range(EC):
                    last = mm(ps[:, 6, f:f + 1], in_w[:, e, f * P:(f + 1) * P], conv_b[:, e:e + 1],
                              start=(e == 0), stop=(e == EC - 1))
            last.then_inc(prep_mm.sem, 1)
            for j in range(TAPS):
                for c in range(DC):
                    last = mm(ps[(j % 2) * VOCAB:(j % 2 + 1) * VOCAB, 4 + j // 2, :], emb_T[:, c, :],
                              tok_w[:, c, j, :], start=(c == 0), stop=(c == DC - 1))
            last.then_inc(prep_mm.sem, 1)
            pe.wait_ge(prep_act.sem, 2)
            for i in range(NT):
                last = mm(ps[:, 7, i * TILES:(i + 1) * TILES], pe_full[:, i * P:(i + 1) * P], sign_T,
                          start=True, stop=True)
            last.then_inc(prep_mm.sem, 1)
            pe.wait_ge(prep_dve.sem, PREP_ROUTE)
            pe.wait_ge(prep_act.sem, 2 + K3 * DC)
            for i in range(NT):
                last = nc.tensor.transpose(ps[0:TILES, i // 4, (i % 4) * P:(i % 4 + 1) * P], route[:, i, :],
                                           ident[:, :])
            last.then_inc(prep_mm.sem, 1)
            pe.wait_ge(prep_dve.sem, PREP_ROUTE + 1)
            for i in range(NT):
                last = mm(tile_bank(i), route_T[:, i * P:(i + 1) * P], b_tiles, start=True, stop=True)
            last.then_inc(prep_mm.sem, 1)
            pe.wait_ge(prep_dve.sem, PREP_DVE)

            def turn(b, k):
                for p in range(NT // 2):
                    pe.wait_ge(ln_norm.sem, ln_norm.at(b, k * NT + 2 * p + 2))
                    if p >= 2:
                        pe.wait_ge(xT_ready.sem, xT_ready.at(b, k * 4 + p - 1))
                    for c in range(DC):
                        for r in range(2):
                            last = nc.tensor.transpose(ps[:, 6 + p % 2, (2 * c + r) * P:(2 * c + r + 1) * P],
                                                       xn[:, 2 * p + r, c * P:(c + 1) * P], ident[:, :])
                    last.then_inc(ln_turned.sem, 1)

            with pe.Fori(0, B) as b:
                pe.wait_ge(onehot_done.sem, onehot_done.at(b, 2))
                for i in range(NT):
                    if i >= 2:
                        pe.wait_ge(tok_rot.sem, tok_rot.at(b, i - 1))
                    n = 0
                    for c in range(2):
                        for part in range(3):
                            last = mm(ps[:, i % 2, :], onehot[:, c, i * P:(i + 1) * P], table[:, part, c, :],
                                      start=(n == 0), stop=(n == 5))
                            n += 1
                    last.then_inc(tok_mm.sem, 1)
                turn(b, 0)
                pe.wait_ge(xT_ready.sem, xT_ready.at(b, 4))
                for n in range(EC * NH):
                    f, half = n // NH, n % NH
                    if n >= 4:
                        pe.wait_ge(u_ready.sem, u_ready.at(b, n - 3))
                    for m in range(K3 * DC):
                        k, c = m // DC, m % DC
                        last = mm(ps[:, n % 4, :], conv_in[:, k, c, f * P:(f + 1) * P],
                                  xT[:, c, half * HALF + k:half * HALF + k + HALF],
                                  start=(m == 0), stop=(m == K3 * DC - 1))
                    last.then_inc(u_mm.sem, 1)
                pe.wait_ge(u_ready.sem, u_ready.at(b, EC * NH))
                for n in range(EC * NH):
                    f, half = n // NH, n % NH
                    if n >= 4:
                        pe.wait_ge(dt_out.sem, dt_out.at(b, n - 3))
                    for e in range(EC):
                        last = mm(ps[:, n % 4, :], dt_w[:, e, f * P:(f + 1) * P],
                                  u[:, e, half * HALF:(half + 1) * HALF], start=(e == 0), stop=(e == EC - 1))
                    last.then_inc(dt_mm.sem, 1)
                for half in range(NH):
                    for e in range(EC):
                        last = mm(ps[0:2 * NS, 4 + half, :], bc_w[:, e, :],
                                  u[:, e, half * HALF:(half + 1) * HALF], start=(e == 0), stop=(e == EC - 1))
                last.then_inc(bc_mm.sem, 1)
                pe.wait_ge(bc_split.sem, bc_split.at(b, 1))
                pe.wait_ge(dt_out.sem, dt_out.at(b, EC * NH))
                alone(pe)
                with pe.Fori(0, NS // 2) as m:
                    for k in range(2):
                        states = m * 2 + k
                        pe.wait_ge(drive_ready.sem, drive_ready.at(b, 0) + m * (2 * EC))
                        for half in range(NH):
                            last = mm(ps[:, 2 * k + half, :], pick_state[:, states, :],
                                      bc_parts[:, half * HALF:(half + 1) * HALF], start=True, stop=True)
                        last.then_inc(b_rows_mm.sem, 1)
                        pe.wait_ge(c_rows_out.sem, c_rows_out.at(b, 0) + m * 2)
                        for half in range(NH):
                            last = mm(ps[:, 4 + 2 * k + half, :], pick_state[:, states + NS, :],
                                      bc_parts[:, half * HALF:(half + 1) * HALF], start=True, stop=True)
                        last.then_inc(c_rows_mm.sem, 1)
                pe.wait_ge(y_added.sem, y_added.at(b, NS * EC))
                for i in range(NT):
                    for e in range(EC):
                        mm(tile_bank(i), y[:, e, i * P:(i + 1) * P], out_w[:, e, :], start=(e == 0), stop=False)
                    last = mm(tile_bank(i), ones_row[:, :], out_b[:, :], start=False, stop=True)
                    if i % 2:
                        last.then_inc(mix_mm.sem, 1)
                turn(b, 1)
                pe.wait_ge(xT_ready.sem, xT_ready.at(b, 8))
                for i in range(NT):
                    for c in range(DC):
                        mm(ps[:, 4, i * NE:(i + 1) * NE], xT[:, c, span(i)], gate_w[:, c, :],
                           start=(c == 0), stop=False)
                    last = mm(ps[:, 4, i * NE:(i + 1) * NE], ones_row[:, :], gate_b[:, :], start=False, stop=True)
                last.then_inc(gate_mm.sem, 1)
                pe.wait_ge(moe_w_in.sem, moe_w_in.at(b, 16))
                alone(pe)
                with pe.Fori(0, NE) as e:
                    for i in range(NT):
                        pe.wait_ge(out_norm.sem, out_norm.at(b, 0) + e * NT)
                        alone(pe)
                        for c in range(DC):
                            mm(tile_bank(i), xT[:, c, span(i)], w_moe[:, 0, e, c, :], start=(c == 0), stop=False)
                        last = mm(tile_bank(i), ones_row[:, :], b1[:, e, :], start=False, stop=True)
                        if i % 2:
                            last.then_inc(hid_mm.sem, 1)
                    for p in range(NT // 2):
                        pe.wait_ge(hid_norm.sem, hid_norm.at(b, 2 * p + 2) + e * NT)
                        if p >= 2:
                            pe.wait_ge(hid_ready.sem, hid_ready.at(b, p - 1) + e * (NT // 2))
                        for c in range(DC):
                            for r in range(2):
                                last = nc.tensor.transpose(ps[:, 6 + p % 2, (2 * c + r) * P:(2 * c + r + 1) * P],
                                                           z[:, 2 * p + r, c * P:(c + 1) * P], ident[:, :])
                        last.then_inc(hid_turned.sem, 1)
                    for i in range(NT):
                        pe.wait_ge(hid_ready.sem, hid_ready.at(b, i // 2 + 1) + e * (NT // 2))
                        for c in range(DC):
                            mm(tile_bank(i), hid_T[:, c, i * P:(i + 1) * P], w_moe[:, 1, e, c, :],
                               start=(c == 0), stop=False)
                        last = mm(tile_bank(i), ones_row[:, :], b2[:, e, :], start=False, stop=True)
                        if i % 2:
                            last.then_inc(out_mm.sem, 1)
                turn(b, 2)
                pe.wait_ge(xT_ready.sem, xT_ready.at(b, 12))
                alone(pe)
                with pe.Fori(0, QUADS) as g:
                    pe.wait_ge(qkv_in.sem, qkv_in.at(b, 16) + g * 16)
                    pe.wait_ge(att_added.sem, att_added.at(b, 0) + g)
                    for r in range(2):
                        for half in range(NH):
                            for c in range(DC):
                                last = mm(ps[:, 2 * r + half, :], w_qkv[:, c, r * P:(r + 1) * P],
                                          xT[:, c, 1 + half * HALF:1 + (half + 1) * HALF],
                                          start=(c == 0), stop=(c == DC - 1))
                        last.then_inc(qkv_mm.sem, 1)
                    for i in range(NT):
                        for c in range(DC):
                            last = mm(ps[:, 4, i * 64:(i + 1) * 64], xT[:, c, span(i)], w_qkv[:, c, 2 * P:2 * P + 64],
                                      start=(c == 0), stop=(c == DC - 1))
                    last.then_inc(qkv_mm.sem, 1)
                    for r in range(2):
                        pe.wait_ge(qk_rot.sem, qk_rot.at(b, r + 1) + g * 2)
                        for half in range(NH):
                            last = mm(ps[:, 2 * r + half, :], pair_sum[:, :],
                                      qk_prod[:, r, half * HALF:(half + 1) * HALF], start=True, stop=True)
                        last.then_inc(qk_mm.sem, 1)
                    pe.wait_ge(qk_ready.sem, qk_ready.at(b, 2) + g * 2)
                    pe.wait_ge(v_ready.sem, v_ready.at(b, 1) + g)
                    n = 0
                    for i, s0, cols, diag in MAX_GROUPS:
                        for pair in range(2):
                            if n >= RING:
                                pe.wait_ge(raw_max.sem, raw_max.at(b, n + 1 - RING) + g * UNITS)
                            for jj in range(2):
                                rows = slice((2 * pair + jj) * 32, (2 * pair + jj + 1) * 32)
                                bank = 2 * (n % RING) + jj
                                last = mm(ps[:, bank, 0:cols], q_T[rows, i * P:(i + 1) * P],
                                          k_T[rows, s0:s0 + cols], start=True, stop=not diag)
                            if diag:
                                for jj in range(2):
                                    last = mm(ps[:, 2 * (n % RING) + jj, cols - P:cols], ident_bf[:, :],
                                              mask_rows[:, :], start=False, stop=True)
                            last.then_inc(raw_mm.sem, 1)
                            n += 1
                    pe.wait_ge(raw_max.sem, raw_max.at(b, UNITS) + g * UNITS)
                    pe.wait_ge(max_ready.sem, max_ready.at(b, 1) + g)
                    for i in range(NT):
                        last = mm(ps[:, i // 4, (i % 4) * P:(i % 4 + 1) * P],
                                  neg_max[:, i, :, :].rearrange("p j d -> p (j d)"), ident[:, :],
                                  start=True, stop=True)
                    last.then_inc(max_turned.sem, 1)
                    pe.wait_ge(q_shifted.sem, q_shifted.at(b, 1) + g)

                    def weigh(n, half, i, t0, pair):
                        cols = (half + 1) * HALF - t0
                        pe.wait_ge(prob_ready.sem, prob_ready.at(b, n + 1) + g * UNITS)
                        if i == 0 and pair == 0 and half == 0:
                            pe.wait_ge(y_copied.sem, y_copied.at(b, 0) + g * NH)
                        for jj in range(2):
                            j = 2 * pair + jj
                            last = mm(ps[32 * j:32 * j + 32, 6 + half, t0 - half * HALF:HALF], v_ext[:, i, j, :],
                                      probs[:, n % RING, jj, 0:cols], start=(i == 0),
                                      stop=(i == (half + 1) * (NT // NH) - 1))
                        last.then_inc(pv_done.sem, 1)

                    n = 0
                    behind = []
                    for half, i, t0, diag in PROB_GROUPS:
                        cols = (half + 1) * HALF - t0
                        for pair in range(2):
                            if n >= RING:
                                pe.wait_ge(prob_ready.sem, prob_ready.at(b, n + 1 - RING) + g * UNITS)
                            for jj in range(2):
                                rows = slice((2 * pair + jj) * 32, (2 * pair + jj + 1) * 32)
                                last = mm(ps[:, 2 * (n % RING) + jj, 0:cols], k_T[rows, i * P:(i + 1) * P],
                                          q_T[rows, t0:t0 + cols], start=True, stop=not diag)
                            if diag:
                                for jj in range(2):
                                    last = mm(ps[:, 2 * (n % RING) + jj, 0:P], ident_bf[:, :],
                                              mask_cols[:, :], start=False, stop=True)
                            last.then_inc(score_mm.sem, 1)
                            behind.append((n, half, i, t0, pair))
                            if len(behind) == RING:
                                weigh(*behind.pop(0))
                            n += 1
                    while behind:
                        weigh(*behind.pop(0))
                    pe.wait_ge(prob_ready.sem, prob_ready.at(b, UNITS) + g * UNITS)
                    pe.wait_ge(y_copied.sem, y_copied.at(b, NH) + g * NH)
                    for half in range(NH):
                        last = mm(ps[:, half, :], spread_den[:, :], y_sum[:, half * HALF:(half + 1) * HALF],
                                  start=True, stop=True)
                    last.then_inc(den_mm.sem, 1)
                    pe.wait_ge(y_norm.sem, y_norm.at(b, 1) + g)
                    for i in range(NT):
                        last = mm(ps[:, 2 + i // 2, (i % 2) * D:(i % 2 + 1) * D], y_T[:, i * P:(i + 1) * P],
                                  w_o[:, g, :], start=True, stop=True)
                    last.then_inc(wo_mm.sem, 1)
                pe.wait_ge(att_added.sem, att_added.at(b, QUADS))
                turn(b, 3)
                pe.wait_ge(xT_ready.sem, xT_ready.at(b, 16))
                pe.wait_ge(route_w_in.sem, route_w_in.at(b, 16))
                alone(pe)
                with pe.Fori(0, TILES // 2) as m:
                    for k in range(2):
                        pe.wait_ge(routed.sem, routed.at(b, 0) + m * 2)
                        for i in range(NT):
                            for c in range(DC):
                                last = mm(ps[:, 4 * k + i // 2, (i % 2) * D:(i % 2 + 1) * D], xT[:, c, span(i)],
                                          w_route[:, m * 2 + k, c, :], start=(c == 0), stop=(c == DC - 1))
                        last.then_inc(route_mm.sem, 1)

        @block.vector
        def _(dve):
            tt, ts = nc.vector.tensor_tensor, nc.vector.tensor_scalar
            own = Chain(dve, prep_dve, 0)
            dve.wait_ge(weights_in.sem, ALL_IN)
            dve.wait_ge(preset.sem, 5)
            dve.wait_ge(prep_act.sem, 1)
            own.step(ts(neg_a[:, :, :], neg_a[:, :, :], -1.0, None, ALU.mult))
            dve.wait_ge(prep_mm.sem, K3 * DC + 3)
            pos_scores = ps[:, 7, 0:NT * TILES].rearrange("p (i t) -> p i t", t=TILES)
            own.step(nc.vector.tensor_reduce(best, pos_scores, AX_X, ALU.max))
            own.step(nc.vector.memset(taken, 0.0))
            own.settle()
            own.step(tt(is_best, pos_scores, best.unsqueeze(2).to_broadcast([P, NT, TILES]), ALU.is_ge))
            own.settle()
            for t in range(TILES):
                own.step(tt(route[:, :, t], is_best[:, :, t], taken, ALU.is_gt))
                own.settle()
                own.step(tt(taken, taken, is_best[:, :, t], ALU.max))
                own.settle()
            assert own.n == PREP_ROUTE, own.n
            dve.wait_ge(prep_mm.sem, K3 * DC + 4)
            own.step(nc.vector.tensor_copy(route_T, ps[0:TILES, 0:2, :].rearrange("p r s -> p (r s)")))
            dve.wait_ge(prep_mm.sem, K3 * DC + 5)
            own.step(nc.vector.tensor_copy(route_b[:, :, :].rearrange("p i n -> p (i n)"),
                                           ps[:, 0:4, :].rearrange("p r s -> p (r s)")))
            own.step(tt(u_bias[:, :], ps[:, 6, 0:EC], in_b[:, :], ALU.add))
            own.step(nc.vector.tensor_copy(table_f, ps[:, 4:6, :].rearrange("p r s -> p (r s)")))
            own.settle()
            last_tap = table_f[VOCAB:P, 2 * D:4 * D]
            own.step(tt(last_tap, last_tap, emb_rows[VOCAB:P, :], ALU.add))
            own.settle()
            own.step(tt(last_tap, last_tap, tok_b[VOCAB:P, :], ALU.add))
            own.settle()
            src = table_f
            for part in range(3):
                dst = table[:, part, :, :].rearrange("p c n -> p (c n)")
                own.step(nc.vector.tensor_copy(dst, src))
                own.settle()
                if part < 2:
                    own.step(tt(table_r, src, dst, ALU.subtract))
                    own.settle()
                    src = table_r
            assert own.n == PREP_DVE, own.n

            def layer_norm(b, k):
                for i in range(NT):
                    nc.vector.bn_stats(stats[:, i, :], h[:, i, :])
                dve.drain()
                for i in range(NT):
                    last = nc.vector.bn_aggr(mv[:, i, :], stats[:, i, :])
                last.then_inc(ln_stats.sem, 1)
                dve.wait_ge(ln_rstd.sem, ln_rstd.at(b, 2 * k + 2))
                for i in range(NT):
                    ts(xn[:, i, :], h[:, i, :], mv[:, i, 0:1], rstd[:, i:i + 1], ALU.subtract,
                       ALU.mult).then_inc(ln_norm.sem, 1)

            all_h = h[:, :, :].rearrange("p i n -> p (i n)")
            with dve.Fori(0, B) as b:
                dve.wait_ge(ids_in.sem, ids_in.at(b, 16 * TAPS))
                for c in range(2):
                    ts(onehot[:, c, :], ids[:, c, :], vocab_col[:, 0:1], None, ALU.is_equal)\
                        .then_inc(onehot_done.sem, 1)
                dve.wait_ge(trig_in.sem, trig_in.at(b, 32))
                dve.wait_ge(stored.sem, stored.at(b, 0))
                for i in range(NT):
                    dve.wait_ge(tok_mm.sem, tok_mm.at(b, i + 1))
                    tt(rotated[:, i % 2, :], ps[:, i % 2, :], trig[:, i, :], ALU.mult).then_inc(tok_rot.sem, 1)
                    dve.wait_ge(tok_rot.sem, tok_rot.at(b, i + 1))
                    tt(h[:, i, :], rotated[:, i % 2, 0:D], rotated[:, i % 2, D:2 * D],
                       ALU.add).then_inc(tok_sum.sem, 1)
                dve.wait_ge(tok_scale.sem, tok_scale.at(b, 2))
                for i in range(NT):
                    nc.vector.scalar_tensor_tensor(h[:, i, :], h[:, i, :], rstd[:, i:i + 1], norm_w[:, :],
                                                   ALU.mult, ALU.mult)
                dve.drain()
                layer_norm(b, 0)
                for c in range(EC):
                    dve.wait_ge(sp_ln.sem, sp_ln.at(b, c + 1))
                    tt(delta[:, c, :], delta[:, c, :], du[:, c, :], ALU.add).then_inc(delta_ready.sem, 1)
                dve.wait_ge(bc_mm.sem, bc_mm.at(b, 1))
                ts(bc_full, ps[0:2 * NS, 4:6, :].rearrange("p r s -> p (r s)"), bc_b[:, 0:1], None, ALU.add)
                dve.drain()
                nc.vector.tensor_copy(bc_parts[0:2 * NS, :], bc_full)
                dve.drain()
                tt(bc_rest, bc_full, bc_parts[0:2 * NS, :], ALU.subtract)
                dve.drain()
                nc.vector.tensor_copy(bc_part[:, 0:S], bc_rest)
                dve.drain()
                nc.vector.tensor_copy(bc_parts[2 * NS:4 * NS, :], bc_part[:, 0:S])
                tt(bc_rest, bc_rest, bc_part[:, 0:S], ALU.subtract)
                dve.drain()
                nc.vector.tensor_copy(bc_parts[4 * NS:6 * NS, :], bc_rest).then_inc(bc_split.sem, 1)
                dve.wait_ge(du_ready.sem, du_ready.at(b, EC))
                alone(dve)
                with dve.Fori(0, NS // 2) as m:
                    for k in range(2):
                        base = m * (2 * EC) + k * EC

                        def make_drive(c):
                            tt(drive[:, c % 2, :], du[:, c, :], ps[:, 2 * k:2 * k + 2, :].rearrange("p r s -> p (r s)"),
                               ALU.mult).then_inc(drive_ready.sem, 1)

                        def make_readout(c):
                            dve.wait_ge(scan_ready.sem, scan_ready.at(b, c + 1) + base)
                            tt(scan[:, c % 2, :], scan[:, c % 2, :], c_rows[:, k, :],
                               ALU.mult).then_inc(read_out.sem, 1)

                        dve.wait_ge(b_rows_mm.sem, b_rows_mm.at(b, k + 1) + m * 2)
                        make_drive(0)
                        for c in range(EC):
                            if c + 1 < EC:
                                make_drive(c + 1)
                            if c == 0:
                                dve.wait_ge(c_rows_out.sem, c_rows_out.at(b, k + 1) + m * 2)
                            dve.wait_ge(decay_ready.sem, decay_ready.at(b, c + 1) + base)
                            dve.wait_ge(drive_ready.sem, drive_ready.at(b, c + 1) + base)
                            if c < 2:
                                dve.wait_ge(y_added.sem, y_added.at(b, 0) + base)
                            else:
                                dve.wait_ge(y_added.sem, y_added.at(b, c - 1) + base)
                            nc.vector.tensor_tensor_scan(scan[:, c % 2, :], decay[:, c, :], drive[:, c % 2, :],
                                                         0.0, ALU.mult, ALU.add).then_inc(scan_ready.sem, 1)
                            make_readout(c)
                for p in range(NT // 2):
                    dve.wait_ge(mix_mm.sem, mix_mm.at(b, p + 1))
                    tt(all_h[:, p * HALF:(p + 1) * HALF], all_h[:, p * HALF:(p + 1) * HALF], ps[:, p, :], ALU.add)
                dve.drain()
                layer_norm(b, 1)
                all_xn = xn[:, :, :].rearrange("p i n -> p (i n)")
                dve.drain()
                tt(all_h, all_h, all_xn, ALU.add)
                dve.wait_ge(gate_mm.sem, gate_mm.at(b, 1))
                nc.vector.tensor_copy(scores4[:, :, :], ps[:, 4, 0:NT * NE].rearrange("p (i e) -> p i e", e=NE))
                dve.drain()
                nc.vector.tensor_reduce(top[:, :], scores4[:, :, :], AX_X, ALU.max)
                for e in range(NE):
                    if e > 0:
                        tt(beats[:, :, e, 0:e], scores4[:, :, 0:e],
                           scores4[:, :, e:e + 1].to_broadcast([P, NT, e]), ALU.is_ge)
                    if e < NE - 1:
                        tt(beats[:, :, e, e + 1:NE], scores4[:, :, e + 1:NE],
                           scores4[:, :, e:e + 1].to_broadcast([P, NT, NE - 1 - e]), ALU.is_gt)
                dve.drain()
                tt(gate[:, :, :], scores4[:, :, :], top[:, :].unsqueeze(2).to_broadcast([P, NT, NE]),
                   ALU.subtract).then_inc(gate_shift.sem, 1)
                nc.vector.tensor_reduce(rank[:, :, :], beats[:, :, :, :], AX_X, ALU.add)
                dve.drain()
                ts(rank[:, :, :], rank[:, :, :], 1.5, None, ALU.is_lt)
                dve.drain()
                dve.wait_ge(gate_exp.sem, gate_exp.at(b, 1))
                tt(gate[:, :, :], gate[:, :, :], rank[:, :, :], ALU.mult)
                dve.drain()
                nc.vector.tensor_reduce(top[:, :], gate[:, :, :], AX_X, ALU.add)
                dve.drain()
                nc.vector.reciprocal(top[:, :], top[:, :])
                dve.drain()
                tt(gate[:, :, :], gate[:, :, :], top[:, :].unsqueeze(2).to_broadcast([P, NT, NE]), ALU.mult)
                dve.drain()
                with dve.Fori(0, NE) as e:
                    for layer in range(2):
                        made, normed = (hid_mm, hid_norm) if layer == 0 else (out_mm, out_norm)
                        for i in range(NT):
                            if i % 2 == 0:
                                dve.wait_ge(made.sem, made.at(b, i // 2 + 1) + e * (NT // 2))
                            nc.vector.bn_stats(stats[:, i, :], tile_bank(i))
                        dve.drain()
                        for i in range(NT):
                            last = nc.vector.bn_aggr(mv[:, i, :], stats[:, i, :])
                        last.then_inc(exp_stats.sem, 1)
                        dve.wait_ge(exp_rstd.sem, exp_rstd.at(b, 2 if layer == 0 else 5) + e * 5)
                        for i in range(NT):
                            ts(z[:, i, :], tile_bank(i), mv[:, i, 0:1], rstd[:, i:i + 1], ALU.subtract,
                               ALU.mult).then_inc(normed.sem, 1)
                    for i in range(NT):
                        nc.vector.scalar_tensor_tensor(h[:, i, :], be2[:, e, :], gate[:, i, bass.ds(e, 1)],
                                                       h[:, i, :], ALU.mult, ALU.add)
                    dve.drain()
                    for i in range(NT):
                        dve.wait_ge(out_scaled.sem, out_scaled.at(b, i + 1) + e * NT)
                        tt(h[:, i, :], h[:, i, :], z[:, i, :], ALU.add)
                    dve.drain()
                layer_norm(b, 2)
                dve.wait_ge(att_clear.sem, att_clear.at(b, 2))
                nc.vector.memset(v_ext[:, :, :, DH:DH + 1], 1.0)
                with dve.Fori(0, QUADS) as g:
                    for r in range(2):
                        dve.wait_ge(qkv_mm.sem, qkv_mm.at(b, r + 1) + g * 3)
                        tt(qk_prod[:, r, :], ps[:, 2 * r:2 * r + 2, :].rearrange("p r s -> p (r s)"),
                           head_rot[:, :], ALU.mult).then_inc(qk_rot.sem, 1)
                    dve.wait_ge(qkv_mm.sem, qkv_mm.at(b, 3) + g * 3)
                    nc.vector.tensor_copy(v_ext[:, :, :, 0:DH],
                                          ps[:, 4, :].rearrange("p (i j d) -> p i j d", i=NT, j=4))\
                        .then_inc(v_ready.sem, 1)
                    n = 0
                    for i, s0, cols, diag in MAX_GROUPS:
                        for pair in range(2):
                            dve.wait_ge(raw_mm.sem, raw_mm.at(b, n + 1) + g * UNITS)
                            slot = n % RING
                            nc.vector.tensor_reduce(part_max[:, i, s0 // HALF, 2 * pair:2 * pair + 2],
                                                    ps[:, 2 * slot:2 * slot + 2, 0:cols], AX_X,
                                                    ALU.max).then_inc(raw_max.sem, 1)
                            n += 1
                    dve.wait_ge(raw_max.sem, raw_max.at(b, UNITS) + g * UNITS)
                    full = NT // NH
                    ts(neg_max[:, 0:full, :, DH], part_max[:, 0:full, 0, :], -1.0, None, ALU.mult)
                    tt(head_max[:, full:NT, :], part_max[:, full:NT, 0, :], part_max[:, full:NT, 1, :], ALU.max)
                    dve.drain()
                    ts(neg_max[:, full:NT, :, DH], head_max[:, full:NT, :], -1.0, None,
                       ALU.mult).then_inc(max_ready.sem, 1)
                    dve.wait_ge(max_turned.sem, max_turned.at(b, 1) + g)
                    tt(q_T, q_T, ps[:, 0:2, :].rearrange("p r s -> p (r s)"), ALU.add).then_inc(q_shifted.sem, 1)
                    dve.wait_ge(den_mm.sem, den_mm.at(b, 1) + g)
                    nc.vector.reciprocal(y_rec, ps[:, 0:2, :].rearrange("p r s -> p (r s)"))\
                        .then_inc(y_rec_done.sem, 1)
                    dve.wait_ge(y_rec_done.sem, y_rec_done.at(b, 1) + g)
                    tt(y_T, y_sum, y_rec, ALU.mult).then_inc(y_norm.sem, 1)
                    dve.wait_ge(wo_mm.sem, wo_mm.at(b, 1) + g)
                    tt(all_h, all_h, ps[:, 2:6, :].rearrange("p r s -> p (r s)"), ALU.add)\
                        .then_inc(att_added.sem, 1)
                dve.wait_ge(att_added.sem, att_added.at(b, QUADS))
                layer_norm(b, 3)
                dve.drain()
                tt(all_h, all_h, route_b[:, :, :].rearrange("p i n -> p (i n)"), ALU.add)
                dve.drain()
                with dve.Fori(0, TILES // 2) as m:
                    for k in range(2):
                        dve.wait_ge(route_mm.sem, route_mm.at(b, k + 1) + m * 2)
                        for i in range(NT):
                            last = nc.vector.scalar_tensor_tensor(
                                h[:, i, :], ps[:, 4 * k + i // 2, (i % 2) * D:(i % 2 + 1) * D],
                                route[:, i, bass.ds(m * 2 + k, 1)], h[:, i, :], ALU.mult, ALU.add)
                        last.then_inc(routed.sem, 1)
                        dve.wait_ge(routed.sem, routed.at(b, k + 1) + m * 2)
                dve.drain().then_inc(h_final.sem, 1)


PREP_MM = K3 * DC + 5
PREP_ROUTE = 4 + 2 * TILES
PREP_DVE = PREP_ROUTE + 11


def constants():
    f32 = np.float32

    def bf16_bits(x):
        return (np.ascontiguousarray(x, f32).view(np.uint32) >> 16).astype(np.uint16)

    c = {}
    c["c_ident"] = np.eye(P, dtype=f32)
    c["c_ident_bf"] = bf16_bits(np.eye(P))
    later = np.triu(np.ones((P, P), bool), 1)
    c["c_mask_rows"] = bf16_bits(np.where(later, MASKED, 0.0))
    c["c_mask_cols"] = bf16_bits(np.where(later.T, MASKED, 0.0))
    c["c_vocab"] = (np.arange(P) % VOCAB).astype(f32)[:, None]
    inv = (1.0 / np.power(f32(10000.0), np.arange(0, D, 2, dtype=f32) / f32(D))).astype(f32)
    freqs = np.arange(S, dtype=f32)[:, None] * inv[None, :]
    emb = np.concatenate([freqs, freqs], axis=-1)
    sign = np.where(np.arange(D) % 2 == 0, -1.0, 1.0).astype(f32)
    both = np.concatenate([np.cos(emb), np.sin(emb) * sign], axis=1).astype(f32)
    c["c_trig"] = both.reshape(NT, P, 2 * D).transpose(1, 0, 2).copy()
    half = DH // 2
    theta = (1.0 / np.power(f32(10000.0), np.arange(half, dtype=f32) / f32(half))).astype(f32)
    ang = np.arange(S, dtype=f32)[:, None] * theta[None, :]
    cos, sin = np.cos(ang).astype(f32).T, np.sin(ang).astype(f32).T
    rows = np.concatenate([cos, cos, -sin, sin], axis=0)
    c["c_head_rot"] = np.tile(rows, (4, 1)).copy()
    pair, den, one16 = np.zeros((P, P), f32), np.zeros((P, P), f32), np.zeros((P, 1), f32)
    for j in range(4):
        for d in range(DH):
            pair[32 * j + d, 32 * j + d] = pair[32 * j + DH + d, 32 * j + d] = 1.0
        den[32 * j + DH, 32 * j:32 * j + 32] = 1.0
        one16[32 * j + DH] = 1.0
    c["c_pair_sum"], c["c_spread_den"], c["c_one_row16"] = pair, den, one16
    pick = np.zeros((3, 2 * NS, 2 * NS, P), f32)
    for n in range(2 * NS):
        pick[:, n, n, :] = 1.0
    c["c_pick_state"] = bf16_bits(pick.reshape(3 * 2 * NS, 2 * NS, P))
    pos = np.arange(S, dtype=f32)[:, None]
    div = np.exp(np.arange(0, PDIM, 2, dtype=f32) * f32(-np.log(10000.0) / PDIM)).astype(f32)
    ang = (pos * div).astype(f32)
    enc = np.zeros((S, PDIM), f32)
    enc[:, 0::2], enc[:, 1::2] = np.sin(ang), np.cos(ang)
    c["c_pe_T"] = enc.T.copy()
    return c


def layouts(i):
    def chunks(w):
        return w.reshape(-1, P, w.shape[1]).transpose(1, 0, 2)

    def column(v):
        return v.reshape(-1, P).T

    swap = np.arange(D) ^ 1
    both = np.concatenate([np.arange(D), swap])
    r = {"x": i["x"]}
    w = i["L0_tok_conv_w"].transpose(1, 2, 0)[:, :, both]
    r["tok_conv_w"] = w.reshape(DC, P, TAPS, 2 * D).transpose(1, 0, 2, 3)
    r["tok_conv_b"] = i["L0_tok_conv_b"][both]
    r["emb_T"] = chunks(i["L0_tok_embed_table"].T)
    r["emb_rows"] = i["L0_tok_embed_table"][:, both]
    r["tok_norm_w"] = i["L0_tok_norm_w"]
    r["mix_conv_w"] = i["L0_attn_conv_w"].transpose(0, 2, 1).reshape(EC, P, K3, D).transpose(1, 0, 2, 3)
    r["mix_conv_b"] = column(i["L0_attn_conv_b"])
    r["in_w"] = chunks(i["L0_attn_in_w"].T)
    r["in_b"] = column(i["L0_attn_in_b"])
    r["dt_w"] = chunks(i["L0_attn_dt_w"].T)
    r["dt_b"] = column(i["L0_attn_dt_b"])
    r["bc_w"] = chunks(np.concatenate([i["L0_attn_Bp_w"], i["L0_attn_Cp_w"]]).T)
    r["bc_b"] = np.concatenate([i["L0_attn_Bp_b"], i["L0_attn_Cp_b"]])[:, None]
    r["a_log"] = i["L0_attn_A_log"].reshape(EC, P, NS).transpose(1, 2, 0)
    r["d_skip"] = column(i["L0_attn_Dskip"])
    r["out_w"] = chunks(i["L0_attn_out_w"].T)
    r["out_b"] = i["L0_attn_out_b"][None]
    r["gate_w"] = chunks(i["L0_ffn_gate_W"])
    r["gate_b"] = i["L0_ffn_gate_b"][None]
    r["b1"], r["b2"] = i["L0_ffn_b1"][None], i["L0_ffn_b2"][None]
    r["g1"] = i["L0_ffn_g1"].reshape(NE, DC, P).transpose(2, 0, 1)
    r["be1"] = i["L0_ffn_be1"].reshape(NE, DC, P).transpose(2, 0, 1)
    r["g2"], r["be2"] = i["L0_ffn_g2"], i["L0_ffn_be2"]
    w = np.stack([i["L0_ffn_W1"], i["L0_ffn_W2"]]).reshape(2, NE, DC, P, D)
    r["w_moe"] = w.transpose(3, 0, 1, 2, 4).reshape(P, -1)
    r["w_route"] = i["L1_ffn_W"].transpose(0, 2, 1).reshape(TILES, DC, P, D).transpose(2, 0, 1, 3).reshape(P, -1)
    r["route_b"] = i["L1_ffn_b"]
    r["sigs_T"] = i["L1_ffn_tile_sigs"].T
    qkv = i["L1_attn_W_qkv"]
    plain = np.arange(DH)
    cols = np.concatenate([np.concatenate([DH * j + plain, DH * j + (plain + DH // 2) % DH]) for j in range(4)])
    quads = []
    for g in range(QUADS):
        q0 = 4 * DH * g
        quads.append(chunks(np.concatenate([qkv[:, q0 + cols], qkv[:, D + q0 + cols],
                                            qkv[:, 2 * D + q0:2 * D + q0 + 4 * DH]], axis=1)))
    r["w_qkv"] = np.stack(quads)
    w = np.zeros((4, 32, QUADS, D), np.float32)
    w[:, 0:DH] = i["L1_attn_W_o"].reshape(QUADS, 4, DH, D).transpose(1, 2, 0, 3)
    r["w_o"] = w.reshape(P, QUADS, D)
    return {k: np.ascontiguousarray(v) for k, v in r.items()}


def kernel(**inputs):
    import concourse.bacc as bacc
    from concourse.bass_utils import run_bass_kernel_spmd

    arrays = layouts({k: np.asarray(v) for k, v in inputs.items()})
    arrays.update(constants())
    nc = bacc.Bacc("TRN2", target_bir_lowering=False, num_devices=1)
    aps = {k: nc.dram_tensor(f"in_{k}", v.shape, mybir.dt.from_np(v.dtype), kind="ExternalInput").ap()
           for k, v in arrays.items()}
    out = nc.dram_tensor("out_h", (B, S, D), F32, kind="ExternalOutput").ap()
    build(nc, aps, out)
    r = run_bass_kernel_spmd(nc, [{f"in_{k}": v for k, v in arrays.items()}], core_ids=[0])
    return r.results[0]["out_h"]
```

```python
from contextlib import ExitStack

import numpy as np

import concourse.bass as bass
from concourse import mybir

ALU = mybir.AluOpType
ACT = mybir.ActivationFunctionType
F32 = mybir.dt.float32
BF16 = mybir.dt.bfloat16
I32 = mybir.dt.int32
AX_X = mybir.AxisListType.X

P = 128
B = 8
S = 1024
D = 256
NT = S // P
DC = D // P
HALF = 512
NH = S // HALF
VOCAB = 64
TAPS = 4
E = 512
EC = E // P
NS = 16
K3 = 3
NE = 4
HEADS = 16
DH = 16
QUADS = HEADS // 4
TILES = 8
PDIM = 32
RMS_EPS = 1.1920929e-07
LN_EPS = 1e-05
MASKED = -1e30


class Signal:

    def __init__(self, sem, per_batch, start):
        self.sem, self.per_batch, self.start = sem, per_batch, start

    def at(self, b, n):
        return b * self.per_batch + (n + self.start)


class Chain:

    def __init__(self, eng, signal, base):
        self.eng, self.sem, self.base, self.n = eng, signal.sem, base, 0

    def step(self, ins):
        self.n += 1
        ins.then_inc(self.sem, 1)

    def settle(self):
        self.eng.wait_ge(self.sem, self.base + self.n)


MAX_GROUPS = [(i, c * HALF, min((i + 1) * P - c * HALF, HALF), (i * P) // HALF == c)
              for i in range(NT) for c in range(NH) if c * HALF < (i + 1) * P]
PROB_GROUPS = [(half, i, max(half * HALF, i * P), i * P >= half * HALF)
               for half in range(NH) for i in range(NT) if i * P < (half + 1) * HALF]
RAW = 4 * len(MAX_GROUPS)
UNITS = 2 * len(PROB_GROUPS)
SLOTS = 2
LAG = SLOTS
PROBS = 3
Q_PARTS = (0, 0, 1, 1, 0, 2)
K_PARTS = (0, 1, 0, 1, 2, 0)
STACK = DH * len(Q_PARTS)
SHIFT = 3


def turn_plan(g):
    plan = []
    for n in range(UNITS + LAG):
        side = []
        if g < QUADS - 1 and 3 <= n < 3 + RAW // 3:
            side += [("raw", g + 1, 3 * (n - 3) + k) for k in range(3)]
        if g > 0 and n == 1:
            side.append(("y", g - 1, 1))
        if n == 2 * (NT // NH) + LAG + 1:
            side.append(("y", g, 0))
        if g < QUADS - 1 and n == RAW // 3 + 5:
            side.append(("rows", g + 1, 0))
        plan.append(side)
    return plan


FIRST = [("raw", 0, k) for k in range(RAW)] + [("rows", 0, 0)]
PLANS = [turn_plan(g) for g in range(QUADS)]
LAST = [("y", QUADS - 1, 1)]
SIDE = {unit: k for k, unit in enumerate(FIRST + [u for plan in PLANS for side in plan for u in side] + LAST)}


def build(nc, a, out):
    with ExitStack() as ctx:
        def sb(name, shape, dt=F32):
            return ctx.enter_context(nc.sbuf_tensor(name, shape, dt))

        def signal(name, per_batch=0, start=0):
            return Signal(ctx.enter_context(nc.semaphore(name)), per_batch, start)

        ident = sb("ident", [P, P])
        ident_bf = sb("ident_bf", [P, P], BF16)
        mask_rows = sb("mask_rows", [P, P], BF16)
        mask_cols = sb("mask_cols", [P, P], BF16)
        ones_row = sb("ones_row", [1, P])
        vocab_col = sb("vocab_col", [P, 1])
        table = sb("table", [P, 3, 2, 2 * D], BF16)
        minus_half = sb("minus_half", [P, NT])
        conv_in = sb("conv_in", [P, K3, DC, E])
        u_bias = sb("u_bias", [P, EC])
        in_b = sb("in_b", [P, EC])
        conv_b = sb("conv_b", [P, EC])
        dt_w = sb("dt_w", [P, EC, E])
        dt_b = sb("dt_b", [P, EC])
        bc_w = sb("bc_w", [P, EC, 2 * NS])
        bc_b = sb("bc_b", [2 * NS, 1])
        neg_a = sb("neg_a", [P, NS, EC])
        d_skip = sb("d_skip", [P, EC])
        out_w = sb("out_w", [P, EC, D])
        out_b = sb("out_b", [1, D])
        pick_state = sb("pick_state", [3 * 2 * NS, 2 * NS, P], BF16)
        gate_w = sb("gate_w", [P, DC, NE])
        gate_b = sb("gate_b", [1, NE])
        b1 = sb("b1", [1, NE, D])
        b2 = sb("b2", [1, NE, D])
        g1 = sb("g1", [P, NE, DC])
        be1 = sb("be1", [P, NE, DC])
        g2 = sb("g2", [P, NE, D])
        be2 = sb("be2", [P, NE, D])
        w_o = sb("w_o", [P, DC, D])
        route = sb("route", [P, NT, TILES])
        route_b = sb("route_b", [P, NT, D])
        w_stream = sb("w_stream", [P, 8 * DC * D])
        w_moe = w_stream[:, :].rearrange("p (l e c n) -> p l e c n", l=2, e=NE, c=DC)
        w_route = w_stream[:, :].rearrange("p (t c n) -> p t c n", t=TILES, c=DC)
        w_v = sb("w_v", [P, DC, D])

        h = sb("h", [P, NT, D])
        xn = sb("xn", [P, NT, D])
        xT = sb("xT", [P, DC, S + 2])
        stats = sb("stats", [P, NT, 6])
        mv = sb("mv", [P, NT, 2])
        rstd = sb("rstd", [P, NT])
        scores4 = sb("scores4", [P, NT, NE])
        top = sb("top", [P, NT])
        beats = sb("beats", [P, NT, NE, NE])
        rank = sb("rank", [P, NT, NE])
        gate = sb("gate", [P, NT, NE])
        neg_max = sb("neg_max", [P, NT, 4])
        max_parts = sb("max_parts", [P, NT, 4, SHIFT], BF16)
        den_rec = sb("den_rec", [P, NH, NT // NH, 4])
        part_max = sb("part_max", [P, NT, NH, 4])

        buf_u = sb("buf_u", [P, EC * S])
        buf_delta = sb("buf_delta", [P, EC * S])
        buf_du = sb("buf_du", [P, EC * S])
        buf_y = sb("buf_y", [P, EC * S])
        buf_decay = sb("buf_decay", [P, EC * S])
        buf_scan = sb("buf_scan", [P, 2 * S])
        conv_in_w = buf_decay[:, 0:EC * K3 * D].rearrange("p (e k n) -> p e k n", e=EC, k=K3)
        in_w = buf_u[:, 0:EC * E].rearrange("p (e n) -> p e n", e=EC)
        tok_w = buf_delta[:, :].rearrange("p (c j n) -> p c j n", c=DC, j=TAPS)
        emb_T = buf_u[:, 2048:2048 + DC * VOCAB].rearrange("p (c v) -> p c v", c=DC)
        emb_rows = buf_u[:, 2304:2304 + 2 * D]
        tok_b = buf_u[:, 2816:2816 + 2 * D]
        pe_T = buf_u[0:PDIM, 3328:3328 + 512].bitcast(F32)
        table_f = buf_y[:, 0:1024]
        table_r = buf_y[:, 1024:2048]
        sigs_T = buf_y[0:PDIM, 2048:2048 + TILES]
        a_log = buf_y[:, 2064:2064 + NS * EC].rearrange("p (n c) -> p n c", c=EC)
        sign_T = buf_y[0:PDIM, 2136:2136 + TILES]
        route_T = buf_y[0:TILES, 2176:2176 + S]
        b_tiles = buf_y[0:TILES, 3200:3200 + D]
        best = buf_y[:, 3456:3456 + NT]
        taken = buf_y[:, 3472:3472 + NT]
        is_best = buf_y[:, 3488:3488 + NT * TILES].rearrange("p (i t) -> p i t", t=TILES)
        pe_full = buf_du[0:PDIM, 0:S]
        ids = buf_scan[:, :].bitcast(I32).rearrange("p (c s) -> p c s", c=2)
        onehot = buf_y[:, 0:S].bitcast(BF16).rearrange("p (c s) -> p c s", c=2)
        trig = buf_delta[:, :].rearrange("p (i n) -> p i n", i=NT)
        rotated = buf_du[:, 0:1024].rearrange("p (r n) -> p r n", r=2)
        norm_w = buf_decay[:, 3 * S:3 * S + D]
        squares = buf_du[:, 1024:1024 + NT * D].rearrange("p (i n) -> p i n", i=NT)
        square_sum = sb("square_sum", [P, NT])
        u = buf_u[:, :].rearrange("p (c s) -> p c s", c=EC)
        delta = buf_delta[:, :].rearrange("p (c s) -> p c s", c=EC)
        du = buf_du[:, :].rearrange("p (c s) -> p c s", c=EC)
        y = buf_y[:, :].rearrange("p (c s) -> p c s", c=EC)
        decay = buf_decay[:, :].rearrange("p (c s) -> p c s", c=EC)
        scan = buf_scan[:, :].rearrange("p (c s) -> p c s", c=2)
        drive = buf_u[:, 0:2 * S].rearrange("p (c s) -> p c s", c=2)
        c_rows = buf_u[:, 2 * S:4 * S].rearrange("p (c s) -> p c s", c=2)
        bc_full = buf_decay[0:2 * NS, 0:S]
        bc_rest = buf_decay[0:2 * NS, S:2 * S]
        bc_part = buf_decay[0:2 * NS, 2 * S:3 * S].bitcast(BF16)
        bc_parts = w_v[0:3 * 2 * NS, :, :].rearrange("p c n -> p (c n)")[:, 0:S // 2].bitcast(BF16)
        z = buf_du[:, 0:NT * D].rearrange("p (i n) -> p i n", i=NT)
        hid_T = buf_du[:, NT * D:].rearrange("p (c s) -> p c s", c=DC)
        half_w = 2 * S
        stack = [[part.bitcast(BF16).rearrange("p (j s) -> p j s", j=4)
                  for part in (buf[:, 0:half_w], buf[:, half_w:])] for buf in (buf_u, buf_y)]
        w_qk = buf_y[:, 0:half_w].rearrange("p (c n m) -> p c n m", c=DC, n=8)
        head_rot = buf_scan[:, :].rearrange("p (r s) -> p r s", r=2)
        plain = buf_decay[:, 0:half_w].rearrange("p (r s) -> p r s", r=2)
        swapped = buf_decay[:, half_w:].rearrange("p (r s) -> p r s", r=2)
        parts = buf_delta[:, 0:2 * SHIFT * S // 2].bitcast(BF16).rearrange("p (r t s) -> p r t s", r=2, t=SHIFT)
        probs = buf_decay[:, 0:PROBS * S].rearrange("p (r j s) -> p r j s", r=PROBS, j=2)
        y_sum = buf_decay[:, PROBS * S:].rearrange("p (r s) -> p r s", r=NH)
        v_cols = HEADS * (DH + 1) + 16
        v_ext = buf_du[:, 0:NT * v_cols].rearrange("p (i n) -> p i n", i=NT)
        max_rows = buf_du[0:4 * SHIFT, NT * v_cols:NT * v_cols + S].bitcast(BF16).rearrange("p (r s) -> p r s", r=2)
        y_tok = xn
        qk_dram = nc.dram_tensor("qk_parts", (4, SHIFT, P, S), BF16, kind="Internal").ap()

        ps = ctx.enter_context(nc.psum_tensor("ps", [P, 8, HALF], F32))

        def tile_bank(i):
            return ps[:, i // 2, (i % 2) * D:(i % 2 + 1) * D]

        def span(i):
            return slice(1 + i * P, 1 + (i + 1) * P)

        weights_in = signal("weights_in")
        preset = signal("preset")
        prep_mm = signal("prep_mm")
        prep_act = signal("prep_act")
        prep_dve = signal("prep_dve")
        ids_clear = signal("ids_clear", 1)
        ids_in = signal("ids_in", 16 * TAPS)
        trig_in = signal("trig_in", 32)
        moe_w_in = signal("moe_w_in", 16)
        route_w_in = signal("route_w_in", 16)
        onehot_done = signal("onehot_done", 2)
        tok_mm = signal("tok_mm", NT)
        tok_rot = signal("tok_rot", NT)
        tok_sum = signal("tok_sum", NT)
        tok_sq = signal("tok_sq", NT)
        tok_scale = signal("tok_scale", 2)
        ln_stats = signal("ln_stats", 4)
        ln_rstd = signal("ln_rstd", 8)
        ln_norm = signal("ln_norm", 4 * NT)
        ln_turned = signal("ln_turned", 5 * NT // 2)
        xT_ready = signal("xT_ready", 5 * NT // 2)
        u_mm = signal("u_mm", EC * NH)
        u_ready = signal("u_ready", EC * NH)
        dt_mm = signal("dt_mm", EC * NH)
        dt_out = signal("dt_out", EC * NH)
        sp_exp = signal("sp_exp", EC)
        sp_ln = signal("sp_ln", EC)
        delta_ready = signal("delta_ready", EC)
        du_ready = signal("du_ready", EC)
        y_init = signal("y_init", EC)
        bc_mm = signal("bc_mm", 1)
        bc_split = signal("bc_split", 1)
        b_rows_mm = signal("b_rows_mm", NS)
        c_rows_mm = signal("c_rows_mm", NS)
        c_rows_out = signal("c_rows_out", NS, start=1)
        decay_ready = signal("decay_ready", NS * EC, start=1)
        drive_ready = signal("drive_ready", NS * EC, start=1)
        scan_ready = signal("scan_ready", NS * EC, start=1)
        read_out = signal("read_out", NS * EC, start=1)
        y_added = signal("y_added", NS * EC, start=1)
        mix_mm = signal("mix_mm", NT // 2)
        gate_mm = signal("gate_mm", 1)
        gate_shift = signal("gate_shift", 1)
        gate_exp = signal("gate_exp", 1)
        gate_ready = signal("gate_ready", 1)
        hid_mm = signal("hid_mm", NE * NT // 2)
        exp_stats = signal("exp_stats", 2 * NE)
        exp_rstd = signal("exp_rstd", 5 * NE)
        hid_norm = signal("hid_norm", NE * NT)
        hid_turned = signal("hid_turned", NE * NT // 2)
        hid_ready = signal("hid_ready", NE * NT // 2)
        out_mm = signal("out_mm", NE * NT // 2)
        out_norm = signal("out_norm", NE * NT, start=1)
        out_scaled = signal("out_scaled", NE * NT)
        att_in = signal("att_in", 16 * 3)
        att_set = signal("att_set", 3)
        qk_mm = signal("qk_mm", 4)
        v_mm = signal("v_mm", 1)
        qk_turned = signal("qk_turned", 8, start=1)
        qk_sum = signal("qk_sum", 4)
        part_high = signal("part_high", 4)
        part_rest = signal("part_rest", 4)
        part_mid = signal("part_mid", 4)
        part_low = signal("part_low", 4)
        parts_out = [signal(f"parts_out{n}", 16, start=1) for n in range(4)]
        v_ready = signal("v_ready", 1)
        placed = [signal(f"placed{g}", 16 * 12, start=1) for g in range(QUADS)]
        side_mm = signal("side_mm", len(SIDE))
        side_read = signal("side_read", len(SIDE))
        max_ready = signal("max_ready", QUADS)
        rows_placed = [signal(f"rows_placed{g}", 16 * 4) for g in range(QUADS)]
        score_mm = signal("score_mm", UNITS * QUADS)
        prob_ready = signal("prob_ready", UNITS * QUADS)
        pv_done = signal("pv_done", UNITS * QUADS)
        y_copied = signal("y_copied", NH * QUADS)
        den_ready = signal("den_ready", NH * QUADS)
        y_ready = signal("y_ready", NH * QUADS)
        wo_mm = signal("wo_mm", NT // 2)
        route_mm = signal("route_mm", TILES, start=1)
        routed = signal("routed", TILES, start=1)
        h_final = signal("h_final", 1)
        stored = signal("stored", 16, start=1)

        loads = [
            (ident, a["c_ident"]), (vocab_col, a["c_vocab"]),
            (in_b, a["in_b"]), (conv_b, a["mix_conv_b"]), (dt_w, a["dt_w"]), (dt_b, a["dt_b"]), (bc_w, a["bc_w"]),
            (bc_b, a["bc_b"]), (d_skip, a["d_skip"]), (out_w, a["out_w"]), (out_b, a["out_b"]),
            (gate_w, a["gate_w"]), (gate_b, a["gate_b"]), (b1, a["b1"]), (b2, a["b2"]), (g1, a["g1"]),
            (be1, a["be1"]), (g2, a["g2"].partition_broadcast(P)), (be2, a["be2"].partition_broadcast(P)),
            (w_o, a["w_o"]), (pick_state, a["c_pick_state"].bitcast(BF16)),
            (ident_bf, a["c_ident_bf"].bitcast(BF16)), (mask_rows, a["c_mask_rows"].bitcast(BF16)), (mask_cols, a["c_mask_cols"].bitcast(BF16)),
            (conv_in_w, a["mix_conv_w"]), (in_w, a["in_w"]), (tok_w, a["tok_conv_w"]), (emb_T, a["emb_T"]),
            (emb_rows[VOCAB:P, :], a["emb_rows"]), (tok_b[VOCAB:P, :], a["tok_conv_b"].partition_broadcast(VOCAB)),
            (pe_full, a["c_pe_T"]), (sigs_T, a["sigs_T"]), (a_log, a["a_log"]), (b_tiles, a["route_b"]),
        ]
        ALL_IN = 16 * len(loads)

        def alone(eng):
            eng.sem_inc(passed.sem, 1)

        passed = signal("passed")

        block = ctx.enter_context(nc.Block())

        @block.sync
        def _(sp):
            for dst, src in loads:
                sp.dma_start(dst if isinstance(dst, bass.AP) else dst.ap(), src).then_inc(weights_in.sem, 16)
            sp.wait_ge(prep_mm.sem, PREP_MM)
            sp.wait_ge(prep_dve.sem, PREP_DVE)

            def place_rows(b, g):
                sp.wait_ge(side_read.sem, side_read.at(b, SIDE["rows", g, 0] + 1))
                for j in range(4):
                    sp.dma_start(stack[g % 2][0][STACK:STACK + SHIFT, j, :],
                                 max_rows[SHIFT * j:SHIFT * (j + 1), g % 2, :]).then_inc(rows_placed[g].sem, 16)

            with sp.Fori(0, B) as b:
                sp.wait_ge(decay_ready.sem, decay_ready.at(b, 0))
                sp.wait_ge(scan_ready.sem, scan_ready.at(b, 0))
                for n in range(4):
                    sp.wait_ge(parts_out[n].sem, parts_out[n].at(b, 0))
                sp.dma_start(trig, a["c_trig"]).then_inc(trig_in.sem, 16)
                sp.dma_start(norm_w, a["tok_norm_w"].partition_broadcast(P)).then_inc(trig_in.sem, 16)
                sp.wait_ge(ids_clear.sem, ids_clear.at(b, 1))
                for j in range(TAPS):
                    late = TAPS - 1 - j
                    half = slice((j % 2) * VOCAB, (j % 2 + 1) * VOCAB)
                    sp.dma_start(ids[half, j // 2, late:S],
                                 a["x"][b, 0:S - late].partition_broadcast(VOCAB)).then_inc(ids_in.sem, 16)
                sp.wait_ge(route_mm.sem, route_mm.at(b, 0))
                sp.dma_start(w_stream[:, :], a["w_moe"]).then_inc(moe_w_in.sem, 16)
                sp.wait_ge(out_mm.sem, out_mm.at(b, NE * NT // 2))
                sp.dma_start(w_stream[:, :], a["w_route"]).then_inc(route_w_in.sem, 16)
                sp.wait_ge(mix_mm.sem, mix_mm.at(b, NT // 2))
                sp.dma_start(w_qk, a["w_qk"]).then_inc(att_in.sem, 16)
                sp.dma_start(w_v[:, :, :], a["w_v"]).then_inc(att_in.sem, 16)
                sp.dma_start(head_rot, a["c_head_rot"]).then_inc(att_in.sem, 16)
                for n in range(4):
                    sp.wait_ge(part_low.sem, part_low.at(b, n + 1))
                    sp.wait_ge(part_mid.sem, part_mid.at(b, n + 1))
                    for g in range(2 * (n // 2), 2 * (n // 2) + 2):
                        sp.wait_ge(placed[g].sem, placed[g].at(b, 0))
                    sp.dma_start(qk_dram[n].rearrange("t p s -> p t s"), parts[:, n % 2, :, :])\
                      .then_inc(parts_out[n].sem, 16)
                for g in range(QUADS):
                    c = g // 2
                    for n in range(2 * c, 2 * c + 2):
                        sp.wait_ge(parts_out[n].sem, parts_out[n].at(b, 16))
                    alone(sp)
                    if g >= 2:
                        sp.wait_ge(score_mm.sem, score_mm.at(b, (g - 1) * UNITS))
                    for r, which in enumerate((Q_PARTS, K_PARTS)):
                        for m, t in enumerate(which):
                            src = qk_dram[2 * c + r, t].rearrange("(q j d) s -> q d j s", q=2, j=4)[g % 2]
                            sp.dma_start(stack[g % 2][r][DH * m:DH * (m + 1), :, :], src).then_inc(placed[g].sem, 16)
                    place_rows(b, g)
                sp.wait_ge(h_final.sem, h_final.at(b, 1))
                sp.dma_start(out[b].rearrange("(i p) n -> p i n", p=P), h[:, :, :]).then_inc(stored.sem, 16)
            sp.wait_ge(stored.sem, stored.at(B, 0))

        @block.gpsimd
        def _(pool):
            for s in (decay_ready, scan_ready, route_mm, read_out, y_added, drive_ready, c_rows_out, out_norm,
                      routed, stored, qk_turned, *parts_out, *placed):
                pool.sem_inc(s.sem, s.start)
            pool.memset(xT[:, :, 0:1], 0.0).then_inc(preset.sem, 1)
            pool.memset(xT[:, :, S + 1:S + 2], 0.0).then_inc(preset.sem, 1)
            pool.memset(ones_row[:, :], 1.0).then_inc(preset.sem, 1)
            pool.memset(minus_half[:, :], -0.5).then_inc(preset.sem, 1)
            pool.memset(beats[:, :, :, :], 0.0).then_inc(preset.sem, 1)

            def root(src, scale, eps, done, first):
                nc.gpsimd.tensor_scalar(rstd[:, :], src, scale, eps, ALU.mult, ALU.add).then_inc(done.sem, 1)
                pool.wait_ge(done.sem, first)
                nc.gpsimd.tensor_tensor(rstd[:, :], rstd[:, :], minus_half[:, :], ALU.pow).then_inc(done.sem, 1)

            def layer_norm(b, k):
                pool.wait_ge(ln_stats.sem, ln_stats.at(b, k + 1))
                alone(pool)
                root(mv[:, :, 1], 1.0, LN_EPS, ln_rstd, ln_rstd.at(b, 2 * k + 1))

            pool.wait_ge(prep_dve.sem, PREP_DVE)
            with pool.Fori(0, B) as b:
                pool.wait_ge(read_out.sem, read_out.at(b, 0))
                pool.wait_ge(qk_turned.sem, qk_turned.at(b, 0))
                alone(pool)
                pool.memset(ids[:, :, 0:TAPS - 1], -1).then_inc(ids_clear.sem, 1)
                pool.wait_ge(tok_sq.sem, tok_sq.at(b, NT))
                alone(pool)
                root(square_sum[:, :], 1.0 / D, RMS_EPS, tok_scale, tok_scale.at(b, 1))
                layer_norm(b, 0)
                for c in range(EC):
                    pool.wait_ge(u_ready.sem, u_ready.at(b, NH * (c + 1)))
                    alone(pool)
                    nc.gpsimd.tensor_scalar(y[:, c, :], u[:, c, :], d_skip[:, c:c + 1], None,
                                            ALU.mult).then_inc(y_init.sem, 1)
                for c in range(EC):
                    pool.wait_ge(delta_ready.sem, delta_ready.at(b, c + 1))
                    nc.gpsimd.tensor_tensor(du[:, c, :], delta[:, c, :], u[:, c, :],
                                            ALU.mult).then_inc(du_ready.sem, 1)
                pool.wait_ge(y_init.sem, y_init.at(b, EC))
                alone(pool)
                with pool.Fori(0, NS) as n:
                    for c in range(EC):
                        pool.wait_ge(read_out.sem, read_out.at(b, 1 + c) + n * EC)
                        pool.wait_ge(y_added.sem, y_added.at(b, 0) + n * EC)
                        nc.gpsimd.tensor_tensor(y[:, c, :], y[:, c, :], scan[:, c % 2, :],
                                                ALU.add).then_inc(y_added.sem, 1)
                layer_norm(b, 1)
                with pool.Fori(0, NE) as e:
                    base = exp_rstd.at(b, 0) + e * 5
                    pool.wait_ge(exp_stats.sem, exp_stats.at(b, 1) + e * 2)
                    alone(pool)
                    root(mv[:, :, 1], 1.0, LN_EPS, exp_rstd, base + 1)
                    pool.wait_ge(exp_stats.sem, exp_stats.at(b, 2) + e * 2)
                    alone(pool)
                    root(mv[:, :, 1], 1.0, LN_EPS, exp_rstd, base + 3)
                    pool.wait_ge(exp_rstd.sem, base + 4)
                    alone(pool)
                    nc.gpsimd.tensor_tensor(rstd[:, :], rstd[:, :], gate[:, :, e],
                                            ALU.mult).then_inc(exp_rstd.sem, 1)
                    for i in range(NT):
                        pool.wait_ge(out_norm.sem, out_norm.at(b, i + 1) + e * NT)
                        alone(pool)
                        nc.gpsimd.tensor_tensor(z[:, i, :], z[:, i, :], g2[:, e, :],
                                                ALU.mult).then_inc(out_scaled.sem, 1)
                layer_norm(b, 2)
                pool.memset(v_ext[:, :, :], 1.0).then_inc(att_set.sem, 1)
                for r in range(2):
                    pool.wait_ge(att_set.sem, att_set.at(b, r + 1))
                    alone(pool)
                    pool.memset(stack[r][1][STACK:STACK + SHIFT, :, :], 1.0).then_inc(att_set.sem, 1)
                pool.wait_ge(att_set.sem, att_set.at(b, 3))
                for n in range(4):
                    pool.wait_ge(part_mid.sem, part_mid.at(b, n + 1))
                    if n >= 2:
                        pool.wait_ge(parts_out[n - 2].sem, parts_out[n - 2].at(b, 16))
                    nc.gpsimd.tensor_tensor(parts[:, n % 2, 2, :], plain[:, n % 2, :], parts[:, n % 2, 1, :],
                                            ALU.subtract).then_inc(part_low.sem, 1)
                layer_norm(b, 3)

        @block.scalar
        def _(act):
            act.wait_ge(weights_in.sem, ALL_IN)
            nc.scalar.activation(neg_a[:, :, :], a_log, ACT.Exp).then_inc(prep_act.sem, 1)
            nc.scalar.activation(sign_T, sigs_T, ACT.Sign).then_inc(prep_act.sem, 1)
            for n in range(K3 * DC):
                act.wait_ge(prep_mm.sem, n + 1)
                nc.scalar.activation(conv_in[:, n // DC, n % DC, :], ps[:, n % 4, :],
                                     ACT.Copy).then_inc(prep_act.sem, 1)

            def copy_turned(b, k):
                for p in range(NT // 2):
                    act.wait_ge(ln_turned.sem, ln_turned.at(b, k * 4 + p + 1))
                    nc.scalar.activation(xT[:, :, 1 + 2 * P * p:1 + 2 * P * (p + 1)],
                                         ps[:, 6 + p % 2, :].rearrange("p (c s) -> p c s", c=DC),
                                         ACT.Copy).then_inc(xT_ready.sem, 1)

            act.wait_ge(prep_dve.sem, PREP_DVE)
            with act.Fori(0, B) as b:
                for i in range(NT):
                    act.wait_ge(tok_sum.sem, tok_sum.at(b, i + 1))
                    nc.scalar.activation(squares[:, i, :], h[:, i, :], ACT.Square,
                                         accum_out=square_sum[:, i:i + 1]).then_inc(tok_sq.sem, 1)
                copy_turned(b, 0)
                for n in range(EC * NH):
                    c, half = n // NH, n % NH
                    act.wait_ge(u_mm.sem, u_mm.at(b, n + 1))
                    nc.scalar.activation(u[:, c, half * HALF:(half + 1) * HALF], ps[:, n % 4, :], ACT.Silu,
                                         bias=u_bias[:, c:c + 1]).then_inc(u_ready.sem, 1)
                for n in range(EC * NH):
                    c, half = n // NH, n % NH
                    act.wait_ge(dt_mm.sem, dt_mm.at(b, n + 1))
                    cols = slice(half * HALF, (half + 1) * HALF)
                    nc.scalar.activation(delta[:, c, cols], ps[:, n % 4, :], ACT.Abs, bias=dt_b[:, c:c + 1])
                    nc.scalar.activation(du[:, c, cols], ps[:, n % 4, :], ACT.Relu,
                                         bias=dt_b[:, c:c + 1]).then_inc(dt_out.sem, 1)
                for c in range(EC):
                    act.wait_ge(dt_out.sem, dt_out.at(b, NH * (c + 1)))
                    nc.scalar.activation(delta[:, c, :], delta[:, c, :], ACT.Exp,
                                         scale=-1.0).then_inc(sp_exp.sem, 1)
                for c in range(EC):
                    act.wait_ge(sp_exp.sem, sp_exp.at(b, c + 1))
                    nc.scalar.activation(delta[:, c, :], delta[:, c, :], ACT.Ln,
                                         bias=1.0).then_inc(sp_ln.sem, 1)
                act.wait_ge(bc_split.sem, bc_split.at(b, 1))
                act.wait_ge(delta_ready.sem, delta_ready.at(b, EC))
                act.wait_ge(du_ready.sem, du_ready.at(b, EC))
                alone(act)
                with act.Fori(0, NS // 2) as m:
                    for k in range(2):
                        states = m * 2 + k
                        act.wait_ge(c_rows_mm.sem, c_rows_mm.at(b, 1) + states)
                        act.wait_ge(read_out.sem, read_out.at(b, 0) + m * (2 * EC))
                        nc.scalar.activation(c_rows[:, k, :],
                                             ps[:, 4 + 2 * k:6 + 2 * k, :].rearrange("p r s -> p (r s)"),
                                             ACT.Copy).then_inc(c_rows_out.sem, 1)
                        for c in range(EC):
                            act.wait_ge(scan_ready.sem, scan_ready.at(b, 0) + states * EC)
                            alone(act)
                            nc.scalar.activation(decay[:, c, :], delta[:, c, :], ACT.Exp,
                                                 scale=neg_a[:, states, c:c + 1]).then_inc(decay_ready.sem, 1)
                copy_turned(b, 1)
                act.wait_ge(gate_shift.sem, gate_shift.at(b, 1))
                nc.scalar.activation(gate[:, :, :], gate[:, :, :], ACT.Exp).then_inc(gate_exp.sem, 1)
                with act.Fori(0, NE) as e:
                    for p in range(NT // 2):
                        act.wait_ge(hid_turned.sem, hid_turned.at(b, p + 1) + e * (NT // 2))
                        alone(act)
                        for c in range(DC):
                            last = nc.scalar.activation(hid_T[:, c, 2 * P * p:2 * P * (p + 1)],
                                                        ps[:, 6 + p % 2, c * 2 * P:(c + 1) * 2 * P], ACT.Relu,
                                                        bias=be1[:, e, c:c + 1], scale=g1[:, e, c:c + 1])
                        last.then_inc(hid_ready.sem, 1)
                copy_turned(b, 2)
                for n in range(4):
                    act.wait_ge(qk_sum.sem, qk_sum.at(b, n + 1))
                    if n >= 2:
                        act.wait_ge(parts_out[n - 2].sem, parts_out[n - 2].at(b, 16))
                    nc.scalar.activation(parts[:, n % 2, 0, :], plain[:, n % 2, :], ACT.Copy)\
                        .then_inc(part_high.sem, 1)
                    act.wait_ge(part_rest.sem, part_rest.at(b, n + 1))
                    nc.scalar.activation(parts[:, n % 2, 1, :], plain[:, n % 2, :], ACT.Copy)\
                        .then_inc(part_mid.sem, 1)
                act.wait_ge(part_low.sem, part_low.at(b, 4))
                for g in range(QUADS):
                    n = g * UNITS
                    for half, i, t0, diag in PROB_GROUPS:
                        cols = (half + 1) * HALF - t0
                        for pair in range(2):
                            act.wait_ge(score_mm.sem, score_mm.at(b, n + 1))
                            if n >= PROBS:
                                act.wait_ge(pv_done.sem, pv_done.at(b, n + 1 - PROBS))
                            bank = 2 + 2 * (n % SLOTS)
                            nc.scalar.activation(probs[:, n % PROBS, :, 0:cols], ps[:, bank:bank + 2, 0:cols],
                                                 ACT.Exp, scale=float(DH) ** -0.5).then_inc(prob_ready.sem, 1)
                            n += 1
                        if n % UNITS == 2 * (NT // NH) + 2 or n % UNITS == 0:
                            done = int(n % UNITS == 0)
                            units = n - 2 if n % UNITS else n
                            act.wait_ge(pv_done.sem, pv_done.at(b, units))
                            if g > 0:
                                act.wait_ge(side_mm.sem, side_mm.at(b, SIDE["y", g - 1, done] + 1))
                            nc.scalar.activation(y_sum[:, done, :], ps[:, 6 + done, :],
                                                 ACT.Copy).then_inc(y_copied.sem, 1)
                copy_turned(b, 3)
                copy_turned(b, 4)

        @block.tensor
        def _(pe):
            mm = nc.tensor.matmul
            pe.wait_ge(weights_in.sem, ALL_IN)
            pe.wait_ge(preset.sem, 5)
            for n in range(K3 * DC):
                k, c = n // DC, n % DC
                if n >= 4:
                    pe.wait_ge(prep_act.sem, 2 + n - 3)
                for e in range(EC):
                    last = mm(ps[:, n % 4, :], conv_in_w[:, e, k, c * P:(c + 1) * P], in_w[:, e, :],
                              start=(e == 0), stop=(e == EC - 1))
                last.then_inc(prep_mm.sem, 1)
            for f in range(EC):
                for e in range(EC):
                    last = mm(ps[:, 6, f:f + 1], in_w[:, e, f * P:(f + 1) * P], conv_b[:, e:e + 1],
                              start=(e == 0), stop=(e == EC - 1))
            last.then_inc(prep_mm.sem, 1)
            for j in range(TAPS):
                for c in range(DC):
                    last = mm(ps[(j % 2) * VOCAB:(j % 2 + 1) * VOCAB, 4 + j // 2, :], emb_T[:, c, :],
                              tok_w[:, c, j, :], start=(c == 0), stop=(c == DC - 1))
            last.then_inc(prep_mm.sem, 1)
            pe.wait_ge(prep_act.sem, 2)
            for i in range(NT):
                last = mm(ps[:, 7, i * TILES:(i + 1) * TILES], pe_full[:, i * P:(i + 1) * P], sign_T,
                          start=True, stop=True)
            last.then_inc(prep_mm.sem, 1)
            pe.wait_ge(prep_dve.sem, PREP_ROUTE)
            pe.wait_ge(prep_act.sem, 2 + K3 * DC)
            for i in range(NT):
                last = nc.tensor.transpose(ps[0:TILES, i // 4, (i % 4) * P:(i % 4 + 1) * P], route[:, i, :],
                                           ident[:, :])
            last.then_inc(prep_mm.sem, 1)
            pe.wait_ge(prep_dve.sem, PREP_ROUTE + 1)
            for i in range(NT):
                last = mm(tile_bank(i), route_T[:, i * P:(i + 1) * P], b_tiles, start=True, stop=True)
            last.then_inc(prep_mm.sem, 1)
            pe.wait_ge(prep_dve.sem, PREP_DVE)

            def turn(b, k, norm):
                for p in range(NT // 2):
                    if norm is not None:
                        pe.wait_ge(ln_norm.sem, ln_norm.at(b, norm * NT + 2 * p + 2))
                    if p >= 2:
                        pe.wait_ge(xT_ready.sem, xT_ready.at(b, k * 4 + p - 1))
                    for c in range(DC):
                        for r in range(2):
                            last = nc.tensor.transpose(ps[:, 6 + p % 2, (2 * c + r) * P:(2 * c + r + 1) * P],
                                                       xn[:, 2 * p + r, c * P:(c + 1) * P], ident[:, :])
                    last.then_inc(ln_turned.sem, 1)

            with pe.Fori(0, B) as b:
                pe.wait_ge(onehot_done.sem, onehot_done.at(b, 2))
                for i in range(NT):
                    if i >= 2:
                        pe.wait_ge(tok_rot.sem, tok_rot.at(b, i - 1))
                    n = 0
                    for c in range(2):
                        for part in range(3):
                            last = mm(ps[:, i % 2, :], onehot[:, c, i * P:(i + 1) * P], table[:, part, c, :],
                                      start=(n == 0), stop=(n == 5))
                            n += 1
                    last.then_inc(tok_mm.sem, 1)
                turn(b, 0, 0)
                pe.wait_ge(xT_ready.sem, xT_ready.at(b, 4))
                for n in range(EC * NH):
                    f, half = n // NH, n % NH
                    if n >= 4:
                        pe.wait_ge(u_ready.sem, u_ready.at(b, n - 3))
                    for m in range(K3 * DC):
                        k, c = m // DC, m % DC
                        last = mm(ps[:, n % 4, :], conv_in[:, k, c, f * P:(f + 1) * P],
                                  xT[:, c, half * HALF + k:half * HALF + k + HALF],
                                  start=(m == 0), stop=(m == K3 * DC - 1))
                    last.then_inc(u_mm.sem, 1)
                pe.wait_ge(u_ready.sem, u_ready.at(b, EC * NH))
                for n in range(EC * NH):
                    f, half = n // NH, n % NH
                    if n >= 4:
                        pe.wait_ge(dt_out.sem, dt_out.at(b, n - 3))
                    for e in range(EC):
                        last = mm(ps[:, n % 4, :], dt_w[:, e, f * P:(f + 1) * P],
                                  u[:, e, half * HALF:(half + 1) * HALF], start=(e == 0), stop=(e == EC - 1))
                    last.then_inc(dt_mm.sem, 1)
                for half in range(NH):
                    for e in range(EC):
                        last = mm(ps[0:2 * NS, 4 + half, :], bc_w[:, e, :],
                                  u[:, e, half * HALF:(half + 1) * HALF], start=(e == 0), stop=(e == EC - 1))
                last.then_inc(bc_mm.sem, 1)
                pe.wait_ge(bc_split.sem, bc_split.at(b, 1))
                pe.wait_ge(dt_out.sem, dt_out.at(b, EC * NH))
                alone(pe)
                with pe.Fori(0, NS // 2) as m:
                    for k in range(2):
                        states = m * 2 + k
                        pe.wait_ge(drive_ready.sem, drive_ready.at(b, 0) + m * (2 * EC))
                        for half in range(NH):
                            last = mm(ps[:, 2 * k + half, :], pick_state[:, states, :],
                                      bc_parts[:, half * HALF:(half + 1) * HALF], start=True, stop=True)
                        last.then_inc(b_rows_mm.sem, 1)
                        pe.wait_ge(c_rows_out.sem, c_rows_out.at(b, 0) + m * 2)
                        for half in range(NH):
                            last = mm(ps[:, 4 + 2 * k + half, :], pick_state[:, states + NS, :],
                                      bc_parts[:, half * HALF:(half + 1) * HALF], start=True, stop=True)
                        last.then_inc(c_rows_mm.sem, 1)
                pe.wait_ge(y_added.sem, y_added.at(b, NS * EC))
                for i in range(NT):
                    for e in range(EC):
                        mm(tile_bank(i), y[:, e, i * P:(i + 1) * P], out_w[:, e, :], start=(e == 0), stop=False)
                    last = mm(tile_bank(i), ones_row[:, :], out_b[:, :], start=False, stop=True)
                    if i % 2:
                        last.then_inc(mix_mm.sem, 1)
                turn(b, 1, 1)
                pe.wait_ge(xT_ready.sem, xT_ready.at(b, 8))
                for i in range(NT):
                    for c in range(DC):
                        mm(ps[:, 4, i * NE:(i + 1) * NE], xT[:, c, span(i)], gate_w[:, c, :],
                           start=(c == 0), stop=False)
                    last = mm(ps[:, 4, i * NE:(i + 1) * NE], ones_row[:, :], gate_b[:, :], start=False, stop=True)
                last.then_inc(gate_mm.sem, 1)
                pe.wait_ge(moe_w_in.sem, moe_w_in.at(b, 16))
                alone(pe)
                with pe.Fori(0, NE) as e:
                    for i in range(NT):
                        pe.wait_ge(out_norm.sem, out_norm.at(b, 0) + e * NT)
                        alone(pe)
                        for c in range(DC):
                            mm(tile_bank(i), xT[:, c, span(i)], w_moe[:, 0, e, c, :], start=(c == 0), stop=False)
                        last = mm(tile_bank(i), ones_row[:, :], b1[:, e, :], start=False, stop=True)
                        if i % 2:
                            last.then_inc(hid_mm.sem, 1)
                    for p in range(NT // 2):
                        pe.wait_ge(hid_norm.sem, hid_norm.at(b, 2 * p + 2) + e * NT)
                        if p >= 2:
                            pe.wait_ge(hid_ready.sem, hid_ready.at(b, p - 1) + e * (NT // 2))
                        for c in range(DC):
                            for r in range(2):
                                last = nc.tensor.transpose(ps[:, 6 + p % 2, (2 * c + r) * P:(2 * c + r + 1) * P],
                                                           z[:, 2 * p + r, c * P:(c + 1) * P], ident[:, :])
                        last.then_inc(hid_turned.sem, 1)
                    for i in range(NT):
                        pe.wait_ge(hid_ready.sem, hid_ready.at(b, i // 2 + 1) + e * (NT // 2))
                        for c in range(DC):
                            mm(tile_bank(i), hid_T[:, c, i * P:(i + 1) * P], w_moe[:, 1, e, c, :],
                               start=(c == 0), stop=False)
                        last = mm(tile_bank(i), ones_row[:, :], b2[:, e, :], start=False, stop=True)
                        if i % 2:
                            last.then_inc(out_mm.sem, 1)
                turn(b, 2, 2)
                pe.wait_ge(xT_ready.sem, xT_ready.at(b, 12))
                alone(pe)
                pe.wait_ge(att_in.sem, att_in.at(b, 48))
                for n in range(4):
                    if n >= 2:
                        pe.wait_ge(qk_turned.sem, qk_turned.at(b, 2 * n - 2))
                    for m in range(4):
                        swap, half = m // 2, m % 2
                        for c in range(DC):
                            last = mm(ps[:, 4 * (n % 2) + m, :], w_qk[:, c, 2 * n + swap, :],
                                      xT[:, c, 1 + half * HALF:1 + (half + 1) * HALF],
                                      start=(c == 0), stop=(c == DC - 1))
                    last.then_inc(qk_mm.sem, 1)
                pe.wait_ge(qk_turned.sem, qk_turned.at(b, 6))
                for i in range(NT):
                    for c in range(DC):
                        last = mm(tile_bank(i), xT[:, c, span(i)], w_v[:, c, :], start=(c == 0),
                                  stop=(c == DC - 1))
                last.then_inc(v_mm.sem, 1)
                pe.wait_ge(v_ready.sem, v_ready.at(b, 1))
                pe.wait_ge(qk_turned.sem, qk_turned.at(b, 8))

                def side_unit(kind, g, k):
                    at = SIDE[kind, g, k]
                    if at >= 2:
                        pe.wait_ge(side_read.sem, side_read.at(b, at - 1))
                    bank = at % 2
                    if kind == "raw":
                        i, s0, cols, diag = MAX_GROUPS[k // 4]
                        q, key = stack[g % 2]
                        if k == 0:
                            pe.wait_ge(placed[g].sem, placed[g].at(b, 16 * 12))
                        last = mm(ps[:, bank, 0:cols], q[0:STACK, k % 4, i * P:(i + 1) * P],
                                  key[0:STACK, k % 4, s0:s0 + cols], start=True, stop=not diag)
                        if diag:
                            last = mm(ps[:, bank, cols - P:cols], ident_bf[:, :], mask_rows[:, :],
                                      start=False, stop=True)
                    elif kind == "rows":
                        pe.wait_ge(max_ready.sem, max_ready.at(b, g + 1))
                        row_bank = ps[0:4 * SHIFT, bank, :].bitcast(BF16)
                        for i in range(NT):
                            last = nc.tensor.transpose(row_bank[:, i * P:(i + 1) * P],
                                                       max_parts[:, i, :, :].rearrange("p j t -> p (j t)"),
                                                       ident_bf[:, :])
                    else:
                        pe.wait_ge(y_copied.sem, y_copied.at(b, NH * g + k + 1))
                        for i in range(NT // NH):
                            last = nc.tensor.transpose(ps[:, bank, i * P:(i + 1) * P],
                                                       y_sum[:, k, i * P:(i + 1) * P], ident[:, :])
                    last.then_inc(side_mm.sem, 1)

                for unit in FIRST:
                    side_unit(*unit)
                for g in range(QUADS):
                    q, key = stack[g % 2]
                    units = [(half, i, t0, diag, pair) for half, i, t0, diag in PROB_GROUPS for pair in range(2)]
                    for n in range(UNITS + LAG):
                        if n < UNITS:
                            half, i, t0, diag, pair = units[n]
                            cols = (half + 1) * HALF - t0
                            if n == 0:
                                pe.wait_ge(rows_placed[g].sem, rows_placed[g].at(b, 16 * 4))
                            if g * UNITS + n >= SLOTS:
                                pe.wait_ge(prob_ready.sem, prob_ready.at(b, g * UNITS + n + 1 - SLOTS))
                            for jj in range(2):
                                bank, j = 2 + 2 * (n % SLOTS) + jj, 2 * pair + jj
                                last = mm(ps[:, bank, 0:cols], key[0:STACK + SHIFT, j, i * P:(i + 1) * P],
                                          q[0:STACK + SHIFT, j, t0:t0 + cols], start=True, stop=not diag)
                                if diag:
                                    last = mm(ps[:, bank, 0:P], ident_bf[:, :], mask_cols[:, :],
                                              start=False, stop=True)
                            last.then_inc(score_mm.sem, 1)
                        if n >= LAG:
                            half, i, t0, diag, pair = units[n - LAG]
                            cols = (half + 1) * HALF - t0
                            at = g * UNITS + n - LAG
                            pe.wait_ge(prob_ready.sem, prob_ready.at(b, at + 1))
                            if i == 0 and g > 0:
                                pe.wait_ge(y_copied.sem, y_copied.at(b, NH * (g - 1) + half + 1))
                            for jj in range(2):
                                j = 2 * pair + jj
                                v0 = (DH + 1) * (4 * g + j)
                                last = mm(ps[32 * j:32 * j + 32, 6 + half, t0 - half * HALF:HALF],
                                          v_ext[:, i, v0:v0 + 32], probs[:, at % PROBS, jj, 0:cols],
                                          start=(i == 0), stop=(i == (half + 1) * (NT // NH) - 1))
                            last.then_inc(pv_done.sem, 1)
                        for unit in PLANS[g][n]:
                            side_unit(*unit)
                for unit in LAST:
                    side_unit(*unit)
                pe.wait_ge(side_read.sem, side_read.at(b, len(SIDE)))
                turn(b, 3, None)
                pe.wait_ge(xT_ready.sem, xT_ready.at(b, 16))
                for i in range(NT):
                    for c in range(DC):
                        last = mm(tile_bank(i), xT[:, c, span(i)], w_o[:, c, :], start=(c == 0), stop=(c == DC - 1))
                    if i % 2:
                        last.then_inc(wo_mm.sem, 1)
                turn(b, 4, 3)
                pe.wait_ge(xT_ready.sem, xT_ready.at(b, 20))
                pe.wait_ge(route_w_in.sem, route_w_in.at(b, 16))
                alone(pe)
                with pe.Fori(0, TILES // 2) as m:
                    for k in range(2):
                        pe.wait_ge(routed.sem, routed.at(b, 0) + m * 2)
                        for i in range(NT):
                            for c in range(DC):
                                last = mm(ps[:, 4 * k + i // 2, (i % 2) * D:(i % 2 + 1) * D], xT[:, c, span(i)],
                                          w_route[:, m * 2 + k, c, :], start=(c == 0), stop=(c == DC - 1))
                        last.then_inc(route_mm.sem, 1)

        @block.vector
        def _(dve):
            tt, ts = nc.vector.tensor_tensor, nc.vector.tensor_scalar
            own = Chain(dve, prep_dve, 0)
            dve.wait_ge(weights_in.sem, ALL_IN)
            dve.wait_ge(preset.sem, 5)
            dve.wait_ge(prep_act.sem, 1)
            own.step(ts(neg_a[:, :, :], neg_a[:, :, :], -1.0, None, ALU.mult))
            dve.wait_ge(prep_mm.sem, K3 * DC + 3)
            pos_scores = ps[:, 7, 0:NT * TILES].rearrange("p (i t) -> p i t", t=TILES)
            own.step(nc.vector.tensor_reduce(best, pos_scores, AX_X, ALU.max))
            own.step(nc.vector.memset(taken, 0.0))
            own.settle()
            own.step(tt(is_best, pos_scores, best.unsqueeze(2).to_broadcast([P, NT, TILES]), ALU.is_ge))
            own.settle()
            for t in range(TILES):
                own.step(tt(route[:, :, t], is_best[:, :, t], taken, ALU.is_gt))
                own.settle()
                own.step(tt(taken, taken, is_best[:, :, t], ALU.max))
                own.settle()
            assert own.n == PREP_ROUTE, own.n
            dve.wait_ge(prep_mm.sem, K3 * DC + 4)
            own.step(nc.vector.tensor_copy(route_T, ps[0:TILES, 0:2, :].rearrange("p r s -> p (r s)")))
            dve.wait_ge(prep_mm.sem, K3 * DC + 5)
            own.step(nc.vector.tensor_copy(route_b[:, :, :].rearrange("p i n -> p (i n)"),
                                           ps[:, 0:4, :].rearrange("p r s -> p (r s)")))
            own.step(tt(u_bias[:, :], ps[:, 6, 0:EC], in_b[:, :], ALU.add))
            own.step(nc.vector.tensor_copy(table_f, ps[:, 4:6, :].rearrange("p r s -> p (r s)")))
            own.settle()
            last_tap = table_f[VOCAB:P, 2 * D:4 * D]
            own.step(tt(last_tap, last_tap, emb_rows[VOCAB:P, :], ALU.add))
            own.settle()
            own.step(tt(last_tap, last_tap, tok_b[VOCAB:P, :], ALU.add))
            own.settle()
            src = table_f
            for part in range(3):
                dst = table[:, part, :, :].rearrange("p c n -> p (c n)")
                own.step(nc.vector.tensor_copy(dst, src))
                own.settle()
                if part < 2:
                    own.step(tt(table_r, src, dst, ALU.subtract))
                    own.settle()
                    src = table_r
            assert own.n == PREP_DVE, own.n

            def layer_norm(b, k):
                for i in range(NT):
                    nc.vector.bn_stats(stats[:, i, :], h[:, i, :])
                dve.drain()
                for i in range(NT):
                    last = nc.vector.bn_aggr(mv[:, i, :], stats[:, i, :])
                last.then_inc(ln_stats.sem, 1)
                dve.wait_ge(ln_rstd.sem, ln_rstd.at(b, 2 * k + 2))
                for i in range(NT):
                    ts(xn[:, i, :], h[:, i, :], mv[:, i, 0:1], rstd[:, i:i + 1], ALU.subtract,
                       ALU.mult).then_inc(ln_norm.sem, 1)

            all_h = h[:, :, :].rearrange("p i n -> p (i n)")
            with dve.Fori(0, B) as b:
                dve.wait_ge(ids_in.sem, ids_in.at(b, 16 * TAPS))
                for c in range(2):
                    ts(onehot[:, c, :], ids[:, c, :], vocab_col[:, 0:1], None, ALU.is_equal)\
                        .then_inc(onehot_done.sem, 1)
                dve.wait_ge(trig_in.sem, trig_in.at(b, 32))
                dve.wait_ge(stored.sem, stored.at(b, 0))
                for i in range(NT):
                    dve.wait_ge(tok_mm.sem, tok_mm.at(b, i + 1))
                    tt(rotated[:, i % 2, :], ps[:, i % 2, :], trig[:, i, :], ALU.mult).then_inc(tok_rot.sem, 1)
                    dve.wait_ge(tok_rot.sem, tok_rot.at(b, i + 1))
                    tt(h[:, i, :], rotated[:, i % 2, 0:D], rotated[:, i % 2, D:2 * D],
                       ALU.add).then_inc(tok_sum.sem, 1)
                dve.wait_ge(tok_scale.sem, tok_scale.at(b, 2))
                for i in range(NT):
                    nc.vector.scalar_tensor_tensor(h[:, i, :], h[:, i, :], rstd[:, i:i + 1], norm_w[:, :],
                                                   ALU.mult, ALU.mult)
                dve.drain()
                layer_norm(b, 0)
                for c in range(EC):
                    dve.wait_ge(sp_ln.sem, sp_ln.at(b, c + 1))
                    tt(delta[:, c, :], delta[:, c, :], du[:, c, :], ALU.add).then_inc(delta_ready.sem, 1)
                dve.wait_ge(bc_mm.sem, bc_mm.at(b, 1))
                ts(bc_full, ps[0:2 * NS, 4:6, :].rearrange("p r s -> p (r s)"), bc_b[:, 0:1], None, ALU.add)
                dve.drain()
                nc.vector.tensor_copy(bc_parts[0:2 * NS, :], bc_full)
                dve.drain()
                tt(bc_rest, bc_full, bc_parts[0:2 * NS, :], ALU.subtract)
                dve.drain()
                nc.vector.tensor_copy(bc_part[:, 0:S], bc_rest)
                dve.drain()
                nc.vector.tensor_copy(bc_parts[2 * NS:4 * NS, :], bc_part[:, 0:S])
                tt(bc_rest, bc_rest, bc_part[:, 0:S], ALU.subtract)
                dve.drain()
                nc.vector.tensor_copy(bc_parts[4 * NS:6 * NS, :], bc_rest).then_inc(bc_split.sem, 1)
                dve.wait_ge(du_ready.sem, du_ready.at(b, EC))
                alone(dve)
                with dve.Fori(0, NS // 2) as m:
                    for k in range(2):
                        base = m * (2 * EC) + k * EC

                        def make_drive(c):
                            tt(drive[:, c % 2, :], du[:, c, :], ps[:, 2 * k:2 * k + 2, :].rearrange("p r s -> p (r s)"),
                               ALU.mult).then_inc(drive_ready.sem, 1)

                        def make_readout(c):
                            dve.wait_ge(scan_ready.sem, scan_ready.at(b, c + 1) + base)
                            tt(scan[:, c % 2, :], scan[:, c % 2, :], c_rows[:, k, :],
                               ALU.mult).then_inc(read_out.sem, 1)

                        dve.wait_ge(b_rows_mm.sem, b_rows_mm.at(b, k + 1) + m * 2)
                        make_drive(0)
                        for c in range(EC):
                            if c + 1 < EC:
                                make_drive(c + 1)
                            if c == 0:
                                dve.wait_ge(c_rows_out.sem, c_rows_out.at(b, k + 1) + m * 2)
                            dve.wait_ge(decay_ready.sem, decay_ready.at(b, c + 1) + base)
                            dve.wait_ge(drive_ready.sem, drive_ready.at(b, c + 1) + base)
                            if c < 2:
                                dve.wait_ge(y_added.sem, y_added.at(b, 0) + base)
                            else:
                                dve.wait_ge(y_added.sem, y_added.at(b, c - 1) + base)
                            nc.vector.tensor_tensor_scan(scan[:, c % 2, :], decay[:, c, :], drive[:, c % 2, :],
                                                         0.0, ALU.mult, ALU.add).then_inc(scan_ready.sem, 1)
                            make_readout(c)
                for p in range(NT // 2):
                    dve.wait_ge(mix_mm.sem, mix_mm.at(b, p + 1))
                    tt(all_h[:, p * HALF:(p + 1) * HALF], all_h[:, p * HALF:(p + 1) * HALF], ps[:, p, :], ALU.add)
                dve.drain()
                layer_norm(b, 1)
                all_xn = xn[:, :, :].rearrange("p i n -> p (i n)")
                dve.drain()
                tt(all_h, all_h, all_xn, ALU.add)
                dve.wait_ge(gate_mm.sem, gate_mm.at(b, 1))
                nc.vector.tensor_copy(scores4[:, :, :], ps[:, 4, 0:NT * NE].rearrange("p (i e) -> p i e", e=NE))
                dve.drain()
                nc.vector.tensor_reduce(top[:, :], scores4[:, :, :], AX_X, ALU.max)
                for e in range(NE):
                    if e > 0:
                        tt(beats[:, :, e, 0:e], scores4[:, :, 0:e],
                           scores4[:, :, e:e + 1].to_broadcast([P, NT, e]), ALU.is_ge)
                    if e < NE - 1:
                        tt(beats[:, :, e, e + 1:NE], scores4[:, :, e + 1:NE],
                           scores4[:, :, e:e + 1].to_broadcast([P, NT, NE - 1 - e]), ALU.is_gt)
                dve.drain()
                tt(gate[:, :, :], scores4[:, :, :], top[:, :].unsqueeze(2).to_broadcast([P, NT, NE]),
                   ALU.subtract).then_inc(gate_shift.sem, 1)
                nc.vector.tensor_reduce(rank[:, :, :], beats[:, :, :, :], AX_X, ALU.add)
                dve.drain()
                ts(rank[:, :, :], rank[:, :, :], 1.5, None, ALU.is_lt)
                dve.drain()
                dve.wait_ge(gate_exp.sem, gate_exp.at(b, 1))
                tt(gate[:, :, :], gate[:, :, :], rank[:, :, :], ALU.mult)
                dve.drain()
                nc.vector.tensor_reduce(top[:, :], gate[:, :, :], AX_X, ALU.add)
                dve.drain()
                nc.vector.reciprocal(top[:, :], top[:, :])
                dve.drain()
                tt(gate[:, :, :], gate[:, :, :], top[:, :].unsqueeze(2).to_broadcast([P, NT, NE]), ALU.mult)
                dve.drain()
                with dve.Fori(0, NE) as e:
                    for layer in range(2):
                        made, normed = (hid_mm, hid_norm) if layer == 0 else (out_mm, out_norm)
                        for i in range(NT):
                            if i % 2 == 0:
                                dve.wait_ge(made.sem, made.at(b, i // 2 + 1) + e * (NT // 2))
                            nc.vector.bn_stats(stats[:, i, :], tile_bank(i))
                        dve.drain()
                        for i in range(NT):
                            last = nc.vector.bn_aggr(mv[:, i, :], stats[:, i, :])
                        last.then_inc(exp_stats.sem, 1)
                        dve.wait_ge(exp_rstd.sem, exp_rstd.at(b, 2 if layer == 0 else 5) + e * 5)
                        for i in range(NT):
                            ts(z[:, i, :], tile_bank(i), mv[:, i, 0:1], rstd[:, i:i + 1], ALU.subtract,
                               ALU.mult).then_inc(normed.sem, 1)
                    for i in range(NT):
                        nc.vector.scalar_tensor_tensor(h[:, i, :], be2[:, e, :], gate[:, i, bass.ds(e, 1)],
                                                       h[:, i, :], ALU.mult, ALU.add)
                    dve.drain()
                    for i in range(NT):
                        dve.wait_ge(out_scaled.sem, out_scaled.at(b, i + 1) + e * NT)
                        tt(h[:, i, :], h[:, i, :], z[:, i, :], ALU.add)
                    dve.drain()
                layer_norm(b, 2)
                for n in range(4):
                    dve.wait_ge(att_in.sem, att_in.at(b, 48))
                    dve.wait_ge(qk_mm.sem, qk_mm.at(b, n + 1))
                    if n >= 2:
                        dve.wait_ge(part_low.sem, part_low.at(b, n - 1))
                        dve.wait_ge(part_mid.sem, part_mid.at(b, n - 1))
                    for r, dst in enumerate((plain, swapped)):
                        bank = 4 * (n % 2) + 2 * r
                        tt(dst[:, n % 2, :], ps[:, bank:bank + 2, :].rearrange("p r s -> p (r s)"),
                           head_rot[:, r, :], ALU.mult).then_inc(qk_turned.sem, 1)
                    dve.wait_ge(qk_turned.sem, qk_turned.at(b, 2 * n + 2))
                    tt(plain[:, n % 2, :], plain[:, n % 2, :], swapped[:, n % 2, :],
                       ALU.add).then_inc(qk_sum.sem, 1)
                    dve.wait_ge(part_high.sem, part_high.at(b, n + 1))
                    tt(plain[:, n % 2, :], plain[:, n % 2, :], parts[:, n % 2, 0, :],
                       ALU.subtract).then_inc(part_rest.sem, 1)
                dve.wait_ge(v_mm.sem, v_mm.at(b, 1))
                dve.wait_ge(att_set.sem, att_set.at(b, 3))
                nc.vector.tensor_copy(
                    v_ext[:, :, 0:HEADS * (DH + 1)].rearrange("p i (h d) -> p i h d", h=HEADS)[:, :, :, 0:DH],
                    ps[:, 0:4, :].rearrange("p k (r h d) -> p (k r) h d", r=2, h=HEADS)).then_inc(v_ready.sem, 1)

                def side_unit(kind, g, k):
                    at = SIDE[kind, g, k]
                    bank = at % 2
                    dve.wait_ge(side_mm.sem, side_mm.at(b, at + 1))
                    if kind == "raw":
                        i, s0, cols, diag = MAX_GROUPS[k // 4]
                        nc.vector.tensor_reduce(part_max[:, i, s0 // HALF, k % 4:k % 4 + 1], ps[:, bank, 0:cols],
                                                AX_X, ALU.max).then_inc(side_read.sem, 1)
                        if k == RAW - 1:
                            minus_maxima(g, at)
                    elif kind == "rows":
                        nc.vector.tensor_copy(max_rows[:, g % 2, :], ps[0:4 * SHIFT, bank, :].bitcast(BF16))\
                            .then_inc(side_read.sem, 1)
                    else:
                        y4 = ps[:, bank, :].rearrange("p (i j d) -> p i j d", i=NT // NH, j=4)
                        nc.vector.reciprocal(den_rec[:, k, :, :], y4[:, :, :, DH]).then_inc(den_ready.sem, 1)
                        dve.wait_ge(den_ready.sem, den_ready.at(b, NH * g + k + 1))
                        tiles = slice(k * (NT // NH), (k + 1) * (NT // NH))
                        tt(y_tok[:, tiles, 4 * DH * g:4 * DH * (g + 1)].rearrange("p i (j d) -> p i j d", j=4),
                           y4[:, :, :, 0:DH], den_rec[:, k, :, :].unsqueeze(3).to_broadcast([P, NT // NH, 4, DH]),
                           ALU.mult).then_inc(side_read.sem, 1)

                def minus_maxima(g, at):
                    dve.wait_ge(side_read.sem, side_read.at(b, at + 1))
                    full = NT // NH
                    ts(neg_max[:, 0:full, :], part_max[:, 0:full, 0, :], -1.0, None, ALU.mult)
                    tt(part_max[:, full:NT, 0, :], part_max[:, full:NT, 0, :], part_max[:, full:NT, 1, :], ALU.max)
                    dve.drain()
                    ts(neg_max[:, full:NT, :], part_max[:, full:NT, 0, :], -1.0, None, ALU.mult)
                    for part in range(SHIFT):
                        dve.drain()
                        last = nc.vector.tensor_copy(max_parts[:, :, :, part], neg_max[:, :, :])
                        if part < SHIFT - 1:
                            dve.drain()
                            tt(neg_max[:, :, :], neg_max[:, :, :], max_parts[:, :, :, part], ALU.subtract)
                    last.then_inc(max_ready.sem, 1)

                for unit in FIRST:
                    side_unit(*unit)
                for g in range(QUADS):
                    for side in PLANS[g]:
                        for unit in side:
                            side_unit(*unit)
                for unit in LAST:
                    side_unit(*unit)
                dve.drain()
                for p in range(NT // 2):
                    dve.wait_ge(wo_mm.sem, wo_mm.at(b, p + 1))
                    tt(all_h[:, p * HALF:(p + 1) * HALF], all_h[:, p * HALF:(p + 1) * HALF], ps[:, p, :], ALU.add)
                dve.drain()
                layer_norm(b, 3)
                dve.drain()
                tt(all_h, all_h, route_b[:, :, :].rearrange("p i n -> p (i n)"), ALU.add)
                dve.drain()
                with dve.Fori(0, TILES // 2) as m:
                    for k in range(2):
                        dve.wait_ge(route_mm.sem, route_mm.at(b, k + 1) + m * 2)
                        for i in range(NT):
                            last = nc.vector.scalar_tensor_tensor(
                                h[:, i, :], ps[:, 4 * k + i // 2, (i % 2) * D:(i % 2 + 1) * D],
                                route[:, i, bass.ds(m * 2 + k, 1)], h[:, i, :], ALU.mult, ALU.add)
                        last.then_inc(routed.sem, 1)
                        dve.wait_ge(routed.sem, routed.at(b, k + 1) + m * 2)
                dve.drain().then_inc(h_final.sem, 1)


PREP_MM = K3 * DC + 5
PREP_ROUTE = 4 + 2 * TILES
PREP_DVE = PREP_ROUTE + 11


def constants():
    f32 = np.float32

    def bf16_bits(x):
        return (np.ascontiguousarray(x, f32).view(np.uint32) >> 16).astype(np.uint16)

    c = {}
    c["c_ident"] = np.eye(P, dtype=f32)
    c["c_ident_bf"] = bf16_bits(np.eye(P))
    later = np.triu(np.ones((P, P), bool), 1)
    c["c_mask_rows"] = bf16_bits(np.where(later, MASKED, 0.0))
    c["c_mask_cols"] = bf16_bits(np.where(later.T, MASKED, 0.0))
    c["c_vocab"] = (np.arange(P) % VOCAB).astype(f32)[:, None]
    inv = (1.0 / np.power(f32(10000.0), np.arange(0, D, 2, dtype=f32) / f32(D))).astype(f32)
    freqs = np.arange(S, dtype=f32)[:, None] * inv[None, :]
    emb = np.concatenate([freqs, freqs], axis=-1)
    sign = np.where(np.arange(D) % 2 == 0, -1.0, 1.0).astype(f32)
    both = np.concatenate([np.cos(emb), np.sin(emb) * sign], axis=1).astype(f32)
    c["c_trig"] = both.reshape(NT, P, 2 * D).transpose(1, 0, 2).copy()
    half = DH // 2
    theta = (1.0 / np.power(f32(10000.0), np.arange(half, dtype=f32) / f32(half))).astype(f32)
    ang = np.arange(S, dtype=f32)[:, None] * theta[None, :]
    cos, sin = np.cos(ang).astype(f32).T, np.sin(ang).astype(f32).T
    rows = np.stack([np.concatenate([cos, cos]), np.concatenate([-sin, sin])], axis=1)
    c["c_head_rot"] = np.tile(rows, (P // DH, 1, 1))
    pick = np.zeros((3, 2 * NS, 2 * NS, P), f32)
    for n in range(2 * NS):
        pick[:, n, n, :] = 1.0
    c["c_pick_state"] = bf16_bits(pick.reshape(3 * 2 * NS, 2 * NS, P))
    pos = np.arange(S, dtype=f32)[:, None]
    div = np.exp(np.arange(0, PDIM, 2, dtype=f32) * f32(-np.log(10000.0) / PDIM)).astype(f32)
    ang = (pos * div).astype(f32)
    enc = np.zeros((S, PDIM), f32)
    enc[:, 0::2], enc[:, 1::2] = np.sin(ang), np.cos(ang)
    c["c_pe_T"] = enc.T.copy()
    return c


def layouts(i):
    def chunks(w):
        return w.reshape(-1, P, w.shape[1]).transpose(1, 0, 2)

    def column(v):
        return v.reshape(-1, P).T

    swap = np.arange(D) ^ 1
    both = np.concatenate([np.arange(D), swap])
    r = {"x": i["x"]}
    w = i["L0_tok_conv_w"].transpose(1, 2, 0)[:, :, both]
    r["tok_conv_w"] = w.reshape(DC, P, TAPS, 2 * D).transpose(1, 0, 2, 3)
    r["tok_conv_b"] = i["L0_tok_conv_b"][both]
    r["emb_T"] = chunks(i["L0_tok_embed_table"].T)
    r["emb_rows"] = i["L0_tok_embed_table"][:, both]
    r["tok_norm_w"] = i["L0_tok_norm_w"]
    r["mix_conv_w"] = i["L0_attn_conv_w"].transpose(0, 2, 1).reshape(EC, P, K3, D).transpose(1, 0, 2, 3)
    r["mix_conv_b"] = column(i["L0_attn_conv_b"])
    r["in_w"] = chunks(i["L0_attn_in_w"].T)
    r["in_b"] = column(i["L0_attn_in_b"])
    r["dt_w"] = chunks(i["L0_attn_dt_w"].T)
    r["dt_b"] = column(i["L0_attn_dt_b"])
    r["bc_w"] = chunks(np.concatenate([i["L0_attn_Bp_w"], i["L0_attn_Cp_w"]]).T)
    r["bc_b"] = np.concatenate([i["L0_attn_Bp_b"], i["L0_attn_Cp_b"]])[:, None]
    r["a_log"] = i["L0_attn_A_log"].reshape(EC, P, NS).transpose(1, 2, 0)
    r["d_skip"] = column(i["L0_attn_Dskip"])
    r["out_w"] = chunks(i["L0_attn_out_w"].T)
    r["out_b"] = i["L0_attn_out_b"][None]
    r["gate_w"] = chunks(i["L0_ffn_gate_W"])
    r["gate_b"] = i["L0_ffn_gate_b"][None]
    r["b1"], r["b2"] = i["L0_ffn_b1"][None], i["L0_ffn_b2"][None]
    r["g1"] = i["L0_ffn_g1"].reshape(NE, DC, P).transpose(2, 0, 1)
    r["be1"] = i["L0_ffn_be1"].reshape(NE, DC, P).transpose(2, 0, 1)
    r["g2"], r["be2"] = i["L0_ffn_g2"], i["L0_ffn_be2"]
    w = np.stack([i["L0_ffn_W1"], i["L0_ffn_W2"]]).reshape(2, NE, DC, P, D)
    r["w_moe"] = w.transpose(3, 0, 1, 2, 4).reshape(P, -1)
    r["w_route"] = i["L1_ffn_W"].transpose(0, 2, 1).reshape(TILES, DC, P, D).transpose(2, 0, 1, 3).reshape(P, -1)
    r["route_b"] = i["L1_ffn_b"]
    r["sigs_T"] = i["L1_ffn_tile_sigs"].T
    qkv = i["L1_attn_W_qkv"]
    swapped = np.arange(D) ^ (DH // 2)
    cols = np.concatenate([r0 * D + order[c * P:(c + 1) * P]
                           for c in range(DC) for r0 in range(2) for order in (np.arange(D), swapped)])
    r["w_qk"] = chunks(qkv[:, cols]).reshape(P, DC, 2 * 2 * DC, P)
    r["w_v"] = chunks(qkv[:, 2 * D:])
    r["w_o"] = chunks(i["L1_attn_W_o"])
    return {k: np.ascontiguousarray(v) for k, v in r.items()}


def kernel(**inputs):
    import concourse.bacc as bacc
    from concourse.bass_utils import run_bass_kernel_spmd

    arrays = layouts({k: np.asarray(v) for k, v in inputs.items()})
    arrays.update(constants())
    nc = bacc.Bacc("TRN2", target_bir_lowering=False, num_devices=1)
    aps = {k: nc.dram_tensor(f"in_{k}", v.shape, mybir.dt.from_np(v.dtype), kind="ExternalInput").ap()
           for k, v in arrays.items()}
    out = nc.dram_tensor("out_h", (B, S, D), F32, kind="ExternalOutput").ap()
    build(nc, aps, out)
    r = run_bass_kernel_spmd(nc, [{f"in_{k}": v for k, v in arrays.items()}], core_ids=[0])
    return r.results[0]["out_h"]
```

```python
from contextlib import ExitStack

import numpy as np

import concourse.bass as bass
from concourse import mybir

ALU = mybir.AluOpType
ACT = mybir.ActivationFunctionType
F32 = mybir.dt.float32
BF16 = mybir.dt.bfloat16
I32 = mybir.dt.int32
AX_X = mybir.AxisListType.X

P = 128
B = 8
S = 1024
D = 256
NT = S // P
DC = D // P
HALF = 512
NH = S // HALF
VOCAB = 64
TAPS = 4
E = 512
EC = E // P
NS = 16
K3 = 3
NE = 4
HEADS = 16
DH = 16
QUADS = HEADS // 4
TILES = 8
PDIM = 32
RMS_EPS = 1.1920929e-07
LN_EPS = 1e-05
MASKED = -1e30


class Signal:

    def __init__(self, sem, per_batch, start):
        self.sem, self.per_batch, self.start = sem, per_batch, start

    def at(self, b, n):
        return b * self.per_batch + (n + self.start)


class Chain:

    def __init__(self, eng, signal, base):
        self.eng, self.sem, self.base, self.n = eng, signal.sem, base, 0

    def step(self, ins):
        self.n += 1
        ins.then_inc(self.sem, 1)

    def settle(self):
        self.eng.wait_ge(self.sem, self.base + self.n)


MAX_GROUPS = [(i, c * HALF, min((i + 1) * P - c * HALF, HALF), (i * P) // HALF == c)
              for i in range(NT) for c in range(NH) if c * HALF < (i + 1) * P]
PROB_GROUPS = [(i, max(half * HALF, i * P), (half + 1) * HALF - max(half * HALF, i * P), i * P >= half * HALF)
               for half in range(NH) for i in range(NT) if i * P < (half + 1) * HALF]


def by_heads(groups, banks):
    units = []
    for group in groups:
        size = banks * (2 if group[2] <= HALF // 2 else 1)
        units += [(*group, tuple(range(j, j + size))) for j in range(0, 4, size)]
    return units


MAX_UNITS = by_heads(MAX_GROUPS, 1)
PROB_UNITS = by_heads(PROB_GROUPS, 2)
RAW = len(MAX_UNITS)
UNITS = len(PROB_UNITS)
HALF_UNITS = sum(t0 < HALF for i, t0, cols, diag, heads in PROB_UNITS)
SLOTS = 2
LAG = SLOTS
PROBS = 3
EARLY = 8
STACKS = 3
U_ORDER = [(0, 0), (1, 0), (0, 1), (1, 1)] + [(c, half) for c in range(2, EC) for half in range(NH)]
Q_PARTS = (0, 1, 2, 0, 1, 0)
K_PARTS = (0, 1, 0, 1, 0, 2)
Q_RUNS = ((0, 0, 3), (3, 0, 2), (5, 0, 1))
K_RUNS = ((0, 0, 2), (2, 0, 2), (4, 0, 1), (5, 2, 1))
PLACEMENTS = len(Q_RUNS) + len(K_RUNS)
STACK = DH * len(Q_PARTS)
SHIFT = 3
BIAS_ROWS = 96
PASS = 2 * NS
STEPS = NE * NT // 2


def turn_plan(g):
    plan = []
    for n in range(UNITS + LAG):
        side = []
        if g + 1 < QUADS and EARLY + 2 * n < RAW:
            side += [("raw", g + 1, EARLY + 2 * n), ("raw", g + 1, EARLY + 2 * n + 1)]
        if g > 0 and n == 1:
            side.append(("y", g - 1, 1))
        if n == HALF_UNITS + LAG + 1:
            side.append(("y", g, 0))
        if g + 1 < QUADS and n == (RAW - EARLY) // 2 + 1:
            side.append(("rows", g + 1, 0))
        early = 2 * (n - (UNITS + LAG)) + EARLY
        if g + 2 < QUADS and early >= 0:
            side += [("raw", g + 2, early), ("raw", g + 2, early + 1)]
        plan.append(side)
    return plan


FIRST = [("raw", 0, k) for k in range(RAW)] + [("rows", 0, 0)] + [("raw", 1, k) for k in range(EARLY)]
PLANS = [turn_plan(g) for g in range(QUADS)]
LAST = [("y", QUADS - 1, 1)]
SIDE = {unit: k for k, unit in enumerate(FIRST + [u for plan in PLANS for side in plan for u in side] + LAST)}
assert len(SIDE) == QUADS * (RAW + 1 + NH)


def side_bank(at):
    return 4 + at % 4 if at < RAW else at % 2


def build(nc, a, out):
    with ExitStack() as ctx:
        def sb(name, shape, dt=F32):
            return ctx.enter_context(nc.sbuf_tensor(name, shape, dt))

        def signal(name, per_batch=0, start=0):
            return Signal(ctx.enter_context(nc.semaphore(name)), per_batch, start)

        ident = sb("ident", [P, P])
        ident_bf = sb("ident_bf", [P, P], BF16)
        mask_rows = sb("mask_rows", [P, P], BF16)
        mask_cols = sb("mask_cols", [P, P], BF16)
        ones_row = sb("ones_row", [1, P])
        ones_bf = sb("ones_bf", [BIAS_ROWS, P], BF16)
        vocab_col = sb("vocab_col", [P, 1])
        norm_w = sb("norm_w", [P, D])
        table = sb("table", [P, 3, 2, 2 * D], BF16)
        rms_eps = sb("rms_eps", [P, 1])
        ln_eps = sb("ln_eps", [P, 1])
        conv_in = sb("conv_in", [P, K3, DC, E])
        u_bias = sb("u_bias", [P, EC])
        in_b = sb("in_b", [P, EC])
        conv_b = sb("conv_b", [P, EC])
        dt_w = sb("dt_w", [P, EC, E])
        dt_b = sb("dt_b", [P, EC])
        bc_w = sb("bc_w", [P, EC, 2 * NS])
        bc_b = sb("bc_b", [2 * NS, 1])
        neg_a = sb("neg_a", [P, NS, EC])
        d_skip = sb("d_skip", [P, EC])
        out_w = sb("out_w", [P, EC, D])
        pick_state = sb("pick_state", [3 * 2 * NS, 2 * NS, P], BF16)
        gate_w = sb("gate_w", [P, DC, NE])
        gate_b = sb("gate_b", [1, NE])
        bias = sb("bias", [BIAS_ROWS, 2 * NE + 1, D], BF16)
        g1 = sb("g1", [P, NE, DC])
        be1 = sb("be1", [P, NE, DC])
        g2 = sb("g2", [P, NE, D])
        be2 = sb("be2", [NE, D])
        w_o = sb("w_o", [P, DC, D])
        route = sb("route", [P, NT, TILES])
        route_b = sb("route_b", [P, NT, D])
        w_stream = sb("w_stream", [P, 8 * DC * D])
        w_moe = w_stream[:, :].rearrange("p (l e c n) -> p l e c n", l=2, e=NE, c=DC)
        w_route = w_stream[:, :].rearrange("p (t c n) -> p t c n", t=TILES, c=DC)
        w_v = sb("w_v", [P, DC, D])

        h = sb("h", [P, NT, D])
        xn = sb("xn", [P, NT, D])
        xT = sb("xT", [P, DC, S + 2])
        stats = sb("stats", [P, NT, 6])
        mv = sb("mv", [P, NT, 2])
        deviation = sb("deviation", [P, NT])
        rstd = sb("rstd", [P, NT])
        exp_bn = sb("exp_bn", [P, 2, 2, 2, 6])
        exp_mv = sb("exp_mv", [P, 2, 2, 2, 2])
        exp_dev = sb("exp_dev", [P, 2, 2, 2])
        exp_rstd = sb("exp_rstd", [P, 2, 2, 2])
        scores4 = sb("scores4", [P, NT, NE])
        top = sb("top", [P, NT])
        beats = sb("beats", [P, NT, NE, NE])
        rank = sb("rank", [P, NT, NE])
        gate = sb("gate", [P, NT, NE])
        neg_max = sb("neg_max", [P, NT, 4])
        max_parts = sb("max_parts", [P, NT, 4, SHIFT], BF16)
        den_rec = sb("den_rec", [P, NH, NT // NH, 4])
        part_max = sb("part_max", [P, NT, NH, 4])

        buf_u = sb("buf_u", [P, EC * S])
        buf_delta = sb("buf_delta", [P, EC * S])
        buf_du = sb("buf_du", [P, EC * S])
        buf_y = sb("buf_y", [P, EC * S])
        buf_decay = sb("buf_decay", [P, EC * S])
        buf_scan = sb("buf_scan", [P, 4 * S])
        conv_in_w = buf_decay[:, 0:EC * K3 * D].rearrange("p (e k n) -> p e k n", e=EC, k=K3)
        in_w = buf_u[:, 0:EC * E].rearrange("p (e n) -> p e n", e=EC)
        tok_w = buf_delta[:, :].rearrange("p (c j n) -> p c j n", c=DC, j=TAPS)
        emb_T = buf_u[:, 2048:2048 + DC * VOCAB].rearrange("p (c v) -> p c v", c=DC)
        emb_rows = buf_u[:, 2304:2304 + 2 * D]
        tok_b = buf_u[:, 2816:2816 + 2 * D]
        table_f = buf_y[:, 0:1024]
        table_r = buf_y[:, 1024:2048]
        sigs_T = buf_y[0:PDIM, 2048:2048 + TILES]
        a_log = buf_y[:, 2064:2064 + NS * EC].rearrange("p (n c) -> p n c", c=EC)
        sign_T = buf_y[0:PDIM, 2136:2136 + TILES]
        route_T = buf_y[0:TILES, 2176:2176 + S]
        b_tiles = buf_y[0:TILES, 3200:3200 + D]
        best = buf_y[:, 3456:3456 + NT]
        taken = buf_y[:, 3472:3472 + NT]
        is_best = buf_y[:, 3488:3488 + NT * TILES].rearrange("p (i t) -> p i t", t=TILES)
        pe_full = buf_du[0:PDIM, 0:S]
        bias_f = buf_du[0:BIAS_ROWS, S:S + (2 * NE + 1) * D].rearrange("p (r n) -> p r n", n=D)
        bias_part = buf_scan[0:BIAS_ROWS, 0:(2 * NE + 1) * D // 2].bitcast(BF16).rearrange("p (r n) -> p r n", n=D)
        ids = buf_scan[:, 0:2 * S].bitcast(I32).rearrange("p (c s) -> p c s", c=2)
        onehot = buf_y[:, 0:S].bitcast(BF16).rearrange("p (c s) -> p c s", c=2)
        trig = buf_delta[:, :].rearrange("p (i n) -> p i n", i=NT)
        rotated = buf_du[:, 0:1024].rearrange("p (r n) -> p r n", r=2)
        squares = buf_du[:, 1024:1024 + NT * D].rearrange("p (i n) -> p i n", i=NT)
        square_sum = sb("square_sum", [P, NT])
        tok_rms = sb("tok_rms", [P, NT])
        tok_scale = sb("tok_scale", [P, NT])
        u = buf_u[:, :].rearrange("p (c s) -> p c s", c=EC)
        delta = buf_delta[:, :].rearrange("p (c s) -> p c s", c=EC)
        du = buf_du[:, :].rearrange("p (c s) -> p c s", c=EC)
        y = buf_y[:, :].rearrange("p (c s) -> p c s", c=EC)
        decay = buf_decay[:, :].rearrange("p (c s) -> p c s", c=EC)
        scan = buf_scan[:, :].rearrange("p (c s) -> p c s", c=4)
        drive = buf_u[:, 0:2 * S].rearrange("p (c s) -> p c s", c=2)
        c_rows = buf_u[:, 2 * S:4 * S].rearrange("p (c s) -> p c s", c=2)
        bc_full = buf_decay[0:2 * NS, 0:S]
        bc_rest = buf_decay[0:2 * NS, S:2 * S]
        bc_part = buf_decay[0:2 * NS, 2 * S:3 * S].bitcast(BF16)
        bc_parts = w_v[0:3 * 2 * NS, :, :].rearrange("p c n -> p (c n)")[:, 0:S // 2].bitcast(BF16)
        z1 = buf_du[:, 0:4 * D].rearrange("p (s i n) -> p s i n", s=2, i=2)
        z2 = buf_du[:, 4 * D:8 * D].rearrange("p (s i n) -> p s i n", s=2, i=2)
        hid_T = buf_du[:, 8 * D:12 * D].rearrange("p (s c t) -> p s c t", s=2, c=DC)
        gate_T = buf_du[0:NE, 12 * D:12 * D + S]
        half_w = 2 * S
        stack = [[part.bitcast(BF16).rearrange("p (j s) -> p j s", j=4)
                  for part in (buf[:, 0:half_w], buf[:, half_w:])] for buf in (buf_u, buf_y, buf_delta)]
        w_qk = buf_y[:, 0:half_w].rearrange("p (c n m) -> p c n m", c=DC, n=8)
        head_rot = buf_scan[:, 0:2 * S].rearrange("p (r s) -> p r s", r=2)
        plain = buf_decay[:, 0:half_w].rearrange("p (r s) -> p r s", r=2)
        swapped = buf_decay[:, half_w:].rearrange("p (r s) -> p r s", r=2)
        parts = buf_delta[:, 0:2 * SHIFT * S // 2].bitcast(BF16).rearrange("p (r t s) -> p r t s", r=2, t=SHIFT)
        probs = buf_decay[:, 0:PROBS * S].rearrange("p (r j s) -> p r j s", r=PROBS, j=2)
        y_sum = buf_decay[:, PROBS * S:].rearrange("p (r s) -> p r s", r=NH)
        v_cols = HEADS * (DH + 1) + 16
        v_ext = buf_du[:, 0:NT * v_cols].rearrange("p (i n) -> p i n", i=NT)
        max_rows = buf_du[0:4 * SHIFT, NT * v_cols:NT * v_cols + S].bitcast(BF16).rearrange("p (r s) -> p r s", r=2)
        y_tok = xn
        qk_dram = nc.dram_tensor("qk_parts", (4, SHIFT, P, S), BF16, kind="Internal").ap()

        ps = ctx.enter_context(nc.psum_tensor("ps", [P, 8, HALF], F32))

        def heads_view(bank, cols, heads):
            if len(heads) == 2:
                return ps[:, bank:bank + 2, 0:cols]
            return ps[:, bank:bank + 2, :].rearrange("p r (h s) -> p (r h) s", h=2)[:, :, 0:cols]

        def raw_view(bank, cols, heads):
            return ps[:, bank, 0:len(heads) * (HALF // len(heads))]\
                .rearrange("p (h s) -> p h s", h=len(heads))[:, :, 0:cols]

        def probs_view(slot, cols, heads):
            if len(heads) == 2:
                return probs[:, slot, :, 0:cols]
            return probs[:, slot, :, :].rearrange("p r (h s) -> p (r h) s", h=2)[:, :, 0:cols]

        def tile_bank(i):
            return ps[:, i // 2, (i % 2) * D:(i % 2 + 1) * D]

        def span(i):
            return slice(1 + i * P, 1 + (i + 1) * P)

        weights_in = signal("weights_in")
        preset = signal("preset")
        prep_mm = signal("prep_mm")
        prep_act = signal("prep_act")
        prep_dve = signal("prep_dve")
        ids_clear = signal("ids_clear", 1)
        ids_in = signal("ids_in", 16 * TAPS)
        trig_in = signal("trig_in", 16)
        moe_w_in = signal("moe_w_in", 16)
        route_w_in = signal("route_w_in", 16)
        onehot_done = signal("onehot_done", 2)
        tok_mm = signal("tok_mm", NT)
        tok_rot = signal("tok_rot", NT)
        tok_sum = signal("tok_sum", NT)
        tok_sq = signal("tok_sq", NT)
        tok_root = signal("tok_root", NT // 2)
        tok_rec = signal("tok_rec", NT // 2)
        ln_stats = signal("ln_stats", 4 * NT // 2)
        ln_dev = signal("ln_dev", 4 * NT // 2)
        ln_rstd = signal("ln_rstd", 4 * NT // 2)
        ln_norm = signal("ln_norm", 4 * NT)
        ln_turned = signal("ln_turned", 5 * NT // 2)
        xT_ready = signal("xT_ready", 5 * NT // 2)
        u_mm = signal("u_mm", EC * NH)
        u_ready = signal("u_ready", EC * NH)
        dt_mm = signal("dt_mm", EC * NH)
        dt_abs = signal("dt_abs", EC * NH)
        dt_relu = signal("dt_relu", EC * NH)
        sp_exp = signal("sp_exp", EC)
        sp_ln = signal("sp_ln", EC)
        delta_ready = signal("delta_ready", EC)
        du_ready = signal("du_ready", 2)
        du_rest = signal("du_rest", 2)
        y_init = signal("y_init", EC)
        bc_mm = signal("bc_mm", 1)
        bc_split = signal("bc_split", 1)
        b_rows_mm = signal("b_rows_mm", 2 * NS)
        c_rows_mm = signal("c_rows_mm", 2 * NS)
        c_rows_out = signal("c_rows_out", 2 * NS, start=1)
        decay_ready = signal("decay_ready", NS * EC, start=1)
        drive_ready = signal("drive_ready", NS * EC, start=1)
        scan_ready = signal("scan_ready", NS * EC, start=4)
        read_out = signal("read_out", NS * EC, start=4)
        y_added = signal("y_added", NS * EC, start=4)
        y_out = signal("y_out", EC)
        mix_mm = signal("mix_mm", NT // 2)
        gate_mm = signal("gate_mm", 1)
        gate_shift = signal("gate_shift", 1)
        gate_exp = signal("gate_exp", 1)
        gate_ready = signal("gate_ready", 1)
        gate_turned = signal("gate_turned", 1)
        gate_T_ready = signal("gate_T_ready", 1)
        be_mm = signal("be_mm", NT // 2)
        be_added = signal("be_added", NT // 2)
        hid_mm = signal("hid_mm", STEPS)
        hid_stats = signal("hid_stats", STEPS)
        hid_dev = signal("hid_dev", STEPS)
        hid_rstd = signal("hid_rstd", STEPS)
        hid_norm = signal("hid_norm", STEPS)
        hid_turned = signal("hid_turned", STEPS)
        hid_ready = signal("hid_ready", STEPS)
        out_mm = signal("out_mm", STEPS)
        out_stats = signal("out_stats", STEPS)
        out_dev = signal("out_dev", STEPS)
        out_rstd = signal("out_rstd", STEPS)
        out_gated = signal("out_gated", STEPS)
        out_norm = signal("out_norm", STEPS)
        out_scaled = signal("out_scaled", STEPS)
        out_added = signal("out_added", STEPS)
        att_in = signal("att_in", 16 * 3)
        att_set = signal("att_set", 4)
        qk_mm = signal("qk_mm", 4)
        v_mm = signal("v_mm", 1)
        qk_turned = signal("qk_turned", 8, start=1)
        qk_sum = signal("qk_sum", 4)
        part_high = signal("part_high", 4)
        part_rest = signal("part_rest", 4)
        part_mid = signal("part_mid", 4)
        part_low = signal("part_low", 4)
        parts_out = [signal(f"parts_out{n}", 16, start=1) for n in range(4)]
        v_ready = signal("v_ready", 1)
        placed = [signal(f"placed{g}", 16 * PLACEMENTS, start=1) for g in range(QUADS)]
        side_mm = signal("side_mm", len(SIDE))
        side_read = signal("side_read", len(SIDE))
        max_ready = signal("max_ready", QUADS)
        rows_placed = [signal(f"rows_placed{g}", 16 * 4) for g in range(QUADS)]
        score_mm = signal("score_mm", UNITS * QUADS)
        prob_ready = signal("prob_ready", UNITS * QUADS)
        pv_done = signal("pv_done", UNITS * QUADS)
        y_copied = signal("y_copied", NH * QUADS)
        den_ready = signal("den_ready", NH * QUADS)
        wo_mm = signal("wo_mm", NT // 2)
        route_mm = signal("route_mm", TILES, start=1)
        routed = signal("routed", TILES, start=2)
        h_final = signal("h_final", 1)
        stored = signal("stored", 16, start=1)

        loads = [
             (ident, a["c_ident"]), (norm_w[:, :], a["tok_norm_w"].partition_broadcast(P)), (vocab_col, a["c_vocab"]),
            (in_b, a["in_b"]), (conv_b, a["mix_conv_b"]), (dt_w, a["dt_w"]), (dt_b, a["dt_b"]), (bc_w, a["bc_w"]),
            (bc_b, a["bc_b"]), (d_skip, a["d_skip"]), (out_w, a["out_w"]),
            (gate_w, a["gate_w"]), (gate_b, a["gate_b"]), (bias_f, a["bias"].partition_broadcast(BIAS_ROWS)), (g1, a["g1"]),
            (be1, a["be1"]), (g2, a["g2"].partition_broadcast(P)), (be2, a["be2"]),
            (w_o, a["w_o"]), (pick_state, a["c_pick_state"].bitcast(BF16)),
            (ident_bf, a["c_ident_bf"].bitcast(BF16)), (mask_rows, a["c_mask_rows"].bitcast(BF16)), (mask_cols, a["c_mask_cols"].bitcast(BF16)),
            (conv_in_w, a["mix_conv_w"]), (in_w, a["in_w"]), (tok_w, a["tok_conv_w"]), (emb_T, a["emb_T"]),
            (emb_rows[VOCAB:P, :], a["emb_rows"]), (tok_b[VOCAB:P, :], a["tok_conv_b"].partition_broadcast(VOCAB)),
            (pe_full, a["c_pe_T"]), (sigs_T, a["sigs_T"]), (a_log, a["a_log"]), (b_tiles, a["route_b"]),
        ]
        ALL_IN = 16 * len(loads)

        def alone(eng):
            eng.sem_inc(passed.sem, 1)

        passed = signal("passed")

        block = ctx.enter_context(nc.Block())

        @block.sync
        def _(sp):
            for dst, src in loads:
                sp.dma_start(dst if isinstance(dst, bass.AP) else dst.ap(), src).then_inc(weights_in.sem, 16)
            sp.wait_ge(prep_mm.sem, PREP_MM)
            sp.wait_ge(prep_dve.sem, PREP_DVE)

            def place_quad(b, g):
                for r, runs in enumerate((Q_RUNS, K_RUNS)):
                    rows = qk_dram[2 * (g // 2) + r].rearrange("t p s -> (t p) s")\
                        .rearrange("(m q j) s -> q m j s", q=2, j=4)[g % 2]
                    for m, t, count in runs:
                        sp.dma_start(stack[g % STACKS][r][DH * m:DH * (m + count), :, :],
                                     rows[DH * t:DH * (t + count)]).then_inc(placed[g].sem, 16)

            def place_rows(b, g):
                sp.wait_ge(side_read.sem, side_read.at(b, SIDE["rows", g, 0] + 1))
                for j in range(4):
                    sp.dma_start(stack[g % STACKS][0][STACK:STACK + SHIFT, j, :],
                                 max_rows[SHIFT * j:SHIFT * (j + 1), g % 2, :]).then_inc(rows_placed[g].sem, 16)

            def load_ids(b):
                for j in range(TAPS):
                    late = TAPS - 1 - j
                    half = slice((j % 2) * VOCAB, (j % 2 + 1) * VOCAB)
                    sp.dma_start(ids[half, j // 2, late:S],
                                 a["x"][b, 0:S - late].partition_broadcast(VOCAB)).then_inc(ids_in.sem, 16)

            sp.dma_start(trig, a["c_trig"]).then_inc(trig_in.sem, 16)
            sp.wait_ge(ids_clear.sem, 1)
            load_ids(0)
            with sp.Fori(0, B) as b:
                sp.wait_ge(route_mm.sem, route_mm.at(b, 0))
                sp.dma_start(w_stream[:, :], a["w_moe"]).then_inc(moe_w_in.sem, 16)
                sp.wait_ge(mix_mm.sem, mix_mm.at(b, NT // 2))
                sp.dma_start(w_qk, a["w_qk"]).then_inc(att_in.sem, 16)
                sp.dma_start(w_v[:, :, :], a["w_v"]).then_inc(att_in.sem, 16)
                sp.dma_start(head_rot, a["c_head_rot"]).then_inc(att_in.sem, 16)
                for n in range(4):
                    sp.wait_ge(part_low.sem, part_low.at(b, n + 1))
                    sp.wait_ge(part_mid.sem, part_mid.at(b, n + 1))
                    for g in range(2 * (n // 2), 2 * (n // 2) + 2):
                        sp.wait_ge(placed[g].sem, placed[g].at(b, 0))
                    sp.dma_start(qk_dram[n].rearrange("t p s -> p t s"), parts[:, n % 2, :, :])\
                      .then_inc(parts_out[n].sem, 16)
                    if n == 1:
                        for r in range(2):
                            sp.wait_ge(parts_out[r].sem, parts_out[r].at(b, 16))
                        place_quad(b, 0)
                sp.wait_ge(qk_mm.sem, qk_mm.at(b, 4))
                place_quad(b, 1)
                for n in range(2, 4):
                    sp.wait_ge(parts_out[n].sem, parts_out[n].at(b, 16))
                place_quad(b, 2)
                place_rows(b, 0)
                place_rows(b, 1)
                sp.wait_ge(score_mm.sem, score_mm.at(b, UNITS))
                place_quad(b, 3)
                sp.wait_ge(out_mm.sem, out_mm.at(b, STEPS))
                sp.dma_start(w_stream[:, :], a["w_route"]).then_inc(route_w_in.sem, 16)
                place_rows(b, 2)
                place_rows(b, 3)
                sp.wait_ge(score_mm.sem, score_mm.at(b, 3 * UNITS))
                sp.dma_start(trig, a["c_trig"]).then_inc(trig_in.sem, 16)
                sp.wait_ge(ids_clear.sem, ids_clear.at(b, 2))
                load_ids(b + 1)
                sp.wait_ge(h_final.sem, h_final.at(b, 1))
                sp.dma_start(out[b].rearrange("(i p) n -> p i n", p=P), h[:, :, :]).then_inc(stored.sem, 16)
            sp.wait_ge(stored.sem, stored.at(B, 0))

        @block.gpsimd
        def _(pool):
            for s in (decay_ready, scan_ready, route_mm, read_out, y_added, drive_ready, c_rows_out,
                      routed, stored, qk_turned, *parts_out, *placed):
                pool.sem_inc(s.sem, s.start)
            pool.memset(xT[:, :, 0:1], 0.0).then_inc(preset.sem, 1)
            pool.memset(xT[:, :, S + 1:S + 2], 0.0).then_inc(preset.sem, 1)
            pool.memset(ones_row[:, :], 1.0).then_inc(preset.sem, 1)
            pool.memset(ones_bf[:, :], 1.0).then_inc(preset.sem, 1)
            pool.memset(bias[:, :, :], 0.0).then_inc(preset.sem, 1)
            pool.memset(rms_eps[:, :], RMS_EPS).then_inc(preset.sem, 1)
            pool.memset(ln_eps[:, :], LN_EPS).then_inc(preset.sem, 1)
            pool.memset(beats[:, :, :, :], 0.0).then_inc(preset.sem, 1)

            pool.wait_ge(prep_dve.sem, PREP_DVE)
            pool.memset(ids[:, :, 0:TAPS - 1], -1).then_inc(ids_clear.sem, 1)
            with pool.Fori(0, B) as b:
                for c in (2, 3):
                    pool.wait_ge(delta_ready.sem, delta_ready.at(b, c + 1))
                    nc.gpsimd.tensor_tensor(du[:, c, :], delta[:, c, :], u[:, c, :], ALU.mult).then_inc(du_rest.sem, 1)
                for q in range(2):
                    with pool.Fori(0, NS // 2) as m:
                        for k in range(2):
                            for j in range(2):
                                pool.wait_ge(c_rows_out.sem, c_rows_out.at(b, q * NS + k + 1) + m * 2)
                                pool.wait_ge(scan_ready.sem, scan_ready.at(b, PASS * q + 2 * k + j + 1) + m * 4)
                                nc.gpsimd.tensor_tensor(scan[:, 2 * k + j, :], scan[:, 2 * k + j, :], c_rows[:, k, :],
                                                        ALU.mult).then_inc(read_out.sem, 1)
                pool.wait_ge(mix_mm.sem, mix_mm.at(b, NT // 2))
                alone(pool)
                for r in range(2):
                    pool.memset(stack[r][1][STACK:STACK + SHIFT, :, :], 1.0).then_inc(att_set.sem, 1)
                    pool.wait_ge(att_set.sem, att_set.at(b, r + 1))
                    alone(pool)
                for s in range(STEPS):
                    e, p = s // (NT // 2), s % (NT // 2)
                    tiles = slice(2 * p, 2 * p + 2)
                    pool.wait_ge(out_norm.sem, out_norm.at(b, s + 1))
                    nc.gpsimd.tensor_tensor(z2[:, s % 2, :, :], z2[:, s % 2, :, :],
                                            g2[:, e, :].unsqueeze(1).to_broadcast([P, 2, D]),
                                            ALU.mult).then_inc(out_scaled.sem, 1)
                    if e == 0:
                        pool.wait_ge(be_added.sem, be_added.at(b, p + 1))
                    else:
                        pool.wait_ge(out_added.sem, out_added.at(b, s - 3))
                    pool.wait_ge(out_scaled.sem, out_scaled.at(b, s + 1))
                    nc.gpsimd.tensor_tensor(h[:, tiles, :], h[:, tiles, :], z2[:, s % 2, :, :],
                                            ALU.add).then_inc(out_added.sem, 1)
                pool.wait_ge(out_mm.sem, out_mm.at(b, STEPS))
                pool.wait_ge(out_added.sem, out_added.at(b, STEPS))
                alone(pool)
                pool.memset(v_ext[:, :, :], 1.0).then_inc(att_set.sem, 1)
                pool.wait_ge(att_set.sem, att_set.at(b, 3))
                for n in range(4):
                    pool.wait_ge(part_mid.sem, part_mid.at(b, n + 1))
                    if n >= 2:
                        pool.wait_ge(parts_out[n - 2].sem, parts_out[n - 2].at(b, 16))
                    nc.gpsimd.tensor_tensor(parts[:, n % 2, 2, :], plain[:, n % 2, :], parts[:, n % 2, 1, :],
                                            ALU.subtract).then_inc(part_low.sem, 1)
                for n in range(2, 4):
                    pool.wait_ge(parts_out[n].sem, parts_out[n].at(b, 16))
                alone(pool)
                pool.memset(stack[2][1][STACK:STACK + SHIFT, :, :], 1.0).then_inc(att_set.sem, 1)
                pool.wait_ge(qk_turned.sem, qk_turned.at(b, 8))
                pool.wait_ge(att_set.sem, att_set.at(b, 4))
                alone(pool)
                pool.memset(ids[:, :, 0:TAPS - 1], -1).then_inc(ids_clear.sem, 1)

        @block.scalar
        def _(act):
            act.wait_ge(weights_in.sem, ALL_IN)
            nc.scalar.activation(neg_a[:, :, :], a_log, ACT.Exp).then_inc(prep_act.sem, 1)
            nc.scalar.activation(sign_T, sigs_T, ACT.Sign).then_inc(prep_act.sem, 1)
            for n in range(K3 * DC):
                act.wait_ge(prep_mm.sem, n + 1)
                nc.scalar.activation(conv_in[:, n // DC, n % DC, :], ps[:, n % 4, :],
                                     ACT.Copy).then_inc(prep_act.sem, 1)

            def copy_turned(b, k, p):
                act.wait_ge(ln_turned.sem, ln_turned.at(b, k * 4 + p + 1))
                nc.scalar.activation(xT[:, :, 1 + 2 * P * p:1 + 2 * P * (p + 1)],
                                     ps[:, 6 + p % 2, :].rearrange("p (c s) -> p c s", c=DC),
                                     ACT.Copy).then_inc(xT_ready.sem, 1)

            def root(dst, src, scale, eps, done):
                nc.scalar.activation(dst, src, ACT.Sqrt, bias=eps[:, 0:1], scale=scale).then_inc(done.sem, 1)

            def norm_root(b, norm, p):
                tiles = slice(2 * p, 2 * p + 2)
                act.wait_ge(ln_stats.sem, ln_stats.at(b, norm * NT // 2 + p + 1))
                root(deviation[:, tiles], mv[:, tiles, 1], 1.0, ln_eps, ln_dev)

            def norm_and_turn(b, norm, k, begun=0):
                for kind, p in (("root", 0), ("root", 1), ("root", 2), ("copy", 0), ("root", 3), ("copy", 1),
                                ("copy", 2), ("copy", 3))[begun:]:
                    if kind == "root":
                        norm_root(b, norm, p)
                    else:
                        copy_turned(b, k, p)

            act.wait_ge(prep_dve.sem, PREP_DVE)
            with act.Fori(0, B) as b:
                for i in range(NT):
                    act.wait_ge(tok_sum.sem, tok_sum.at(b, i + 1))
                    nc.scalar.activation(squares[:, i, :], xn[:, i, :], ACT.Square,
                                         accum_out=square_sum[:, i:i + 1]).then_inc(tok_sq.sem, 1)
                    if i % 2:
                        act.wait_ge(tok_sq.sem, tok_sq.at(b, i + 1))
                        alone(act)
                        root(tok_rms[:, i - 1:i + 1], square_sum[:, i - 1:i + 1], 1.0 / D, rms_eps, tok_root)
                norm_and_turn(b, 0, 0)
                for n, (c, half) in enumerate(U_ORDER):
                    act.wait_ge(u_mm.sem, u_mm.at(b, n + 1))
                    nc.scalar.activation(u[:, c, half * HALF:(half + 1) * HALF], ps[:, n % 4, :], ACT.Silu,
                                         bias=u_bias[:, c:c + 1]).then_inc(u_ready.sem, 1)
                    if half:
                        act.wait_ge(u_ready.sem, u_ready.at(b, n + 1))
                        alone(act)
                        nc.scalar.activation(y[:, c, :], u[:, c, :], ACT.Identity,
                                             scale=d_skip[:, c:c + 1]).then_inc(y_init.sem, 1)
                for chunks in ((0, 1), (2,), (3,)):
                    for c in chunks:
                        for half in range(NH):
                            n = c * NH + half
                            act.wait_ge(dt_mm.sem, dt_mm.at(b, n + 1))
                            nc.scalar.activation(delta[:, c, half * HALF:(half + 1) * HALF], ps[:, n % 4, :], ACT.Abs,
                                                 bias=dt_b[:, c:c + 1]).then_inc(dt_abs.sem, 1)
                    for c in chunks:
                        act.wait_ge(dt_abs.sem, dt_abs.at(b, NH * (c + 1)))
                        alone(act)
                        nc.scalar.activation(delta[:, c, :], delta[:, c, :], ACT.Exp,
                                             scale=-1.0).then_inc(sp_exp.sem, 1)
                    for c in chunks:
                        act.wait_ge(sp_exp.sem, sp_exp.at(b, c + 1))
                        nc.scalar.activation(delta[:, c, :], delta[:, c, :], ACT.Ln,
                                             bias=1.0).then_inc(sp_ln.sem, 1)
                act.wait_ge(bc_split.sem, bc_split.at(b, 1))
                act.wait_ge(delta_ready.sem, delta_ready.at(b, EC))
                act.wait_ge(y_init.sem, y_init.at(b, EC))
                alone(act)

                def state_pair(q, m):
                    for k in range(2):
                        states = m * 2 + k
                        for j in range(2):
                            act.wait_ge(scan_ready.sem, scan_ready.at(b, PASS * q + 2 * k + j - 3) + m * 4)
                            alone(act)
                            c = 2 * q + j
                            nc.scalar.activation(decay[:, 2 * k + j, :], delta[:, c, :], ACT.Exp,
                                                 scale=neg_a[:, states, c:c + 1]).then_inc(decay_ready.sem, 1)
                        if q == 0:
                            act.wait_ge(du_ready.sem, du_ready.at(b, 2))
                            act.wait_ge(du_rest.sem, du_rest.at(b, 2))
                        act.wait_ge(c_rows_mm.sem, c_rows_mm.at(b, q * NS + k + 1) + m * 2)
                        act.wait_ge(read_out.sem, read_out.at(b, PASS * q + 2 * k - 2) + m * 4)
                        nc.scalar.activation(c_rows[:, k, :], ps[:, 2:4, :].rearrange("p r s -> p (r s)"),
                                             ACT.Copy).then_inc(c_rows_out.sem, 1)

                for q in range(2):
                    with act.Fori(0, NS // 2) as m:
                        state_pair(q, m)
                norm_and_turn(b, 1, 1)
                for k in range(STEPS + 2):
                    if k < STEPS:
                        act.wait_ge(hid_stats.sem, hid_stats.at(b, k + 1))
                        root(exp_dev[:, 0, k % 2, :], exp_mv[:, 0, k % 2, :, 1], 1.0, ln_eps, hid_dev)
                    if k >= 2:
                        s = k - 2
                        act.wait_ge(out_stats.sem, out_stats.at(b, s + 1))
                        root(exp_dev[:, 1, s % 2, :], exp_mv[:, 1, s % 2, :, 1], 1.0, ln_eps, out_dev)
                    if 1 <= k <= STEPS:
                        s = k - 1
                        e = s // (NT // 2)
                        act.wait_ge(hid_turned.sem, hid_turned.at(b, s + 1))
                        if s >= 2:
                            act.wait_ge(out_mm.sem, out_mm.at(b, s - 1))
                        alone(act)
                        for c in range(DC):
                            last = nc.scalar.activation(hid_T[:, s % 2, c, :], ps[:, 6 + s % 2, c * 2 * P:(c + 1) * 2 * P],
                                                        ACT.Relu, bias=be1[:, e, c:c + 1], scale=g1[:, e, c:c + 1])
                        last.then_inc(hid_ready.sem, 1)
                    if k == 1:
                        act.wait_ge(gate_shift.sem, gate_shift.at(b, 1))
                        nc.scalar.activation(gate[:, :, :], gate[:, :, :], ACT.Exp).then_inc(gate_exp.sem, 1)
                    if k == 2:
                        act.wait_ge(gate_turned.sem, gate_turned.at(b, 1))
                        nc.scalar.activation(gate_T, ps[0:NE, 4:6, :].rearrange("p r s -> p (r s)"),
                                             ACT.Copy).then_inc(gate_T_ready.sem, 1)
                    if k >= STEPS:
                        norm_root(b, 2, k - STEPS)
                norm_and_turn(b, 2, 2, begun=2)
                for n in range(4):
                    act.wait_ge(qk_sum.sem, qk_sum.at(b, n + 1))
                    if n >= 2:
                        act.wait_ge(parts_out[n - 2].sem, parts_out[n - 2].at(b, 16))
                    nc.scalar.activation(parts[:, n % 2, 0, :], plain[:, n % 2, :], ACT.Copy)\
                        .then_inc(part_high.sem, 1)
                    act.wait_ge(part_rest.sem, part_rest.at(b, n + 1))
                    nc.scalar.activation(parts[:, n % 2, 1, :], plain[:, n % 2, :], ACT.Copy)\
                        .then_inc(part_mid.sem, 1)
                act.wait_ge(part_low.sem, part_low.at(b, 4))
                for g in range(QUADS):
                    for k, (i, t0, cols, diag, heads) in enumerate(PROB_UNITS):
                        n = g * UNITS + k
                        act.wait_ge(score_mm.sem, score_mm.at(b, n + 1))
                        if n >= PROBS:
                            act.wait_ge(pv_done.sem, pv_done.at(b, n + 1 - PROBS))
                        nc.scalar.activation(probs_view(n % PROBS, cols, heads),
                                             heads_view(2 + 2 * (n % SLOTS), cols, heads),
                                             ACT.Exp, scale=float(DH) ** -0.5).then_inc(prob_ready.sem, 1)
                        if k + 1 in (HALF_UNITS + 2, UNITS):
                            done = int(k + 1 == UNITS)
                            act.wait_ge(pv_done.sem, pv_done.at(b, g * UNITS + (UNITS if done else HALF_UNITS)))
                            if g > 0:
                                act.wait_ge(side_mm.sem, side_mm.at(b, SIDE["y", g - 1, done] + 1))
                            nc.scalar.activation(y_sum[:, done, :], ps[:, 6 + done, :],
                                                 ACT.Copy).then_inc(y_copied.sem, 1)
                for p in range(NT // 2):
                    copy_turned(b, 3, p)
                norm_and_turn(b, 3, 4)

        @block.tensor
        def _(pe):
            mm = nc.tensor.matmul
            pe.wait_ge(weights_in.sem, ALL_IN)
            pe.wait_ge(preset.sem, 8)
            for n in range(K3 * DC):
                k, c = n // DC, n % DC
                if n >= 4:
                    pe.wait_ge(prep_act.sem, 2 + n - 3)
                for e in range(EC):
                    last = mm(ps[:, n % 4, :], conv_in_w[:, e, k, c * P:(c + 1) * P], in_w[:, e, :],
                              start=(e == 0), stop=(e == EC - 1))
                last.then_inc(prep_mm.sem, 1)
            for f in range(EC):
                for e in range(EC):
                    last = mm(ps[:, 6, f:f + 1], in_w[:, e, f * P:(f + 1) * P], conv_b[:, e:e + 1],
                              start=(e == 0), stop=(e == EC - 1))
            last.then_inc(prep_mm.sem, 1)
            for j in range(TAPS):
                for c in range(DC):
                    last = mm(ps[(j % 2) * VOCAB:(j % 2 + 1) * VOCAB, 4 + j // 2, :], emb_T[:, c, :],
                              tok_w[:, c, j, :], start=(c == 0), stop=(c == DC - 1))
            last.then_inc(prep_mm.sem, 1)
            pe.wait_ge(prep_act.sem, 2)
            for i in range(NT):
                last = mm(ps[:, 7, i * TILES:(i + 1) * TILES], pe_full[:, i * P:(i + 1) * P], sign_T,
                          start=True, stop=True)
            last.then_inc(prep_mm.sem, 1)
            pe.wait_ge(prep_dve.sem, PREP_ROUTE)
            pe.wait_ge(prep_act.sem, 2 + K3 * DC)
            for i in range(NT):
                last = nc.tensor.transpose(ps[0:TILES, i // 4, (i % 4) * P:(i % 4 + 1) * P], route[:, i, :],
                                           ident[:, :])
            last.then_inc(prep_mm.sem, 1)
            pe.wait_ge(prep_dve.sem, PREP_ROUTE + 1)
            for i in range(NT):
                last = mm(tile_bank(i), route_T[:, i * P:(i + 1) * P], b_tiles, start=True, stop=True)
            last.then_inc(prep_mm.sem, 1)
            pe.wait_ge(prep_dve.sem, PREP_DVE)

            def turn(b, k, norm, pairs=range(NT // 2)):
                for p in pairs:
                    if norm is not None:
                        pe.wait_ge(ln_norm.sem, ln_norm.at(b, norm * NT + 2 * p + 2))
                    if p >= 2:
                        pe.wait_ge(xT_ready.sem, xT_ready.at(b, k * 4 + p - 1))
                    for c in range(DC):
                        for r in range(2):
                            last = nc.tensor.transpose(ps[:, 6 + p % 2, (2 * c + r) * P:(2 * c + r + 1) * P],
                                                       xn[:, 2 * p + r, c * P:(c + 1) * P], ident[:, :])
                    last.then_inc(ln_turned.sem, 1)

            with pe.Fori(0, B) as b:
                pe.wait_ge(routed.sem, routed.at(b, -1))
                alone(pe)
                pe.wait_ge(onehot_done.sem, onehot_done.at(b, 2))
                for i in range(NT):
                    if i >= 2:
                        pe.wait_ge(tok_rot.sem, tok_rot.at(b, i - 1))
                    n = 0
                    for c in range(2):
                        for part in range(3):
                            last = mm(ps[:, i % 2, :], onehot[:, c, i * P:(i + 1) * P], table[:, part, c, :],
                                      start=(n == 0), stop=(n == 5))
                            n += 1
                    last.then_inc(tok_mm.sem, 1)
                turn(b, 0, 0, pairs=range(3))
                pe.wait_ge(xT_ready.sem, xT_ready.at(b, 3))
                alone(pe)
                for n, (f, half) in enumerate(U_ORDER):
                    if n == 2:
                        pe.wait_ge(xT_ready.sem, xT_ready.at(b, 4))
                    if n == 1:
                        turn(b, 0, 0, pairs=(3,))
                    if n >= 4:
                        pe.wait_ge(u_ready.sem, u_ready.at(b, n - 3))
                    for m in range(K3 * DC):
                        k, c = m // DC, m % DC
                        last = mm(ps[:, n % 4, :], conv_in[:, k, c, f * P:(f + 1) * P],
                                  xT[:, c, half * HALF + k:half * HALF + k + HALF],
                                  start=(m == 0), stop=(m == K3 * DC - 1))
                    last.then_inc(u_mm.sem, 1)
                pe.wait_ge(u_ready.sem, u_ready.at(b, EC * NH))
                for half in range(NH):
                    for e in range(EC):
                        last = mm(ps[0:2 * NS, 4 + half, :], bc_w[:, e, :],
                                  u[:, e, half * HALF:(half + 1) * HALF], start=(e == 0), stop=(e == EC - 1))
                last.then_inc(bc_mm.sem, 1)
                for n in range(EC * NH):
                    f, half = n // NH, n % NH
                    if n >= 4:
                        pe.wait_ge(dt_abs.sem, dt_abs.at(b, n - 3))
                        pe.wait_ge(dt_relu.sem, dt_relu.at(b, n - 3))
                    for e in range(EC):
                        last = mm(ps[:, n % 4, :], dt_w[:, e, f * P:(f + 1) * P],
                                  u[:, e, half * HALF:(half + 1) * HALF], start=(e == 0), stop=(e == EC - 1))
                    last.then_inc(dt_mm.sem, 1)
                pe.wait_ge(bc_split.sem, bc_split.at(b, 1))
                pe.wait_ge(dt_abs.sem, dt_abs.at(b, EC * NH))
                pe.wait_ge(dt_relu.sem, dt_relu.at(b, EC * NH))
                alone(pe)

                def state_rows(q, m, k):
                    states = m * 2 + k
                    pe.wait_ge(drive_ready.sem, drive_ready.at(b, PASS * q + 2 * k) + m * 4)
                    for half in range(NH):
                        last = mm(ps[:, half, :], pick_state[:, states, :],
                                  bc_parts[:, half * HALF:(half + 1) * HALF], start=True, stop=True)
                    last.then_inc(b_rows_mm.sem, 1)
                    pe.wait_ge(c_rows_out.sem, c_rows_out.at(b, q * NS + k) + m * 2)
                    for half in range(NH):
                        last = mm(ps[:, 2 + half, :], pick_state[:, states + NS, :],
                                  bc_parts[:, half * HALF:(half + 1) * HALF], start=True, stop=True)
                    last.then_inc(c_rows_mm.sem, 1)

                def add_shares(q, m, k, start=False, stop=False):
                    for j in range(2):
                        pe.wait_ge(read_out.sem, read_out.at(b, PASS * q + 2 * k + j + 1) + m * 4)
                        alone(pe)
                        for half in range(NH):
                            last = mm(ps[:, 4 + 2 * j + half, :], ident[:, :],
                                      scan[:, 2 * k + j, half * HALF:(half + 1) * HALF], start=start, stop=stop)
                        last.then_inc(y_added.sem, 1)

                for q in range(2):
                    for k in range(2):
                        state_rows(q, 0, k)
                        if q == 1:
                            add_shares(0, NS // 2 - 1, k, stop=(k == 1))
                    if q == 1:
                        pe.wait_ge(y_out.sem, y_out.at(b, 2))
                    for k in range(2):
                        state_rows(q, 1, k)
                        add_shares(q, 0, k, start=(k == 0))
                    with pe.Fori(2, NS // 2) as m:
                        for k in range(2):
                            state_rows(q, m, k)
                            add_shares(q, m - 1, k)
                pe.wait_ge(drive_ready.sem, drive_ready.at(b, NS * EC))
                pe.wait_ge(c_rows_out.sem, c_rows_out.at(b, 2 * NS))
                alone(pe)
                for p in range(NT // 2):
                    mm(ps[:, p, :], ones_bf[:, :], bias[:, 2 * NE, :].unsqueeze(1).to_broadcast([BIAS_ROWS, 2, D]),
                       start=True, stop=False)
                for e in range(EC):
                    if e == 2:
                        for k in range(2):
                            add_shares(1, NS // 2 - 1, k, stop=(k == 1))
                    if e >= 2:
                        pe.wait_ge(y_out.sem, y_out.at(b, e + 1))
                    for i in range(NT):
                        last = mm(tile_bank(i), y[:, e, i * P:(i + 1) * P], out_w[:, e, :], start=False,
                                  stop=(e == EC - 1 and i % 2 == 1))
                        if e == EC - 1 and i % 2:
                            last.then_inc(mix_mm.sem, 1)
                turn(b, 1, 1)
                pe.wait_ge(moe_w_in.sem, moe_w_in.at(b, 16))
                for k in range(STEPS + 2):
                    if k < STEPS:
                        e, p = k // (NT // 2), k % (NT // 2)
                        if e == 0:
                            pe.wait_ge(xT_ready.sem, xT_ready.at(b, 4 + p + 1))
                        if k >= 2:
                            pe.wait_ge(hid_norm.sem, hid_norm.at(b, k - 1))
                        mm(ps[:, k % 2, :], ones_bf[:, :], bias[:, e, :].unsqueeze(1).to_broadcast([BIAS_ROWS, 2, D]),
                           start=True, stop=False)
                        for r in range(2):
                            for c in range(DC):
                                last = mm(ps[:, k % 2, r * D:(r + 1) * D], xT[:, c, span(2 * p + r)],
                                          w_moe[:, 0, e, c, :], start=False, stop=(r == 1 and c == DC - 1))
                        last.then_inc(hid_mm.sem, 1)
                    if k == 1:
                        pe.wait_ge(xT_ready.sem, xT_ready.at(b, 8))
                        for i in range(NT):
                            for c in range(DC):
                                mm(ps[:, 4, i * NE:(i + 1) * NE], xT[:, c, span(i)], gate_w[:, c, :],
                                   start=(c == 0), stop=False)
                            last = mm(ps[:, 4, i * NE:(i + 1) * NE], ones_row[:, :], gate_b[:, :],
                                      start=False, stop=True)
                        last.then_inc(gate_mm.sem, 1)
                    if k >= 2:
                        s = k - 2
                        e = s // (NT // 2)
                        pe.wait_ge(hid_ready.sem, hid_ready.at(b, s + 1))
                        if s >= 2:
                            pe.wait_ge(out_norm.sem, out_norm.at(b, s - 1))
                        mm(ps[:, 2 + s % 2, :], ones_bf[:, :],
                           bias[:, NE + e, :].unsqueeze(1).to_broadcast([BIAS_ROWS, 2, D]), start=True, stop=False)
                        for r in range(2):
                            for c in range(DC):
                                last = mm(ps[:, 2 + s % 2, r * D:(r + 1) * D], hid_T[:, s % 2, c, r * P:(r + 1) * P],
                                          w_moe[:, 1, e, c, :], start=False, stop=(r == 1 and c == DC - 1))
                        last.then_inc(out_mm.sem, 1)
                    if 1 <= k <= STEPS:
                        s = k - 1
                        pe.wait_ge(hid_norm.sem, hid_norm.at(b, s + 1))
                        if s >= 2:
                            pe.wait_ge(hid_ready.sem, hid_ready.at(b, s - 1))
                        for c in range(DC):
                            for r in range(2):
                                last = nc.tensor.transpose(ps[:, 6 + s % 2, (2 * c + r) * P:(2 * c + r + 1) * P],
                                                           z1[:, s % 2, r, c * P:(c + 1) * P], ident[:, :])
                        last.then_inc(hid_turned.sem, 1)
                    if k == 2:
                        pe.wait_ge(gate_ready.sem, gate_ready.at(b, 1))
                        for i in range(NT):
                            last = nc.tensor.transpose(ps[0:NE, 4 + i // 4, (i % 4) * P:(i % 4 + 1) * P],
                                                       gate[:, i, :], ident[:, :])
                        last.then_inc(gate_turned.sem, 1)
                    if 3 <= k < 3 + NT // 2:
                        p = k - 3
                        pe.wait_ge(gate_T_ready.sem, gate_T_ready.at(b, 1))
                        if p >= 2:
                            pe.wait_ge(be_added.sem, be_added.at(b, p - 1))
                        for r in range(2):
                            last = mm(ps[:, 4 + p % 2, r * D:(r + 1) * D],
                                      gate_T[:, (2 * p + r) * P:(2 * p + r + 1) * P], be2[:, :], start=True, stop=True)
                        last.then_inc(be_mm.sem, 1)
                turn(b, 2, 2, pairs=range(2))
                pe.wait_ge(att_in.sem, att_in.at(b, 48))
                pe.wait_ge(xT_ready.sem, xT_ready.at(b, 10))
                alone(pe)
                def project(n, bank, before):
                    if before:
                        pe.wait_ge(qk_turned.sem, qk_turned.at(b, before))
                    for half, swap in ((0, 0), (0, 1), (1, 0), (1, 1)):
                        if n == 0 and half == 1 and swap == 0:
                            turn(b, 2, 2, pairs=range(2, 4))
                            pe.wait_ge(xT_ready.sem, xT_ready.at(b, 12))
                        for c in range(DC):
                            last = mm(ps[:, bank + 2 * swap + half, :], w_qk[:, c, 2 * n + swap, :],
                                      xT[:, c, 1 + half * HALF:1 + (half + 1) * HALF],
                                      start=(c == 0), stop=(c == DC - 1))
                    last.then_inc(qk_mm.sem, 1)

                project(0, 0, 0)
                project(1, 4, 0)
                pe.wait_ge(qk_turned.sem, qk_turned.at(b, 2))
                for i in range(NT):
                    for c in range(DC):
                        last = mm(tile_bank(i), xT[:, c, span(i)], w_v[:, c, :], start=(c == 0),
                                  stop=(c == DC - 1))
                last.then_inc(v_mm.sem, 1)
                project(2, 4, 4)
                pe.wait_ge(v_ready.sem, v_ready.at(b, 1))
                project(3, 0, 6)
                pe.wait_ge(qk_turned.sem, qk_turned.at(b, 8))

                def side_unit(kind, g, k):
                    at = SIDE[kind, g, k]
                    bank = side_bank(at)
                    if at >= RAW:
                        pe.wait_ge(side_read.sem, side_read.at(b, at - 1))
                    elif at >= 4:
                        pe.wait_ge(side_read.sem, side_read.at(b, at - 3))
                    if kind == "raw":
                        i, s0, cols, diag, heads = MAX_UNITS[k]
                        q, key = stack[g % STACKS]
                        if k == 0:
                            pe.wait_ge(placed[g].sem, placed[g].at(b, 16 * PLACEMENTS))
                        view = raw_view(bank, cols, heads)
                        for jj, j in enumerate(heads):
                            last = mm(view[:, jj, :], q[0:STACK, j, i * P:(i + 1) * P],
                                      key[0:STACK, j, s0:s0 + cols], start=True, stop=not diag)
                            if diag:
                                last = mm(view[:, jj, cols - P:cols], ident_bf[:, :], mask_rows[:, :],
                                          start=False, stop=True)
                    elif kind == "rows":
                        pe.wait_ge(max_ready.sem, max_ready.at(b, g + 1))
                        row_bank = ps[0:4 * SHIFT, bank, :].bitcast(BF16)
                        for i in range(NT):
                            last = nc.tensor.transpose(row_bank[:, i * P:(i + 1) * P],
                                                       max_parts[:, i, :, :].rearrange("p j t -> p (j t)"),
                                                       ident_bf[:, :])
                    else:
                        pe.wait_ge(y_copied.sem, y_copied.at(b, NH * g + k + 1))
                        for i in range(NT // NH):
                            last = nc.tensor.transpose(ps[:, bank, i * P:(i + 1) * P],
                                                       y_sum[:, k, i * P:(i + 1) * P], ident[:, :])
                    last.then_inc(side_mm.sem, 1)

                for unit in FIRST:
                    side_unit(*unit)
                for g in range(QUADS):
                    q, key = stack[g % STACKS]
                    for n in range(UNITS + LAG):
                        if n < UNITS:
                            i, t0, cols, diag, heads = PROB_UNITS[n]
                            if n == 0:
                                pe.wait_ge(rows_placed[g].sem, rows_placed[g].at(b, 16 * 4))
                                if g == 2:
                                    pe.wait_ge(att_set.sem, att_set.at(b, 4))
                            if g * UNITS + n >= SLOTS:
                                pe.wait_ge(prob_ready.sem, prob_ready.at(b, g * UNITS + n + 1 - SLOTS))
                            view = heads_view(2 + 2 * ((g * UNITS + n) % SLOTS), cols, heads)
                            for jj, j in enumerate(heads):
                                last = mm(view[:, jj, :], key[0:STACK + SHIFT, j, i * P:(i + 1) * P],
                                          q[0:STACK + SHIFT, j, t0:t0 + cols], start=True, stop=not diag)
                                if diag:
                                    last = mm(view[:, jj, 0:P], ident_bf[:, :], mask_cols[:, :],
                                              start=False, stop=True)
                            last.then_inc(score_mm.sem, 1)
                        if n >= LAG:
                            i, t0, cols, diag, heads = PROB_UNITS[n - LAG]
                            half = t0 // HALF
                            at = g * UNITS + n - LAG
                            pe.wait_ge(prob_ready.sem, prob_ready.at(b, at + 1))
                            if i == 0 and g > 0:
                                pe.wait_ge(y_copied.sem, y_copied.at(b, NH * (g - 1) + half + 1))
                            weights = probs_view(at % PROBS, cols, heads)
                            for jj, j in enumerate(heads):
                                v0 = (DH + 1) * (4 * g + j)
                                last = mm(ps[32 * j:32 * j + 32, 6 + half, t0 - half * HALF:HALF],
                                          v_ext[:, i, v0:v0 + 32], weights[:, jj, :],
                                          start=(i == 0), stop=(i == (half + 1) * (NT // NH) - 1))
                            last.then_inc(pv_done.sem, 1)
                        for unit in PLANS[g][n]:
                            side_unit(*unit)
                for unit in LAST:
                    side_unit(*unit)
                pe.wait_ge(side_read.sem, side_read.at(b, len(SIDE)))
                turn(b, 3, None)
                pe.wait_ge(xT_ready.sem, xT_ready.at(b, 16))
                for i in range(NT):
                    for c in range(DC):
                        last = mm(tile_bank(i), xT[:, c, span(i)], w_o[:, c, :], start=(c == 0), stop=(c == DC - 1))
                    if i % 2:
                        last.then_inc(wo_mm.sem, 1)
                turn(b, 4, 3)
                pe.wait_ge(xT_ready.sem, xT_ready.at(b, 20))
                pe.wait_ge(route_w_in.sem, route_w_in.at(b, 16))
                alone(pe)
                with pe.Fori(0, TILES // 2) as m:
                    for k in range(2):
                        pe.wait_ge(routed.sem, routed.at(b, k - 1) + m * 2)
                        for i in range(NT):
                            for c in range(DC):
                                last = mm(ps[:, 4 * k + i // 2, (i % 2) * D:(i % 2 + 1) * D], xT[:, c, span(i)],
                                          w_route[:, m * 2 + k, c, :], start=(c == 0), stop=(c == DC - 1))
                        last.then_inc(route_mm.sem, 1)

        @block.vector
        def _(dve):
            tt, ts = nc.vector.tensor_tensor, nc.vector.tensor_scalar
            own = Chain(dve, prep_dve, 0)
            dve.wait_ge(weights_in.sem, ALL_IN)
            dve.wait_ge(preset.sem, 8)
            dve.wait_ge(prep_act.sem, 1)
            own.step(ts(neg_a[:, :, :], neg_a[:, :, :], -1.0, None, ALU.mult))
            dve.wait_ge(prep_mm.sem, K3 * DC + 3)
            pos_scores = ps[:, 7, 0:NT * TILES].rearrange("p (i t) -> p i t", t=TILES)
            own.step(nc.vector.tensor_reduce(best, pos_scores, AX_X, ALU.max))
            own.step(nc.vector.memset(taken, 0.0))
            own.settle()
            own.step(tt(is_best, pos_scores, best.unsqueeze(2).to_broadcast([P, NT, TILES]), ALU.is_ge))
            own.settle()
            for t in range(TILES):
                own.step(tt(route[:, :, t], is_best[:, :, t], taken, ALU.is_gt))
                own.settle()
                own.step(tt(taken, taken, is_best[:, :, t], ALU.max))
                own.settle()
            assert own.n == PREP_ROUTE, own.n
            dve.wait_ge(prep_mm.sem, K3 * DC + 4)
            own.step(nc.vector.tensor_copy(route_T, ps[0:TILES, 0:2, :].rearrange("p r s -> p (r s)")))
            dve.wait_ge(prep_mm.sem, K3 * DC + 5)
            own.step(nc.vector.tensor_copy(route_b[:, :, :].rearrange("p i n -> p (i n)"),
                                           ps[:, 0:4, :].rearrange("p r s -> p (r s)")))
            own.step(tt(u_bias[:, :], ps[:, 6, 0:EC], in_b[:, :], ALU.add))
            own.step(nc.vector.tensor_copy(table_f, ps[:, 4:6, :].rearrange("p r s -> p (r s)")))
            own.settle()
            last_tap = table_f[VOCAB:P, 2 * D:4 * D]
            own.step(tt(last_tap, last_tap, emb_rows[VOCAB:P, :], ALU.add))
            own.settle()
            own.step(tt(last_tap, last_tap, tok_b[VOCAB:P, :], ALU.add))
            own.settle()
            src = table_f
            for part in range(3):
                dst = table[:, part, :, :].rearrange("p c n -> p (c n)")
                own.step(nc.vector.tensor_copy(dst, src))
                own.settle()
                if part < 2:
                    own.step(tt(table_r, src, dst, ALU.subtract))
                    own.settle()
                    src = table_r
            for part in range(3):
                row = slice(32 * part, 32 * part + 1)
                own.step(nc.vector.tensor_copy(bias_part, bias_f))
                own.settle()
                own.step(nc.vector.tensor_copy(bias[row, :, :], bias_part[row, :, :]))
                if part < 2:
                    own.step(tt(bias_f, bias_f, bias_part, ALU.subtract))
                own.settle()
            assert own.n == PREP_DVE, own.n

            def layer_norm_phase(b, k, prepare, p):
                if p < NT // 2:
                    prepare(p)
                    dve.drain()
                    for i in (2 * p, 2 * p + 1):
                        nc.vector.bn_stats(stats[:, i, :], h[:, i, :])
                    dve.drain()
                    for i in (2 * p, 2 * p + 1):
                        last = nc.vector.bn_aggr(mv[:, i, :], stats[:, i, :])
                    last.then_inc(ln_stats.sem, 1)
                if p > 0:
                    pair = slice(2 * p - 2, 2 * p)
                    dve.wait_ge(ln_dev.sem, ln_dev.at(b, k * NT // 2 + p))
                    nc.vector.reciprocal(rstd[:, pair], deviation[:, pair]).then_inc(ln_rstd.sem, 1)
                    dve.wait_ge(ln_rstd.sem, ln_rstd.at(b, k * NT // 2 + p))
                    for i in (2 * p - 2, 2 * p - 1):
                        ts(xn[:, i, :], h[:, i, :], mv[:, i, 0:1], rstd[:, i:i + 1], ALU.subtract,
                           ALU.mult).then_inc(ln_norm.sem, 1)

            def layer_norm(b, k, prepare):
                for p in range(NT // 2 + 1):
                    layer_norm_phase(b, k, prepare, p)

            all_h = h[:, :, :].rearrange("p i n -> p (i n)")

            def match_words(b):
                dve.wait_ge(ids_in.sem, ids_in.at(b, 16 * TAPS))
                for c in range(2):
                    ts(onehot[:, c, :], ids[:, c, :], vocab_col[:, 0:1], None, ALU.is_equal)\
                        .then_inc(onehot_done.sem, 1)

            match_words(0)
            with dve.Fori(0, B) as b:
                dve.wait_ge(trig_in.sem, trig_in.at(b, 16))
                for i in range(NT):
                    dve.wait_ge(tok_mm.sem, tok_mm.at(b, i + 1))
                    tt(rotated[:, i % 2, :], ps[:, i % 2, :], trig[:, i, :], ALU.mult).then_inc(tok_rot.sem, 1)
                    dve.wait_ge(tok_rot.sem, tok_rot.at(b, i + 1))
                    tt(xn[:, i, :], rotated[:, i % 2, 0:D], rotated[:, i % 2, D:2 * D],
                       ALU.add).then_inc(tok_sum.sem, 1)
                dve.wait_ge(stored.sem, stored.at(b, 0))
                alone(dve)

                def scale_tokens(p):
                    tiles = slice(2 * p, 2 * p + 2)
                    dve.wait_ge(tok_root.sem, tok_root.at(b, p + 1))
                    nc.vector.reciprocal(tok_scale[:, tiles], tok_rms[:, tiles]).then_inc(tok_rec.sem, 1)
                    dve.wait_ge(tok_rec.sem, tok_rec.at(b, p + 1))
                    for i in (2 * p, 2 * p + 1):
                        nc.vector.scalar_tensor_tensor(h[:, i, :], xn[:, i, :], tok_scale[:, i:i + 1], norm_w[:, :],
                                                       ALU.mult, ALU.mult)

                layer_norm(b, 0, scale_tokens)
                def finish_delta(c):
                    dve.wait_ge(sp_ln.sem, sp_ln.at(b, c + 1))
                    dve.wait_ge(dt_relu.sem, dt_relu.at(b, NH * (c + 1)))
                    tt(delta[:, c, :], delta[:, c, :], du[:, c, :], ALU.add).then_inc(delta_ready.sem, 1)
                    if c < 2:
                        dve.wait_ge(delta_ready.sem, delta_ready.at(b, c + 1))
                        tt(du[:, c, :], delta[:, c, :], u[:, c, :], ALU.mult).then_inc(du_ready.sem, 1)

                dve.wait_ge(bc_mm.sem, bc_mm.at(b, 1))
                ts(bc_full, ps[0:2 * NS, 4:6, :].rearrange("p r s -> p (r s)"), bc_b[:, 0:1], None, ALU.add)
                dve.drain()
                nc.vector.tensor_copy(bc_parts[0:2 * NS, :], bc_full)
                dve.drain()
                tt(bc_rest, bc_full, bc_parts[0:2 * NS, :], ALU.subtract)
                dve.drain()
                nc.vector.tensor_copy(bc_part[:, 0:S], bc_rest)
                dve.drain()
                nc.vector.tensor_copy(bc_parts[2 * NS:4 * NS, :], bc_part[:, 0:S])
                tt(bc_rest, bc_rest, bc_part[:, 0:S], ALU.subtract)
                dve.drain()
                nc.vector.tensor_copy(bc_parts[4 * NS:6 * NS, :], bc_rest).then_inc(bc_split.sem, 1)
                for c in range(EC):
                    for half in range(NH):
                        n = c * NH + half
                        dve.wait_ge(dt_abs.sem, dt_abs.at(b, n + 1))
                        ts(du[:, c, half * HALF:(half + 1) * HALF], ps[:, n % 4, :], dt_b[:, c:c + 1], 0.0, ALU.add,
                           ALU.max).then_inc(dt_relu.sem, 1)
                    if c < 2:
                        continue
                    finish_delta(c - 2)
                for c in (2, 3):
                    finish_delta(c)
                dve.wait_ge(du_ready.sem, du_ready.at(b, 2))
                dve.wait_ge(dt_mm.sem, dt_mm.at(b, EC * NH))
                dve.wait_ge(y_init.sem, y_init.at(b, EC))
                alone(dve)
                def state_pair(q, m):
                    for k in range(2):
                        dve.wait_ge(b_rows_mm.sem, b_rows_mm.at(b, q * NS + k + 1) + m * 2)
                        for j in range(2):
                            dve.wait_ge(scan_ready.sem, scan_ready.at(b, PASS * q + 2 * k + j - 1) + m * 4)
                            tt(drive[:, j, :], du[:, 2 * q + j, :], ps[:, 0:2, :].rearrange("p r s -> p (r s)"),
                               ALU.mult).then_inc(drive_ready.sem, 1)
                        for j in range(2):
                            at = PASS * q + 2 * k + j + 1
                            dve.wait_ge(y_added.sem, y_added.at(b, at - 4) + m * 4)
                            dve.wait_ge(decay_ready.sem, decay_ready.at(b, at) + m * 4)
                            dve.wait_ge(drive_ready.sem, drive_ready.at(b, at) + m * 4)
                            nc.vector.tensor_tensor_scan(scan[:, 2 * k + j, :], decay[:, 2 * k + j, :],
                                                         drive[:, j, :], 0.0, ALU.mult,
                                                         ALU.add).then_inc(scan_ready.sem, 1)

                def complete_y(q):
                    for j in range(2):
                        dve.wait_ge(y_added.sem, y_added.at(b, PASS * (q + 1) - 1 + j))
                        tt(y[:, 2 * q + j, :], y[:, 2 * q + j, :],
                           ps[:, 4 + 2 * j:6 + 2 * j, :].rearrange("p r s -> p (r s)"), ALU.add).then_inc(y_out.sem, 1)

                for q in range(2):
                    state_pair(q, 0)
                    if q == 1:
                        complete_y(0)
                    with dve.Fori(1, NS // 2) as m:
                        state_pair(q, m)
                complete_y(1)

                def add_product(made):
                    def add(p):
                        dve.wait_ge(made.sem, made.at(b, p + 1))
                        tt(all_h[:, p * HALF:(p + 1) * HALF], all_h[:, p * HALF:(p + 1) * HALF], ps[:, p, :], ALU.add)
                    return add

                layer_norm(b, 1, add_product(mix_mm))
                def statistics(layer, s, made, done):
                    dve.wait_ge(made.sem, made.at(b, s + 1))
                    for r in range(2):
                        nc.vector.bn_stats(exp_bn[:, layer, s % 2, r, :],
                                           ps[:, 2 * layer + s % 2, r * D:(r + 1) * D])
                    dve.drain()
                    for r in range(2):
                        last = nc.vector.bn_aggr(exp_mv[:, layer, s % 2, r, :], exp_bn[:, layer, s % 2, r, :])
                    last.then_inc(done.sem, 1)

                def normalise(layer, s, dst, done):
                    for r in range(2):
                        last = ts(dst[:, s % 2, r, :], ps[:, 2 * layer + s % 2, r * D:(r + 1) * D],
                                  exp_mv[:, layer, s % 2, r, 0:1], exp_rstd[:, layer, s % 2, r:r + 1],
                                  ALU.subtract, ALU.mult)
                    last.then_inc(done.sem, 1)

                def expert_stage(k):
                    s = k - 2
                    if k < STEPS:
                        statistics(0, k, hid_mm, hid_stats)
                    if s >= 0:
                        statistics(1, s, out_mm, out_stats)
                    if k < STEPS:
                        if k >= 2:
                            dve.wait_ge(hid_turned.sem, hid_turned.at(b, k - 1))
                        dve.wait_ge(hid_dev.sem, hid_dev.at(b, k + 1))
                        nc.vector.reciprocal(exp_rstd[:, 0, k % 2, :], exp_dev[:, 0, k % 2, :]).then_inc(hid_rstd.sem, 1)
                        dve.wait_ge(hid_rstd.sem, hid_rstd.at(b, k + 1))
                        normalise(0, k, z1, hid_norm)
                    if s >= 0:
                        dve.wait_ge(out_dev.sem, out_dev.at(b, s + 1))
                        nc.vector.reciprocal(exp_rstd[:, 1, s % 2, :], exp_dev[:, 1, s % 2, :]).then_inc(out_rstd.sem, 1)
                        dve.wait_ge(out_rstd.sem, out_rstd.at(b, s + 1))
                        tt(exp_rstd[:, 1, s % 2, :], exp_rstd[:, 1, s % 2, :],
                           gate[:, 2 * (s % 4):2 * (s % 4) + 2, s // (NT // 2)], ALU.mult).then_inc(out_gated.sem, 1)
                        if s >= 2:
                            dve.wait_ge(out_added.sem, out_added.at(b, s - 1))
                        dve.wait_ge(out_gated.sem, out_gated.at(b, s + 1))
                        normalise(1, s, z2, out_norm)

                all_xn = xn[:, :, :].rearrange("p i n -> p (i n)")
                dve.drain()
                tt(all_h, all_h, all_xn, ALU.add)
                expert_stage(0)
                expert_stage(1)
                dve.wait_ge(gate_mm.sem, gate_mm.at(b, 1))
                nc.vector.tensor_copy(scores4[:, :, :], ps[:, 4, 0:NT * NE].rearrange("p (i e) -> p i e", e=NE))
                dve.drain()
                nc.vector.tensor_reduce(top[:, :], scores4[:, :, :], AX_X, ALU.max)
                for e in range(NE):
                    if e > 0:
                        tt(beats[:, :, e, 0:e], scores4[:, :, 0:e],
                           scores4[:, :, e:e + 1].to_broadcast([P, NT, e]), ALU.is_ge)
                    if e < NE - 1:
                        tt(beats[:, :, e, e + 1:NE], scores4[:, :, e + 1:NE],
                           scores4[:, :, e:e + 1].to_broadcast([P, NT, NE - 1 - e]), ALU.is_gt)
                dve.drain()
                tt(gate[:, :, :], scores4[:, :, :], top[:, :].unsqueeze(2).to_broadcast([P, NT, NE]),
                   ALU.subtract).then_inc(gate_shift.sem, 1)
                nc.vector.tensor_reduce(rank[:, :, :], beats[:, :, :, :], AX_X, ALU.add)
                dve.drain()
                ts(rank[:, :, :], rank[:, :, :], 1.5, None, ALU.is_lt)
                dve.drain()
                dve.wait_ge(gate_exp.sem, gate_exp.at(b, 1))
                tt(gate[:, :, :], gate[:, :, :], rank[:, :, :], ALU.mult)
                dve.drain()
                nc.vector.tensor_reduce(top[:, :], gate[:, :, :], AX_X, ALU.add)
                dve.drain()
                nc.vector.reciprocal(top[:, :], top[:, :])
                dve.drain()
                tt(gate[:, :, :], gate[:, :, :], top[:, :].unsqueeze(2).to_broadcast([P, NT, NE]), ALU.mult)
                dve.drain().then_inc(gate_ready.sem, 1)
                def last_added(p):
                    dve.wait_ge(out_added.sem, out_added.at(b, STEPS - NT // 2 + p + 1))
                    alone(dve)

                for k in range(2, STEPS + 2):
                    expert_stage(k)
                    if 3 <= k < 3 + NT // 2:
                        p = k - 3
                        dve.wait_ge(be_mm.sem, be_mm.at(b, p + 1))
                        tt(all_h[:, p * HALF:(p + 1) * HALF], all_h[:, p * HALF:(p + 1) * HALF], ps[:, 4 + p % 2, :],
                           ALU.add).then_inc(be_added.sem, 1)
                    if k >= STEPS:
                        layer_norm_phase(b, 2, last_added, k - STEPS)
                for p in range(2, NT // 2 + 1):
                    layer_norm_phase(b, 2, last_added, p)

                for n in range(4):
                    dve.wait_ge(att_in.sem, att_in.at(b, 48))
                    dve.wait_ge(qk_mm.sem, qk_mm.at(b, n + 1))
                    if n >= 2:
                        dve.wait_ge(part_low.sem, part_low.at(b, n - 1))
                        dve.wait_ge(part_mid.sem, part_mid.at(b, n - 1))
                    for r, dst in enumerate((plain, swapped)):
                        bank = 4 * (n in (1, 2)) + 2 * r
                        tt(dst[:, n % 2, :], ps[:, bank:bank + 2, :].rearrange("p r s -> p (r s)"),
                           head_rot[:, r, :], ALU.mult).then_inc(qk_turned.sem, 1)
                    dve.wait_ge(qk_turned.sem, qk_turned.at(b, 2 * n + 2))
                    tt(plain[:, n % 2, :], plain[:, n % 2, :], swapped[:, n % 2, :],
                       ALU.add).then_inc(qk_sum.sem, 1)
                    dve.wait_ge(part_high.sem, part_high.at(b, n + 1))
                    tt(plain[:, n % 2, :], plain[:, n % 2, :], parts[:, n % 2, 0, :],
                       ALU.subtract).then_inc(part_rest.sem, 1)
                    if n == 1:
                        dve.wait_ge(v_mm.sem, v_mm.at(b, 1))
                        dve.wait_ge(att_set.sem, att_set.at(b, 3))
                        nc.vector.tensor_copy(
                            v_ext[:, :, 0:HEADS * (DH + 1)].rearrange("p i (h d) -> p i h d", h=HEADS)[:, :, :, 0:DH],
                            ps[:, 0:4, :].rearrange("p k (r h d) -> p (k r) h d", r=2, h=HEADS))\
                            .then_inc(v_ready.sem, 1)

                def side_unit(kind, g, k):
                    at = SIDE[kind, g, k]
                    bank = side_bank(at)
                    dve.wait_ge(side_mm.sem, side_mm.at(b, at + 1))
                    if kind == "raw":
                        i, s0, cols, diag, heads = MAX_UNITS[k]
                        nc.vector.tensor_reduce(part_max[:, i, s0 // HALF, heads[0]:heads[-1] + 1],
                                                raw_view(bank, cols, heads), AX_X, ALU.max)\
                            .then_inc(side_read.sem, 1)
                        if k == RAW - 1:
                            minus_maxima(g, at)
                    elif kind == "rows":
                        nc.vector.tensor_copy(max_rows[:, g % 2, :], ps[0:4 * SHIFT, bank, :].bitcast(BF16))\
                            .then_inc(side_read.sem, 1)
                    else:
                        y4 = ps[:, bank, :].rearrange("p (i j d) -> p i j d", i=NT // NH, j=4)
                        nc.vector.reciprocal(den_rec[:, k, :, :], y4[:, :, :, DH]).then_inc(den_ready.sem, 1)
                        dve.wait_ge(den_ready.sem, den_ready.at(b, NH * g + k + 1))
                        tiles = slice(k * (NT // NH), (k + 1) * (NT // NH))
                        tt(y_tok[:, tiles, 4 * DH * g:4 * DH * (g + 1)].rearrange("p i (j d) -> p i j d", j=4),
                           y4[:, :, :, 0:DH], den_rec[:, k, :, :].unsqueeze(3).to_broadcast([P, NT // NH, 4, DH]),
                           ALU.mult).then_inc(side_read.sem, 1)

                def minus_maxima(g, at):
                    dve.wait_ge(side_read.sem, side_read.at(b, at + 1))
                    full = NT // NH
                    ts(neg_max[:, 0:full, :], part_max[:, 0:full, 0, :], -1.0, None, ALU.mult)
                    tt(part_max[:, full:NT, 0, :], part_max[:, full:NT, 0, :], part_max[:, full:NT, 1, :], ALU.max)
                    dve.drain()
                    ts(neg_max[:, full:NT, :], part_max[:, full:NT, 0, :], -1.0, None, ALU.mult)
                    for part in range(SHIFT):
                        dve.drain()
                        last = nc.vector.tensor_copy(max_parts[:, :, :, part], neg_max[:, :, :])
                        if part < SHIFT - 1:
                            dve.drain()
                            tt(neg_max[:, :, :], neg_max[:, :, :], max_parts[:, :, :, part], ALU.subtract)
                    last.then_inc(max_ready.sem, 1)

                for unit in FIRST:
                    side_unit(*unit)
                for g in range(QUADS):
                    for side in PLANS[g]:
                        for unit in side:
                            side_unit(*unit)
                for unit in LAST:
                    side_unit(*unit)
                dve.drain()
                layer_norm(b, 3, add_product(wo_mm))
                dve.drain()
                tt(all_h, all_h, route_b[:, :, :].rearrange("p i n -> p (i n)"), ALU.add)
                dve.drain()
                match_words(b + 1)
                with dve.Fori(0, TILES // 2) as m:
                    for k in range(2):
                        dve.wait_ge(route_mm.sem, route_mm.at(b, k + 1) + m * 2)
                        for i in range(NT):
                            last = nc.vector.scalar_tensor_tensor(
                                h[:, i, :], ps[:, 4 * k + i // 2, (i % 2) * D:(i % 2 + 1) * D],
                                route[:, i, bass.ds(m * 2 + k, 1)], h[:, i, :], ALU.mult, ALU.add)
                        last.then_inc(routed.sem, 1)
                        dve.wait_ge(routed.sem, routed.at(b, k + 1) + m * 2)
                dve.drain().then_inc(h_final.sem, 1)


PREP_MM = K3 * DC + 5
PREP_ROUTE = 4 + 2 * TILES
PREP_DVE = PREP_ROUTE + 19


def constants():
    f32 = np.float32

    def bf16_bits(x):
        return (np.ascontiguousarray(x, f32).view(np.uint32) >> 16).astype(np.uint16)

    c = {}
    c["c_ident"] = np.eye(P, dtype=f32)
    c["c_ident_bf"] = bf16_bits(np.eye(P))
    later = np.triu(np.ones((P, P), bool), 1)
    c["c_mask_rows"] = bf16_bits(np.where(later, MASKED, 0.0))
    c["c_mask_cols"] = bf16_bits(np.where(later.T, MASKED, 0.0))
    c["c_vocab"] = (np.arange(P) % VOCAB).astype(f32)[:, None]
    inv = (1.0 / np.power(f32(10000.0), np.arange(0, D, 2, dtype=f32) / f32(D))).astype(f32)
    freqs = np.arange(S, dtype=f32)[:, None] * inv[None, :]
    emb = np.concatenate([freqs, freqs], axis=-1)
    sign = np.where(np.arange(D) % 2 == 0, -1.0, 1.0).astype(f32)
    both = np.concatenate([np.cos(emb), np.sin(emb) * sign], axis=1).astype(f32)
    c["c_trig"] = both.reshape(NT, P, 2 * D).transpose(1, 0, 2).copy()
    half = DH // 2
    theta = (1.0 / np.power(f32(10000.0), np.arange(half, dtype=f32) / f32(half))).astype(f32)
    ang = np.arange(S, dtype=f32)[:, None] * theta[None, :]
    cos, sin = np.cos(ang).astype(f32).T, np.sin(ang).astype(f32).T
    rows = np.stack([np.concatenate([cos, cos]), np.concatenate([-sin, sin])], axis=1)
    c["c_head_rot"] = np.repeat(rows, P // DH, axis=0)
    pick = np.zeros((3, 2 * NS, 2 * NS, P), f32)
    for n in range(2 * NS):
        pick[:, n, n, :] = 1.0
    c["c_pick_state"] = bf16_bits(pick.reshape(3 * 2 * NS, 2 * NS, P))
    pos = np.arange(S, dtype=f32)[:, None]
    div = np.exp(np.arange(0, PDIM, 2, dtype=f32) * f32(-np.log(10000.0) / PDIM)).astype(f32)
    ang = (pos * div).astype(f32)
    enc = np.zeros((S, PDIM), f32)
    enc[:, 0::2], enc[:, 1::2] = np.sin(ang), np.cos(ang)
    c["c_pe_T"] = enc.T.copy()
    return c


def layouts(i):
    def chunks(w):
        return w.reshape(-1, P, w.shape[1]).transpose(1, 0, 2)

    def column(v):
        return v.reshape(-1, P).T

    swap = np.arange(D) ^ 1
    both = np.concatenate([np.arange(D), swap])
    r = {"x": np.concatenate([i["x"], i["x"][:1]])}
    w = i["L0_tok_conv_w"].transpose(1, 2, 0)[:, :, both]
    r["tok_conv_w"] = w.reshape(DC, P, TAPS, 2 * D).transpose(1, 0, 2, 3)
    r["tok_conv_b"] = i["L0_tok_conv_b"][both]
    r["emb_T"] = chunks(i["L0_tok_embed_table"].T)
    r["emb_rows"] = i["L0_tok_embed_table"][:, both]
    r["tok_norm_w"] = i["L0_tok_norm_w"]
    r["mix_conv_w"] = i["L0_attn_conv_w"].transpose(0, 2, 1).reshape(EC, P, K3, D).transpose(1, 0, 2, 3)
    r["mix_conv_b"] = column(i["L0_attn_conv_b"])
    r["in_w"] = chunks(i["L0_attn_in_w"].T)
    r["in_b"] = column(i["L0_attn_in_b"])
    r["dt_w"] = chunks(i["L0_attn_dt_w"].T)
    r["dt_b"] = column(i["L0_attn_dt_b"])
    r["bc_w"] = chunks(np.concatenate([i["L0_attn_Bp_w"], i["L0_attn_Cp_w"]]).T)
    r["bc_b"] = np.concatenate([i["L0_attn_Bp_b"], i["L0_attn_Cp_b"]])[:, None]
    r["a_log"] = i["L0_attn_A_log"].reshape(EC, P, NS).transpose(1, 2, 0)
    r["d_skip"] = column(i["L0_attn_Dskip"])
    r["out_w"] = chunks(i["L0_attn_out_w"].T)
    r["gate_w"] = chunks(i["L0_ffn_gate_W"])
    r["gate_b"] = i["L0_ffn_gate_b"][None]
    r["bias"] = np.concatenate([i["L0_ffn_b1"], i["L0_ffn_b2"], i["L0_attn_out_b"][None]])
    r["g1"] = i["L0_ffn_g1"].reshape(NE, DC, P).transpose(2, 0, 1)
    r["be1"] = i["L0_ffn_be1"].reshape(NE, DC, P).transpose(2, 0, 1)
    r["g2"], r["be2"] = i["L0_ffn_g2"], i["L0_ffn_be2"]
    w = np.stack([i["L0_ffn_W1"], i["L0_ffn_W2"]]).reshape(2, NE, DC, P, D)
    r["w_moe"] = w.transpose(3, 0, 1, 2, 4).reshape(P, -1)
    r["w_route"] = i["L1_ffn_W"].transpose(0, 2, 1).reshape(TILES, DC, P, D).transpose(2, 0, 1, 3).reshape(P, -1)
    r["route_b"] = i["L1_ffn_b"]
    r["sigs_T"] = i["L1_ffn_tile_sigs"].T
    qkv = i["L1_attn_W_qkv"]
    swapped = np.arange(D) ^ (DH // 2)
    by_feature = np.arange(P).reshape(P // DH, DH).T.reshape(-1)
    cols = np.concatenate([r0 * D + order[c * P:(c + 1) * P][by_feature]
                           for c in range(DC) for r0 in range(2) for order in (np.arange(D), swapped)])
    r["w_qk"] = chunks(qkv[:, cols]).reshape(P, DC, 2 * 2 * DC, P)
    r["w_v"] = chunks(qkv[:, 2 * D:])
    r["w_o"] = chunks(i["L1_attn_W_o"])
    return {k: np.ascontiguousarray(v) for k, v in r.items()}


def kernel(**inputs):
    import concourse.bacc as bacc
    from concourse.bass_utils import run_bass_kernel_spmd

    arrays = layouts({k: np.asarray(v) for k, v in inputs.items()})
    arrays.update(constants())
    nc = bacc.Bacc("TRN2", target_bir_lowering=False, num_devices=1)
    aps = {k: nc.dram_tensor(f"in_{k}", v.shape, mybir.dt.from_np(v.dtype), kind="ExternalInput").ap()
           for k, v in arrays.items()}
    out = nc.dram_tensor("out_h", (B, S, D), F32, kind="ExternalOutput").ap()
    build(nc, aps, out)
    r = run_bass_kernel_spmd(nc, [{f"in_{k}": v for k, v in arrays.items()}], core_ids=[0])
    return r.results[0]["out_h"]
```
